# Optimizing a Trainium2 kernel written in Bass

```python
import numpy as np
import jax
import jax.numpy as jnp

def _softmax(x, axis=-1):
    return jax.nn.softmax(x, axis=axis)

def _gelu(x):
    return jax.nn.gelu(x, approximate=True)

def _silu(x):
    return jax.nn.silu(x)

def _sigmoid(x):
    return jax.nn.sigmoid(x)

def _layernorm(x, axis=-1, eps=1e-05):
    m = jnp.mean(x, axis=axis, keepdims=True)
    v = jnp.var(x, axis=axis, keepdims=True)
    return (x - m) / jnp.sqrt(v + eps)

def _scatter_add(tgt, idx, src, axis=0):
    return tgt.at[idx].add(src)

def _segment_sum(src, seg, n):
    return jax.ops.segment_sum(src, seg, n)
kernel_name = 'mk_audio_tower_d2_tok_aud1d256_r4_503f62'

def setup_inputs(seed: int=0):
    np.random.seed(seed)
    _w = jnp.asarray

    def _rec_inputs():
        import jax
        import jax.numpy as jnp
        _rk = jax.random.key(seed)
        x = -0.000292821 + 1.00034 * jax.random.normal(jax.random.fold_in(_rk, 1), (64, 8192), jnp.float32)
        return x
    x = _rec_inputs()

    def _L0_tok_setup():
        import jax, jax.numpy as jnp
        import numpy as np
        EPS = 1e-05

        def _conv1d(x, W, b, stride, pad):
            y = jax.lax.conv_general_dilated(x, W, (stride,), [(pad, pad)], dimension_numbers=('NCH', 'OIH', 'NCH'))
            return y + b[None, :, None]

        def _bn(x, g, b, m, v):
            return (x - m[None, :, None]) * (g * jax.lax.rsqrt(v + EPS))[None, :, None] + b[None, :, None]

        def _maxpool(x, k):
            B, C, L = x.shape
            return x.reshape(B, C, L // k, k).max(axis=-1)

        def _self_attn(x, Wq, bq, Wk, bk, Wv, bv, gamma):
            q = jnp.einsum('oc,bcl->bol', Wq, x) + bq[None, :, None]
            k = jnp.einsum('oc,bcl->bol', Wk, x) + bk[None, :, None]
            v = jnp.einsum('oc,bcl->bol', Wv, x) + bv[None, :, None]
            energy = jnp.einsum('bci,bcj->bij', q, k)
            attn = jax.nn.softmax(energy, axis=-1)
            out = jnp.einsum('bcj,bij->bci', v, attn)
            return gamma * out + x
        key = jax.random.key(seed)
        ks = jax.random.split(key, 32)
        B, D = (128, 8192)
        r = lambda i, shape, s=0.1: jax.random.normal(ks[i], shape, jnp.float32) * s
        return {'x': jax.random.normal(ks[0], (B, D), jnp.float32), 'w1': r(1, (16, 2, 3)), 'b1': r(2, (16,)), 'g1': 1.0 + r(3, (16,)), 'be1': r(4, (16,)), 'm1': r(5, (16,)), 'v1': 0.5 + jax.random.uniform(ks[6], (16,), jnp.float32), 'w2': r(7, (64, 16, 3)), 'b2': r(8, (64,)), 'g2': 1.0 + r(9, (64,)), 'be2': r(10, (64,)), 'm2': r(11, (64,)), 'v2': 0.5 + jax.random.uniform(ks[12], (64,), jnp.float32), 'wq': r(13, (8, 64)), 'bq': r(14, (8,)), 'wk': r(15, (8, 64)), 'bk': r(16, (8,)), 'wv': r(17, (64, 64)), 'bv': r(18, (64,)), 'gamma': jnp.float32(0.7), 'w3': r(19, (128, 64, 4)), 'b3': r(20, (128,)), 'g3': 1.0 + r(21, (128,)), 'be3': r(22, (128,)), 'm3': r(23, (128,)), 'v3': 0.5 + jax.random.uniform(ks[24], (128,), jnp.float32)}
    _L0_tok_all = _L0_tok_setup()
    _L0_tok_in = {k: v for k, v in _L0_tok_all.items() if k in ('w1', 'b1', 'g1', 'be1', 'm1', 'v1', 'w2', 'b2', 'g2', 'be2', 'm2', 'v2', 'wq', 'bq', 'wk', 'bk', 'wv', 'bv', 'gamma', 'w3', 'b3', 'g3', 'be3', 'm3', 'v3')}
    del _L0_tok_all

    def _L0_attn_setup():
        import jax, jax.numpy as jnp
        import numpy as np
        B, L, DIM = (8, 4096, 64)
        WINDOW, SHIFT, HEADS = (128, 64, 8)
        key = jax.random.key(seed)
        k0, k1, k2, k3 = jax.random.split(key, 4)
        x = jax.random.normal(k0, (B, L, DIM), dtype=jnp.float32)
        qkv_weight = jax.random.normal(k1, (3 * DIM, DIM), dtype=jnp.float32) * 0.02
        qkv_bias = jnp.zeros((3 * DIM,), dtype=jnp.float32)
        proj_weight = jax.random.normal(k2, (DIM, DIM), dtype=jnp.float32) * 0.02
        proj_bias = jnp.zeros((DIM,), dtype=jnp.float32)
        bias_table = jax.random.normal(k3, (2 * WINDOW - 1, HEADS), dtype=jnp.float32) * 0.02
        return {'x': x, 'qkv_weight': qkv_weight, 'qkv_bias': qkv_bias, 'proj_weight': proj_weight, 'proj_bias': proj_bias, 'bias_table': bias_table}
    _L0_attn_all = _L0_attn_setup()
    _L0_attn_in = {k: v for k, v in _L0_attn_all.items() if k in ('qkv_weight', 'qkv_bias', 'proj_weight', 'proj_bias', 'bias_table')}
    del _L0_attn_all

    def _L0_ffn_setup():
        import jax, jax.numpy as jnp
        import numpy as np
        DIM = 64
        H = 8
        D = 64
        G = 64
        INNER = H * D
        SCALE = D ** (-0.5)
        key = jax.random.key(seed)
        ks = jax.random.split(key, 12)
        B, N = (4, 4096)
        x = jax.random.normal(ks[0], (B, N, DIM), dtype=jnp.float32)
        s = lambda fan_in: 1.0 / np.sqrt(fan_in)
        W_fx = jax.random.normal(ks[1], (DIM, INNER), dtype=jnp.float32) * s(DIM)
        b_fx = jnp.zeros((INNER,), dtype=jnp.float32)
        W_x = jax.random.normal(ks[2], (DIM, INNER), dtype=jnp.float32) * s(DIM)
        b_x = jnp.zeros((INNER,), dtype=jnp.float32)
        A = jax.random.normal(ks[3], (G, D), dtype=jnp.float32)
        Q, _ = jnp.linalg.qr(A.T)
        W_slice = Q[:, :G].astype(jnp.float32)
        b_slice = jnp.zeros((G,), dtype=jnp.float32)
        W_q = jax.random.normal(ks[4], (D, D), dtype=jnp.float32) * s(D)
        W_k = jax.random.normal(ks[5], (D, D), dtype=jnp.float32) * s(D)
        W_v = jax.random.normal(ks[6], (D, D), dtype=jnp.float32) * s(D)
        W_out = jax.random.normal(ks[7], (INNER, DIM), dtype=jnp.float32) * s(INNER)
        b_out = jnp.zeros((DIM,), dtype=jnp.float32)
        temperature = jnp.ones((1, H, 1, 1), dtype=jnp.float32) * 0.5
        return {'x': x, 'W_fx': W_fx, 'b_fx': b_fx, 'W_x': W_x, 'b_x': b_x, 'W_slice': W_slice, 'b_slice': b_slice, 'W_q': W_q, 'W_k': W_k, 'W_v': W_v, 'W_out': W_out, 'b_out': b_out, 'temperature': temperature}
    _L0_ffn_all = _L0_ffn_setup()
    _L0_ffn_in = {k: v for k, v in _L0_ffn_all.items() if k in ('W_fx', 'b_fx', 'W_x', 'b_x', 'W_slice', 'b_slice', 'W_q', 'W_k', 'W_v', 'W_out', 'b_out', 'temperature')}
    del _L0_ffn_all

    def _L1_attn_setup():
        import jax, jax.numpy as jnp
        import numpy as np
        B, S, D = (32, 512, 64)
        LN_EPS = 1e-05

        def layer_norm(x, g, b):
            mu = jnp.mean(x, axis=-1, keepdims=True)
            var = jnp.mean(jnp.square(x - mu), axis=-1, keepdims=True)
            return (x - mu) * jax.lax.rsqrt(var + LN_EPS) * g + b

        def gru_scan(x, w_ih, w_hh, b_ih, b_hh):
            H = w_hh.shape[1]
            xp = jnp.einsum('bsd,hd->bsh', x, w_ih) + b_ih
            xp = jnp.swapaxes(xp, 0, 1)
            h0 = jnp.zeros((x.shape[0], H), x.dtype)

            def step(h, xt):
                gh = h @ w_hh.T + b_hh
                r = jax.nn.sigmoid(xt[:, :H] + gh[:, :H])
                z = jax.nn.sigmoid(xt[:, H:2 * H] + gh[:, H:2 * H])
                n = jnp.tanh(xt[:, 2 * H:] + r * gh[:, 2 * H:])
                h_new = (1.0 - z) * n + z * h
                return (h_new, h_new)
            _, ys = jax.lax.scan(step, h0, xp)
            return jnp.swapaxes(ys, 0, 1)
        key = jax.random.key(seed)
        ks = jax.random.split(key, 16)
        s = 1.0 / np.sqrt(D)
        u = lambda k, shape: jax.random.uniform(k, shape, jnp.float32, -s, s)
        return {'x': jax.random.normal(ks[0], (B, S, D), jnp.float32), 'ln_g': jnp.ones((D,), jnp.float32), 'ln_b': jnp.zeros((D,), jnp.float32), 'fwd_w_ih': u(ks[1], (3 * D, D)), 'fwd_w_hh': u(ks[2], (3 * D, D)), 'fwd_b_ih': u(ks[3], (3 * D,)), 'fwd_b_hh': u(ks[4], (3 * D,)), 'rev_w_ih': u(ks[5], (3 * D, D)), 'rev_w_hh': u(ks[6], (3 * D, D)), 'rev_b_ih': u(ks[7], (3 * D,)), 'rev_b_hh': u(ks[8], (3 * D,)), 'gate_w': u(ks[9], (D, 2 * D)), 'gate_b': u(ks[10], (D,)), 'out_w': u(ks[11], (D, D)), 'out_b': u(ks[12], (D,))}
    _L1_attn_all = _L1_attn_setup()
    _L1_attn_in = {k: v for k, v in _L1_attn_all.items() if k in ('ln_g', 'ln_b', 'fwd_w_ih', 'fwd_w_hh', 'fwd_b_ih', 'fwd_b_hh', 'rev_w_ih', 'rev_w_hh', 'rev_b_ih', 'rev_b_hh', 'gate_w', 'gate_b', 'out_w', 'out_b')}
    del _L1_attn_all

    def _L1_ffn_setup():
        import jax, jax.numpy as jnp
        import numpy as np
        D_MODEL = 64
        EXPERT_DIM = 128
        NUM_EXPERTS = 8
        TOP_K = 2
        SEQ_LEN = 512
        BATCH = 2
        key = jax.random.key(seed)
        ks = jax.random.split(key, 8)
        s = 0.02
        x = jax.random.normal(ks[0], (SEQ_LEN, BATCH, D_MODEL), dtype=jnp.float32)
        Wg = jax.random.normal(ks[1], (D_MODEL, NUM_EXPERTS), dtype=jnp.float32) * s
        bg = jax.random.normal(ks[2], (NUM_EXPERTS,), dtype=jnp.float32) * s
        bias = jnp.zeros((NUM_EXPERTS,), dtype=jnp.float32)
        W1 = jax.random.normal(ks[3], (NUM_EXPERTS, D_MODEL, EXPERT_DIM), dtype=jnp.float32) * s
        b1 = jax.random.normal(ks[4], (NUM_EXPERTS, EXPERT_DIM), dtype=jnp.float32) * s
        W2 = jax.random.normal(ks[5], (NUM_EXPERTS, EXPERT_DIM, D_MODEL), dtype=jnp.float32) * s
        b2 = jax.random.normal(ks[6], (NUM_EXPERTS, D_MODEL), dtype=jnp.float32) * s
        return {'x': x, 'Wg': Wg, 'bg': bg, 'bias': bias, 'W1': W1, 'b1': b1, 'W2': W2, 'b2': b2}
    _L1_ffn_all = _L1_ffn_setup()
    _L1_ffn_in = {k: v for k, v in _L1_ffn_all.items() if k in ('Wg', 'bg', 'bias', 'W1', 'b1', 'W2', 'b2')}
    del _L1_ffn_all
    return {'x': x, 'L0_tok_w1': _L0_tok_in['w1'], 'L0_tok_b1': _L0_tok_in['b1'], 'L0_tok_g1': _L0_tok_in['g1'], 'L0_tok_be1': _L0_tok_in['be1'], 'L0_tok_m1': _L0_tok_in['m1'], 'L0_tok_v1': _L0_tok_in['v1'], 'L0_tok_w2': _L0_tok_in['w2'], 'L0_tok_b2': _L0_tok_in['b2'], 'L0_tok_g2': _L0_tok_in['g2'], 'L0_tok_be2': _L0_tok_in['be2'], 'L0_tok_m2': _L0_tok_in['m2'], 'L0_tok_v2': _L0_tok_in['v2'], 'L0_tok_wq': _L0_tok_in['wq'], 'L0_tok_bq': _L0_tok_in['bq'], 'L0_tok_wk': _L0_tok_in['wk'], 'L0_tok_bk': _L0_tok_in['bk'], 'L0_tok_wv': _L0_tok_in['wv'], 'L0_tok_bv': _L0_tok_in['bv'], 'L0_tok_gamma': _L0_tok_in['gamma'], 'L0_tok_w3': _L0_tok_in['w3'], 'L0_tok_b3': _L0_tok_in['b3'], 'L0_tok_g3': _L0_tok_in['g3'], 'L0_tok_be3': _L0_tok_in['be3'], 'L0_tok_m3': _L0_tok_in['m3'], 'L0_tok_v3': _L0_tok_in['v3'], 'L0_attn_qkv_weight': _L0_attn_in['qkv_weight'], 'L0_attn_qkv_bias': _L0_attn_in['qkv_bias'], 'L0_attn_proj_weight': _L0_attn_in['proj_weight'], 'L0_attn_proj_bias': _L0_attn_in['proj_bias'], 'L0_attn_bias_table': _L0_attn_in['bias_table'], 'L0_ffn_W_fx': _L0_ffn_in['W_fx'], 'L0_ffn_b_fx': _L0_ffn_in['b_fx'], 'L0_ffn_W_x': _L0_ffn_in['W_x'], 'L0_ffn_b_x': _L0_ffn_in['b_x'], 'L0_ffn_W_slice': _L0_ffn_in['W_slice'], 'L0_ffn_b_slice': _L0_ffn_in['b_slice'], 'L0_ffn_W_q': _L0_ffn_in['W_q'], 'L0_ffn_W_k': _L0_ffn_in['W_k'], 'L0_ffn_W_v': _L0_ffn_in['W_v'], 'L0_ffn_W_out': _L0_ffn_in['W_out'], 'L0_ffn_b_out': _L0_ffn_in['b_out'], 'L0_ffn_temperature': _L0_ffn_in['temperature'], 'L1_attn_ln_g': _L1_attn_in['ln_g'], 'L1_attn_ln_b': _L1_attn_in['ln_b'], 'L1_attn_fwd_w_ih': _L1_attn_in['fwd_w_ih'], 'L1_attn_fwd_w_hh': _L1_attn_in['fwd_w_hh'], 'L1_attn_fwd_b_ih': _L1_attn_in['fwd_b_ih'], 'L1_attn_fwd_b_hh': _L1_attn_in['fwd_b_hh'], 'L1_attn_rev_w_ih': _L1_attn_in['rev_w_ih'], 'L1_attn_rev_w_hh': _L1_attn_in['rev_w_hh'], 'L1_attn_rev_b_ih': _L1_attn_in['rev_b_ih'], 'L1_attn_rev_b_hh': _L1_attn_in['rev_b_hh'], 'L1_attn_gate_w': _L1_attn_in['gate_w'], 'L1_attn_gate_b': _L1_attn_in['gate_b'], 'L1_attn_out_w': _L1_attn_in['out_w'], 'L1_attn_out_b': _L1_attn_in['out_b'], 'L1_ffn_Wg': _L1_ffn_in['Wg'], 'L1_ffn_bg': _L1_ffn_in['bg'], 'L1_ffn_bias': _L1_ffn_in['bias'], 'L1_ffn_W1': _L1_ffn_in['W1'], 'L1_ffn_b1': _L1_ffn_in['b1'], 'L1_ffn_W2': _L1_ffn_in['W2'], 'L1_ffn_b2': _L1_ffn_in['b2']}

def reference(x, L0_tok_w1, L0_tok_b1, L0_tok_g1, L0_tok_be1, L0_tok_m1, L0_tok_v1, L0_tok_w2, L0_tok_b2, L0_tok_g2, L0_tok_be2, L0_tok_m2, L0_tok_v2, L0_tok_wq, L0_tok_bq, L0_tok_wk, L0_tok_bk, L0_tok_wv, L0_tok_bv, L0_tok_gamma, L0_tok_w3, L0_tok_b3, L0_tok_g3, L0_tok_be3, L0_tok_m3, L0_tok_v3, L0_attn_qkv_weight, L0_attn_qkv_bias, L0_attn_proj_weight, L0_attn_proj_bias, L0_attn_bias_table, L0_ffn_W_fx, L0_ffn_b_fx, L0_ffn_W_x, L0_ffn_b_x, L0_ffn_W_slice, L0_ffn_b_slice, L0_ffn_W_q, L0_ffn_W_k, L0_ffn_W_v, L0_ffn_W_out, L0_ffn_b_out, L0_ffn_temperature, L1_attn_ln_g, L1_attn_ln_b, L1_attn_fwd_w_ih, L1_attn_fwd_w_hh, L1_attn_fwd_b_ih, L1_attn_fwd_b_hh, L1_attn_rev_w_ih, L1_attn_rev_w_hh, L1_attn_rev_b_ih, L1_attn_rev_b_hh, L1_attn_gate_w, L1_attn_gate_b, L1_attn_out_w, L1_attn_out_b, L1_ffn_Wg, L1_ffn_bg, L1_ffn_bias, L1_ffn_W1, L1_ffn_b1, L1_ffn_W2, L1_ffn_b2):
    import jax
    import jax.numpy as jnp

    def _L0_tok_ref(x, w1, b1, g1, be1, m1, v1, w2, b2, g2, be2, m2, v2, wq, bq, wk, bk, wv, bv, gamma, w3, b3, g3, be3, m3, v3):
        import jax, jax.numpy as jnp
        import numpy as np
        EPS = 1e-05

        def _conv1d(x, W, b, stride, pad):
            y = jax.lax.conv_general_dilated(x, W, (stride,), [(pad, pad)], dimension_numbers=('NCH', 'OIH', 'NCH'))
            return y + b[None, :, None]

        def _bn(x, g, b, m, v):
            return (x - m[None, :, None]) * (g * jax.lax.rsqrt(v + EPS))[None, :, None] + b[None, :, None]

        def _maxpool(x, k):
            B, C, L = x.shape
            return x.reshape(B, C, L // k, k).max(axis=-1)

        def _self_attn(x, Wq, bq, Wk, bk, Wv, bv, gamma):
            q = jnp.einsum('oc,bcl->bol', Wq, x) + bq[None, :, None]
            k = jnp.einsum('oc,bcl->bol', Wk, x) + bk[None, :, None]
            v = jnp.einsum('oc,bcl->bol', Wv, x) + bv[None, :, None]
            energy = jnp.einsum('bci,bcj->bij', q, k)
            attn = jax.nn.softmax(energy, axis=-1)
            out = jnp.einsum('bcj,bij->bci', v, attn)
            return gamma * out + x
        B, D = x.shape
        emb_sample, emb_task = (x[:, :D // 2], x[:, D // 2:])
        h = jnp.stack([emb_sample, emb_task], axis=1)
        h = _maxpool(jax.nn.relu(_bn(_conv1d(h, w1, b1, 1, 1), g1, be1, m1, v1)), 8)
        h = _maxpool(jax.nn.relu(_bn(_conv1d(h, w2, b2, 1, 1), g2, be2, m2, v2)), 4)
        h = _self_attn(h, wq, bq, wk, bk, wv, bv, gamma)
        h = _bn(_conv1d(h, w3, b3, 2, 1), g3, be3, m3, v3)
        return h

    def _L0_attn_ref(x, qkv_weight, qkv_bias, proj_weight, proj_bias, bias_table):
        import jax, jax.numpy as jnp
        import numpy as np
        B, L, DIM = (8, 4096, 64)
        WINDOW, SHIFT, HEADS = (128, 64, 8)
        Bb, Ll, C = x.shape
        hd = C // HEADS
        pad = (WINDOW - Ll % WINDOW) % WINDOW
        xp = jnp.pad(x, ((0, 0), (0, pad), (0, 0)))
        pad_L = Ll + pad
        shift = 0 if WINDOW >= pad_L else SHIFT
        if shift > 0:
            xp = jnp.roll(xp, -shift, axis=1)
        nW = pad_L // WINDOW
        xw = xp.reshape(Bb * nW, WINDOW, C)
        qkv = xw @ qkv_weight.T + qkv_bias
        qkv = qkv.reshape(Bb * nW, WINDOW, 3, HEADS, hd).transpose(2, 0, 3, 1, 4)
        q, k, v = (qkv[0], qkv[1], qkv[2])
        scale = hd ** (-0.5)
        attn = jnp.einsum('whqd,whkd->whqk', q * scale, k)
        coords = jnp.arange(WINDOW)
        rel_idx = coords[:, None] - coords[None, :] + WINDOW - 1
        rpb = bias_table[rel_idx]
        attn = attn + jnp.transpose(rpb, (2, 0, 1))[None]
        if shift > 0:
            region = jnp.zeros((pad_L,), dtype=x.dtype)
            region = region.at[pad_L - WINDOW:pad_L - shift].set(1.0)
            region = region.at[pad_L - shift:].set(2.0)
            region = region.reshape(nW, WINDOW)
            mask = jnp.where(region[:, None, :] != region[:, :, None], -100.0, 0.0).astype(x.dtype)
            attn = attn.reshape(Bb, nW, HEADS, WINDOW, WINDOW) + mask[None, :, None]
            attn = attn.reshape(Bb * nW, HEADS, WINDOW, WINDOW)
        attn = jax.nn.softmax(attn, axis=-1)
        out = jnp.einsum('whqk,whkd->wqhd', attn, v).reshape(Bb * nW, WINDOW, C)
        out = out @ proj_weight.T + proj_bias
        out = out.reshape(Bb, pad_L, C)
        if shift > 0:
            out = jnp.roll(out, shift, axis=1)
        return out[:, :Ll, :]

    def _L0_ffn_ref(x, W_fx, b_fx, W_x, b_x, W_slice, b_slice, W_q, W_k, W_v, W_out, b_out, temperature):
        import jax, jax.numpy as jnp
        import numpy as np
        DIM = 64
        H = 8
        D = 64
        G = 64
        INNER = H * D
        SCALE = D ** (-0.5)
        B, N, _ = x.shape
        fx_mid = (x @ W_fx + b_fx).reshape(B, N, H, D).transpose(0, 2, 1, 3)
        x_mid = (x @ W_x + b_x).reshape(B, N, H, D).transpose(0, 2, 1, 3)
        temp = jnp.clip(temperature, 0.1, 5.0)
        slice_weights = jax.nn.softmax((x_mid @ W_slice + b_slice) / temp, axis=-1)
        slice_norm = slice_weights.sum(axis=2)
        slice_token = jnp.einsum('bhnc,bhng->bhgc', fx_mid, slice_weights)
        slice_token = slice_token / (slice_norm[..., None] + 1e-05)
        q = slice_token @ W_q
        k = slice_token @ W_k
        v = slice_token @ W_v
        attn = jax.nn.softmax(jnp.einsum('bhgc,bhkc->bhgk', q, k) * SCALE, axis=-1)
        out_slice = jnp.einsum('bhgk,bhkc->bhgc', attn, v)
        out_x = jnp.einsum('bhgc,bhng->bhnc', out_slice, slice_weights)
        out_x = out_x.transpose(0, 2, 1, 3).reshape(B, N, INNER)
        return out_x @ W_out + b_out

    def _L1_attn_ref(x, ln_g, ln_b, fwd_w_ih, fwd_w_hh, fwd_b_ih, fwd_b_hh, rev_w_ih, rev_w_hh, rev_b_ih, rev_b_hh, gate_w, gate_b, out_w, out_b):
        import jax, jax.numpy as jnp
        import numpy as np
        B, S, D = (32, 512, 64)
        LN_EPS = 1e-05

        def layer_norm(x, g, b):
            mu = jnp.mean(x, axis=-1, keepdims=True)
            var = jnp.mean(jnp.square(x - mu), axis=-1, keepdims=True)
            return (x - mu) * jax.lax.rsqrt(var + LN_EPS) * g + b

        def gru_scan(x, w_ih, w_hh, b_ih, b_hh):
            H = w_hh.shape[1]
            xp = jnp.einsum('bsd,hd->bsh', x, w_ih) + b_ih
            xp = jnp.swapaxes(xp, 0, 1)
            h0 = jnp.zeros((x.shape[0], H), x.dtype)

            def step(h, xt):
                gh = h @ w_hh.T + b_hh
                r = jax.nn.sigmoid(xt[:, :H] + gh[:, :H])
                z = jax.nn.sigmoid(xt[:, H:2 * H] + gh[:, H:2 * H])
                n = jnp.tanh(xt[:, 2 * H:] + r * gh[:, 2 * H:])
                h_new = (1.0 - z) * n + z * h
                return (h_new, h_new)
            _, ys = jax.lax.scan(step, h0, xp)
            return jnp.swapaxes(ys, 0, 1)
        residual = x
        xn = layer_norm(x, ln_g, ln_b)
        fwd_out = gru_scan(xn, fwd_w_ih, fwd_w_hh, fwd_b_ih, fwd_b_hh)
        rev_out = gru_scan(xn[:, ::-1], rev_w_ih, rev_w_hh, rev_b_ih, rev_b_hh)[:, ::-1]
        g = jax.nn.sigmoid(jnp.concatenate([fwd_out, rev_out], axis=-1) @ gate_w.T + gate_b)
        combined = g * fwd_out + (1.0 - g) * rev_out
        out = combined @ out_w.T + out_b
        return out + residual

    def _L1_ffn_ref(x, Wg, bg, bias, W1, b1, W2, b2):
        import jax, jax.numpy as jnp
        import numpy as np
        D_MODEL = 64
        EXPERT_DIM = 128
        NUM_EXPERTS = 8
        TOP_K = 2
        SEQ_LEN = 512
        BATCH = 2
        x_flat = x.reshape(-1, D_MODEL)
        gate_logits = x_flat @ Wg + bg + bias
        topk_vals, topk_idx = jax.lax.top_k(gate_logits, TOP_K)
        topk_w = jax.nn.softmax(topk_vals, axis=-1)
        combine = (jax.nn.one_hot(topk_idx, NUM_EXPERTS, dtype=x.dtype) * topk_w[..., None]).sum(axis=1)
        h = jax.nn.relu(jnp.einsum('td,edh->teh', x_flat, W1) + b1)
        y = jnp.einsum('teh,ehd->ted', h, W2) + b2
        out = jnp.einsum('ted,te->td', y, combine)
        return out.reshape(x.shape)
    h = _L0_tok_ref(x, L0_tok_w1, L0_tok_b1, L0_tok_g1, L0_tok_be1, L0_tok_m1, L0_tok_v1, L0_tok_w2, L0_tok_b2, L0_tok_g2, L0_tok_be2, L0_tok_m2, L0_tok_v2, L0_tok_wq, L0_tok_bq, L0_tok_wk, L0_tok_bk, L0_tok_wv, L0_tok_bv, L0_tok_gamma, L0_tok_w3, L0_tok_b3, L0_tok_g3, L0_tok_be3, L0_tok_m3, L0_tok_v3)
    h = h + _L0_attn_ref(_layernorm(h, axis=-1), L0_attn_qkv_weight, L0_attn_qkv_bias, L0_attn_proj_weight, L0_attn_proj_bias, L0_attn_bias_table)
    h = h + _L0_ffn_ref(_layernorm(h, axis=-1), L0_ffn_W_fx, L0_ffn_b_fx, L0_ffn_W_x, L0_ffn_b_x, L0_ffn_W_slice, L0_ffn_b_slice, L0_ffn_W_q, L0_ffn_W_k, L0_ffn_W_v, L0_ffn_W_out, L0_ffn_b_out, L0_ffn_temperature)
    h = h + _L1_attn_ref(_layernorm(h, axis=-1), L1_attn_ln_g, L1_attn_ln_b, L1_attn_fwd_w_ih, L1_attn_fwd_w_hh, L1_attn_fwd_b_ih, L1_attn_fwd_b_hh, L1_attn_rev_w_ih, L1_attn_rev_w_hh, L1_attn_rev_b_ih, L1_attn_rev_b_hh, L1_attn_gate_w, L1_attn_gate_b, L1_attn_out_w, L1_attn_out_b)
    h = h + _L1_ffn_ref(_layernorm(h, axis=-1), L1_ffn_Wg, L1_ffn_bg, L1_ffn_bias, L1_ffn_W1, L1_ffn_b1, L1_ffn_W2, L1_ffn_b2)
    return h

_drawn_inputs = setup_inputs


def setup_inputs(seed=0):
    import zlib

    import numpy as np

    out = dict(_drawn_inputs(seed))
    spreads = {'L0_attn_qkv_bias': (0.0, 0.1),
     'L0_attn_proj_bias': (0.0, 0.1),
     'L0_ffn_b_fx': (0.0, 0.1),
     'L0_ffn_b_x': (0.0, 0.584),
     'L0_ffn_b_slice': (0.0, 0.699),
     'L0_ffn_b_out': (0.0, 0.1),
     'L0_ffn_temperature': (0.5, 0.549),
     'L1_attn_ln_g': (1.0, 0.6),
     'L1_attn_ln_b': (0.0, 0.8),
     'L1_ffn_bias': (0.0, 0.8)}
    factors = {'L0_tok_wq': 8.0,
     'L0_tok_bq': 8.0,
     'L0_tok_wk': 8.0,
     'L0_tok_bk': 64.0,
     'L0_attn_qkv_weight': 3.213,
     'L0_attn_bias_table': 46.52,
     'L1_attn_fwd_w_hh': 3.229,
     'L1_attn_fwd_b_ih': 8.0,
     'L1_attn_fwd_b_hh': 8.0,
     'L1_attn_rev_b_ih': 5.959,
     'L1_attn_rev_b_hh': 8.0,
     'L1_attn_gate_b': 8.0,
     'L1_ffn_Wg': 5.469,
     'L1_ffn_bg': 8.0,
     'L1_ffn_W1': 7.595,
     'L1_ffn_b1': 8.0,
     'L1_ffn_W2': 6.002,
     'L1_ffn_b2': 7.314}
    for name, (base, spread) in spreads.items():
        noise = np.random.default_rng([zlib.crc32(name.encode()), seed]).standard_normal(out[name].shape)
        drawn = base * np.exp(spread * noise) if base else spread * noise
        out[name] = jnp.asarray(drawn.astype(out[name].dtype))
    for name, factor in factors.items():
        out[name] = (out[name] * factor).astype(out[name].dtype)
    return out
```

```python
import numpy as np
import concourse.bass as bass
from concourse import mybir

F32 = mybir.dt.float32
BF16 = mybir.dt.bfloat16
U32 = mybir.dt.uint32
ALU = mybir.AluOpType
ACT = mybir.ActivationFunctionType
X = mybir.AxisListType.X
EPS = 1e-5
B, L, C = 64, 128, 64
NP = B // 2
HEADS, HD = 8, 8
G = 64
E = 8
LEN = 4096

PARTS = [
    ("eye", 128),
    ("w1", 2 * 128), ("w2", 12 * 128), ("w3", 8 * 128),
    ("bn_v", 83), ("bn_g", 83), ("bn_b", 3), ("bn_m", 3), ("bn_be", 3),
    ("wq", 256), ("wk", 128), ("bq", 2), ("bk", 1), ("wv", 128), ("bv", 1), ("gamma", 1),
    ("a_q", 128), ("a_k", 128), ("a_bq", 1), ("a_bk", 1), ("a_mask", 16), ("a_v", 128), ("a_bv", 128), ("a_p", 128), ("a_bp", 128),
    ("a_bias", HEADS * 128),
    ("f_fxT", 512), ("f_bfxT", 8), ("f_xT", 512), ("f_bxT", 8), ("f_slice", 64), ("f_bslice", 64),
    ("f_wqT", 64), ("f_wkT", 64), ("f_wvT", 64), ("f_out", 512), ("f_bout", 1), ("f_temp", 8),
    ("g_lng", 1), ("g_lnb", 1), ("g_ih", 3 * 128), ("g_hh", 3 * 128), ("g_bih", 3), ("g_bhh", 3),
    ("g_gate", 64), ("g_bgate", 1), ("g_diff", 64), ("g_out", 64), ("g_bout", 256),
    ("m_g", 16), ("m_bg", 64), ("m_bias", 64), ("m_w1", 16 * 128), ("m_b1", 8), ("m_w2", 512 + 32), ("m_b2", 512), ("iota", 8),
]
AT, WIDTH = {}, 0
for _n, _w in PARTS:
    AT[_n] = (WIDTH, _w)
    WIDTH += _w


def build(nc, xp, consts, out):
    def sb(name, shape, dt=F32):
        return nc.alloc_sbuf_tensor(name, shape, dt)

    def sem(name):
        return nc.alloc_semaphore(name)

    cst = sb("cst", [128, WIDTH])

    def c(name, a=0, b=None):
        o, w = AT[name]
        return cst[:, o + a:o + (w if b is None else b)]

    eye = c("eye")
    eye16 = sb("eye16", [128, 128], BF16)
    h = sb("h", [128, B, C])
    xc = sb("xc", [128, B, C])
    big1 = sb("big1", [128, 2 * LEN])
    big2 = sb("big2", [128, 2 * LEN])
    pt = [nc.alloc_psum_tensor(f"bank{l}", [128, 4 * 512], F32) for l in range(2)]

    def T(l, k, n=1):
        return pt[l][:, 512 * k:512 * (k + n)]

    xin = [big1[0:96, 0:LEN], big1[0:96, LEN:2 * LEN]]
    bn_s = sb("bn_s", [128, 83])
    bn_t = sb("bn_t", [128, 3])
    w1s = sb("w1s", [128, 2 * 128])
    half_neg = sb("half_neg", [128, 1])
    spare = sb("spare", [128, 32])
    one, one_set = sb("one", [128, 1]), sem("one_set")
    h1raw = [big2[:, 512 * k:512 * (k + 1)] for k in range(2)]
    h1 = [big2[:, 1024 + 520 * k:1024 + 520 * k + 514] for k in range(2)]
    h2raw = [big2[:, 2100 + 512 * k:2100 + 512 * (k + 1)] for k in range(2)]
    h2all = xc[:, :, :].rearrange("p (q s) c -> p q (s c)", s=2)

    loaded = sem("consts_loaded")
    x_loaded = [sem("x_loaded0"), sem("x_loaded1")]
    bn_var, bn_rs, bn_scale, bn_shift = sem("bn_var"), sem("bn_rsqrt"), sem("bn_scale"), sem("bn_shift")
    w_scaled, pads_zero, eye_cast = sem("conv_weights_scaled"), sem("pads_zero"), sem("eye_cast")
    c1_sum, c1_max, h1_ready = sem("conv1_sum"), sem("conv1_max"), sem("h1_ready")
    c2_sum, c2_max, h2_ready = sem("conv2_sum"), sem("conv2_max"), sem("h2_ready")
    stored = sem("out_stored")
    b_copy, b_proj, b_q, b_k, b_v = (sem("1b_" + n) for n in ("h2_copied", "projected", "q_ready", "k_ready", "v_ready"))
    b_energy, b_max, b_exp, b_rs, b_norm = (sem("1b_" + n) for n in ("energy", "max", "exp", "rsum", "normed"))
    b_pT, b_pTc, b_att, b_h3, b_c3, b_h = (sem("1b_" + n) for n in ("pT", "pT_copied", "attended", "h3_ready", "conv3", "h_written"))
    gbv_ready = sem("gamma_bv_ready")
    gbv = sb("gbv", [128, 1])

    def buf(name, cols, dt=F32):
        return [sb(f"{name}{l}", [128, cols], dt) for l in range(2)]

    def big2_lane(at, cols):
        return [big2[:, at + cols * l:at + cols * (l + 1)] for l in range(2)]
    h2p = big2_lane(3200, 128)
    bq_s, bk_s = big2_lane(5800, 256), big2_lane(3712, 128)
    bvT = big2_lane(3968, 128)
    bP, bPT = big2_lane(4224, 256), big2_lane(4736, 256)
    bmx, bsum, brs = big2_lane(5248, 2), big2_lane(5252, 2), big2_lane(5256, 2)
    h3g = big2[:, 5260:5260 + 4 * 130].rearrange("p (r n) -> p r n", r=4)

    JA = 8

    def stage1a_pe(pe):
        pe.wait_ge(w_scaled, 1)
        pe.wait_ge(pads_zero, 3)
        with pe.Fori(0, JA // 4) as ii:
            for w, g in ((0, 0), (0, 1), (1, 0), (1, 1)):
                j = ii * 4 + (2 * w + g)
                if g == 0:
                    pe.wait_ge(x_loaded[w], ii * 48 + 48)
                for q in range(4):
                    pe.wait_ge(c1_max, (j * 4) + (q + 1))
                    for k in range(2):
                        m = nc.tensor.matmul(T(0, 2 * (q % 2) + k), w1s[0:96, 128 * g:128 * (g + 1)],
                                             xin[w][:, (2 * q + k) * 512:(2 * q + k + 1) * 512], start=True, stop=True)
                    m.then_inc(c1_sum, 1)
                pe.wait_ge(h1_ready, j + 3)
                for p in range(4):
                    pe.wait_ge(c2_max, (j * 4) + (p + 1))
                    for t in range(3):
                        m = nc.tensor.matmul(T(1, p % 2), w2s(p, t), h1[g][:, t:t + 512], start=(t == 0), stop=(t == 2))
                    m.then_inc(c2_sum, 1)

    def w2s(p, t):
        return c("w2", (3 * p + t) * 128, (3 * p + t + 1) * 128)

    def stage1a_dve(v):
        with v.Fori(0, JA // 2) as i:
            for g in range(2):
                j = i * 2 + g
                v.wait_ge(h1_ready, j + 1)
                for q in range(4):
                    v.wait_ge(c1_sum, (j * 4) + (q + 1))
                    nc.vector.tensor_reduce(h1raw[g][:, 128 * q:128 * (q + 1)],
                                            T(0, 2 * (q % 2), 2).rearrange("p (n k) -> p n k", k=8), X, ALU.max).then_inc(c1_max, 1)
                v.wait_ge(h2_ready, j + 1)
                for p in range(4):
                    v.wait_ge(c2_sum, (j * 4) + (p + 1))
                    nc.vector.tensor_reduce(h2raw[g][:, 128 * p:128 * (p + 1)],
                                            T(1, p % 2).rearrange("p (n k) -> p n k", k=4), X, ALU.max).then_inc(c2_max, 1)

    def stage1a_act(act):
        act.wait_ge(bn_shift, 2)
        act.wait_ge(pads_zero, 3)
        with act.Fori(0, JA // 2) as i:
            for g in range(2):
                j = i * 2 + g
                act.wait_ge(c1_max, j * 4 + 6)
                nc.scalar.activation(h1[g][:, 1:513], h1raw[g], ACT.Relu, bias=bn_t[:, 0:1]).then_inc(h1_ready, 1)
                act.wait_ge(c2_max, j * 4 + 6)
                nc.scalar.activation(h2all[:, bass.ds(4 * j, 4), :], h2raw[g].rearrange("p (r n) -> p r n", r=4),
                                     ACT.Relu, bias=bn_t[:, 1:2]).then_inc(h2_ready, 1)

    IB = NP // 4

    def stage1b_pe(pe):
        with pe.Fori(0, IB) as i:
            for rr in (0, 2):
                R = [(r, r % 2, i * 4 + (r + 1)) for r in (rr, rr + 1)]
                for r, l, n in R:
                    pe.wait_ge(b_copy, n)
                    if r == 0:
                        pe.wait_ge(b_h, i + 1)
                    for s in range(2):
                        nc.tensor.matmul(T(l, 0)[:, 128 * s:128 * (s + 1)], c("wq", 128 * s, 128 * (s + 1)), h2p[l], start=True, stop=True)
                    nc.tensor.matmul(T(l, 2)[:, 256:384], c("wk"), h2p[l], start=True, stop=True)
                    nc.tensor.matmul(T(l, 1)[:, 0:128], h2p[l], c("wv"), start=True, stop=True).then_inc(b_proj, 1)
                for r, l, n in R:
                    pe.wait_ge(b_q, n)
                    pe.wait_ge(b_k, n)
                    for s in range(2):
                        m = nc.tensor.matmul(T(l, 2)[:, 128 * s:128 * (s + 1)], bq_s[l][:, 128 * s:128 * (s + 1)],
                                             bk_s[l], start=True, stop=True)
                    m.then_inc(b_energy, 1)
                for r, l, n in R:
                    pe.wait_ge(b_norm, n)
                    for s in range(2):
                        m = nc.tensor.transpose(T(l, 3)[:, 128 * s:128 * (s + 1)], bP[l][:, 128 * s:128 * (s + 1)], eye)
                    m.then_inc(b_pT, 1)
                for r, l, n in R:
                    pe.wait_ge(b_pTc, n)
                    pe.wait_ge(b_v, n)
                    for s in range(2):
                        m = nc.tensor.matmul(T(l, 1)[64 * s:64 * s + 64, 128:256], bvT[l][:, 64 * s:64 * s + 64],
                                             bPT[l][:, 128 * s:128 * (s + 1)], start=True, stop=True)
                    m.then_inc(b_att, 1)
            pe.wait_ge(b_h3, i * 4 + 6)
            for s in range(2):
                for t in range(4):
                    m = nc.tensor.matmul(T(0, 0)[:, 256 * s:256 * (s + 1)], c("w3", (4 * s + t) * 128, (4 * s + t + 1) * 128),
                                         h3g[:, :, t:t + 127:2], start=(t == 0), stop=(t == 3))
            m.then_inc(b_c3, 1)

    def stage1b_dve(v):
        v.wait_ge(h2_ready, JA + 2)
        with v.Fori(0, IB) as i:
            for rr in (0, 2):
                R = [(r, r % 2, i * 4 + (r + 1)) for r in (rr, rr + 1)]
                for r, l, n in R:
                    v.wait_ge(b_h3, i * 4 + (r + 1))
                    nc.vector.tensor_copy(h2p[l], h2all[:, i * 4 + r, :]).then_inc(b_copy, 1)
                for r, l, n in R:
                    v.wait_ge(b_proj, n)
                    nc.vector.tensor_scalar(bk_s[l], T(l, 2)[:, 256:384], c("bk"), None, ALU.add).then_inc(b_k, 1)
                for r, l, n in R:
                    v.wait_ge(b_energy, n)
                    nc.vector.tensor_reduce(bmx[l], T(l, 2)[:, 0:256].rearrange("p (s n) -> p s n", s=2), X, ALU.max,
                                            negate=True).then_inc(b_max, 1)
                for r, l, n in R:
                    v.wait_ge(b_exp, n)
                    nc.vector.reciprocal(brs[l], bsum[l]).then_inc(b_rs, 1)
                for r, l, n in R:
                    v.wait_ge(b_rs, n)
                    for s in range(2):
                        m = nc.vector.tensor_scalar(bP[l][:, 128 * s:128 * (s + 1)], bP[l][:, 128 * s:128 * (s + 1)],
                                                    brs[l][:, s:s + 1], c("gamma"), ALU.mult, ALU.mult)
                    m.then_inc(b_norm, 1)
                for r, l, n in R:
                    v.wait_ge(b_att, n)
                    if r == 0:
                        v.wait_ge(b_c3, i + 1)
                    nc.vector.scalar_tensor_tensor(h3g[:, r, 1:129], T(l, 1)[:, 128:256], gbv[:, 0:1], h2p[l],
                                                   ALU.add, ALU.add).then_inc(b_h3, 1)

    def stage1b_act(act):
        with act.Fori(0, IB) as i:
            for rr in (0, 2):
                R = [(r, r % 2, i * 4 + (r + 1)) for r in (rr, rr + 1)]
                for r, l, n in R:
                    act.wait_ge(b_proj, n)
                    for s in range(2):
                        m = nc.scalar.activation(bq_s[l][:, 128 * s:128 * (s + 1)], T(l, 0)[:, 128 * s:128 * (s + 1)],
                                                 ACT.Identity, bias=c("bq", s, s + 1))
                    m.then_inc(b_q, 1)
                    nc.scalar.copy(bvT[l], T(l, 1)[:, 0:128]).then_inc(b_v, 1)
                for r, l, n in R:
                    act.wait_ge(b_max, n)
                    nc.scalar.activation(bP[l][:, 0:128], T(l, 2)[:, 0:128], ACT.Exp, bias=bmx[l][:, 0:1], accum_out=bsum[l][:, 0:1])
                    nc.scalar.activation(bP[l][:, 128:256], T(l, 2)[:, 128:256], ACT.Exp, bias=bmx[l][:, 1:2],
                                         accum_out=bsum[l][:, 1:2]).then_inc(b_exp, 1)
                for r, l, n in R:
                    act.wait_ge(b_pT, n)
                    nc.scalar.copy(bPT[l], T(l, 3)[:, 0:256]).then_inc(b_pTc, 1)
            act.wait_ge(b_c3, i + 2)
            nc.scalar.activation(h[:, bass.ds(8 * i, 8), :].rearrange("p (r s) c -> p s r c", s=2),
                                 T(0, 0).rearrange("p (s r c) -> p s r c", s=2, r=4), ACT.Identity,
                                 bias=bn_t[:, 2:3], scale=bn_s[:, 82:83]).then_inc(b_h, 1)

    rowsum, rowsq, rstd = sb("rowsum", [128, B]), sb("rowsq", [128, B]), sb("rstd", [128, B])
    eps_var = sb("eps_var", [128, B])
    squares = [sb(f"squares{k}", [128, 16 * C]) for k in range(2)]
    ln_sum, ln_cent, ln_sq, ln_var, ln_eps, ln_rstd = (sem("ln_" + n) for n in ("sum", "centred", "squared", "var", "eps", "rstd"))

    def blk(t, b):
        return t[:, 16 * b:16 * (b + 1)]

    def norm_dve(v, k, src):
        def variance(b):
            v.wait_ge(ln_sq, 4 * k + b + 1)
            nc.vector.tensor_reduce(blk(rowsq, b), squares[b % 2][:, :].rearrange("p (b c) -> p b c", c=C), X, ALU.add).then_inc(ln_var, 1)
        for b in range(4):
            nc.vector.tensor_reduce(blk(rowsum, b), blk(src, b), X, ALU.add).then_inc(ln_sum, 1)
            if b:
                variance(b - 1)
            v.wait_ge(ln_sum, 4 * k + b + 1)
            nc.vector.scalar_tensor_tensor(blk(xc, b), blk(rowsum, b).unsqueeze(2).to_broadcast([128, 16, C]), -1.0 / C,
                                           blk(src, b), ALU.mult, ALU.add).then_inc(ln_cent, 1)
        variance(3)

    def norm_act(act, k):
        for b in range(4):
            act.wait_ge(ln_cent, 4 * k + b + 1)
            if b >= 2:
                act.wait_ge(ln_var, 4 * k + b - 1)
            nc.scalar.activation(squares[b % 2][:, :].rearrange("p (b c) -> p b c", c=C), blk(xc, b), ACT.Square).then_inc(ln_sq, 1)

    def norm_pool(pool, k):
        for b in range(4):
            pool.wait_ge(ln_var, 4 * k + b + 1)
            nc.gpsimd.tensor_scalar(blk(eps_var, b), blk(rowsq, b), 1.0 / C, EPS, ALU.mult, ALU.add).then_inc(ln_eps, 1)
            pool.wait_ge(ln_eps, 4 * k + b + 1)
            nc.gpsimd.tensor_tensor(blk(rstd, b), blk(eps_var, b), half_neg[:, 0:1].to_broadcast([128, 16]), ALU.pow).then_inc(ln_rstd, 1)

    def rstd_of(first, n):
        return rstd[:, bass.ds(first, n)].unsqueeze(2).to_broadcast([128, n, C])

    big = [big1, big2]

    def lane(at, cols):
        return [big[l][:, at:at + cols] for l in range(2)]
    xs, xT, a_q, a_k = lane(0, 128), lane(128, 128), lane(256, 128), lane(384, 128)
    a_v = lane(512, 2 * 168)
    a_kz = lane(1024, 2048)
    a_P, a_PT = lane(3072, 1024), lane(4096, 1024)
    a_mx, a_rs, a_o, a_oT = lane(5120, 8), lane(5128, 8), lane(5136, 128), lane(5264, 128)
    bias16 = [sb(f"bias16_{k}", [128, HEADS * L], BF16) for k in range(3)]
    bias_left = big2[:, 6500:7524]
    a_bqs, a_pb = sb("a_bqs", [128, 1]), sb("a_pb", [128, 128])
    (a_xs_r, a_t_r, a_xT_r, a_qkv_r, a_q_r, a_k_r, a_kz_r, a_sc_r, a_mx_r, a_e_r, a_pt_r, a_pta_r, a_ptv_r, a_av_r, a_rs_r,
     a_o_r, a_ot_r, a_oT_r, a_pr_r, a_h_r) = (sem("2_" + n) for n in (
         "rows", "rowsT", "rowsT_copied", "qkv", "q_v_ready", "k_ready", "k_spread", "scores", "max", "exp", "pT", "pT_lo", "pT_hi",
         "attended", "rsum", "heads_out", "outT", "outT_copied", "projected", "h_written"))
    a_split, a_pb_ps, a_pb_r, a_ones = sem("2_bias_split"), sem("2_pb_product"), sem("2_pb"), sem("2_ones")

    def stage2_pool(pool):
        with pool.Fori(0, NP // 2) as i:
            for l in range(2):
                n = i * 2 + (l + 1)
                pool.wait_ge(a_h_r, n)
                nc.gpsimd.tensor_tensor(xs[l].rearrange("p (b c) -> p b c", c=C), xc[:, bass.ds(i * 4 + 2 * l, 2), :],
                                        rstd_of(i * 4 + 2 * l, 2), ALU.mult).then_inc(a_xs_r, 1)
            for s in range(2):
                for l in range(2):
                    n = i * 2 + (l + 1)
                    pool.wait_ge(a_k_r, n)
                    nc.gpsimd.tensor_tensor(a_kz[l][:, 1024 * s:1024 * (s + 1)].rearrange("p (h k) -> p h k", h=8),
                                            a_k[l].unsqueeze(1).to_broadcast([128, 8, 128]),
                                            c("a_mask", 8 * s, 8 * s + 8).unsqueeze(2).to_broadcast([128, 8, 128]), ALU.mult).then_inc(a_kz_r, 1)

    def stage2_pe(pe):
        with pe.Fori(0, NP // 2) as i:
            LN = [(l, i * 2 + (l + 1)) for l in range(2)]
            for l, n in LN:
                pe.wait_ge(a_xs_r, n)
                nc.tensor.transpose(T(l, 0)[:, 0:128], xs[l], eye).then_inc(a_t_r, 1)
            for l, n in LN:
                pe.wait_ge(a_xT_r, n)
                nc.tensor.matmul(T(l, 0)[:, 128:256], c("a_q"), xT[l], start=True, stop=True)
                nc.tensor.matmul(T(l, 0)[:, 256:384], xT[l], c("a_v"), start=True, stop=True)
                nc.tensor.matmul(T(l, 1)[:, 0:128], c("a_k"), xT[l], start=True, stop=True).then_inc(a_qkv_r, 1)
            for s in range(2):
                for l, n in LN:
                    m = i * 4 + (2 * s + l + 1)
                    pe.wait_ge(a_q_r, n)
                    pe.wait_ge(a_kz_r, m)
                    if s:
                        pe.wait_ge(a_o_r, m - 2)
                    for k in range(2):
                        for part in range(3):
                            nc.tensor.matmul(T(l, k), eye16[:, :], bias16[part][:, 512 * k:512 * (k + 1)], start=(part == 0), stop=False)
                        mm = nc.tensor.matmul(T(l, k), a_q[l], a_kz[l][:, 1024 * s + 512 * k:1024 * s + 512 * (k + 1)], start=False, stop=True)
                    mm.then_inc(a_sc_r, 1)
                for l, n in LN:
                    m = i * 4 + (2 * s + l + 1)
                    pe.wait_ge(a_e_r, m)
                    for k in range(8):
                        mm = nc.tensor.transpose(T(l, 2 + k // 4)[:, 128 * (k % 4):128 * (k % 4 + 1)], a_P[l][:, 128 * k:128 * (k + 1)], eye)
                    mm.then_inc(a_pt_r, 1)
                for l, n in LN:
                    m = i * 4 + (2 * s + l + 1)
                    pe.wait_ge(a_pta_r, m)
                    pe.wait_ge(a_ptv_r, m)
                    for k in range(8):
                        mm = nc.tensor.matmul(T(l, k // 4)[:, 96 * (k % 4):96 * (k % 4 + 1)], a_PT[l][:, 128 * k:128 * (k + 1)],
                                              a_v[l][:, 168 * s + 9 * k:168 * s + 9 * k + 96], start=True, stop=True)
                    mm.then_inc(a_av_r, 1)
            for l, n in LN:
                pe.wait_ge(a_o_r, i * 4 + (l + 3))
                nc.tensor.transpose(T(l, 2)[:, 0:128], a_o[l], eye).then_inc(a_ot_r, 1)
            for l, n in LN:
                pe.wait_ge(a_oT_r, n)
                nc.tensor.matmul(T(l, 3)[:, 0:128], a_oT[l], c("a_p"), start=True, stop=False)
                nc.tensor.matmul(T(l, 3)[:, 0:128], eye, a_pb[:, :], start=False, stop=True).then_inc(a_pr_r, 1)

    def stage2_act(act):
        with act.Fori(0, NP // 2) as i:
            LN = [(l, i * 2 + (l + 1)) for l in range(2)]
            for l, n in LN:
                act.wait_ge(a_t_r, n)
                nc.scalar.copy(xT[l], T(l, 0)[:, 0:128]).then_inc(a_xT_r, 1)
            for l, n in LN:
                act.wait_ge(a_qkv_r, n)
                nc.scalar.activation(a_q[l], T(l, 0)[:, 128:256], ACT.Identity, bias=a_bqs[:, 0:1], scale=HD ** -0.5)
                for s in range(2):
                    m = nc.scalar.copy(a_v[l][:, 168 * s:168 * s + 72].rearrange("p (h d) -> p h d", h=8)[:, :, 0:8],
                                       T(l, 0)[:, 256 + 64 * s:320 + 64 * s].rearrange("p (h d) -> p h d", h=8))
                m.then_inc(a_q_r, 1)
            for s in range(2):
                for l, n in LN:
                    m = i * 4 + (2 * s + l + 1)
                    act.wait_ge(a_mx_r, m)
                    for k in range(8):
                        mm = nc.scalar.activation(a_P[l][:, 128 * k:128 * (k + 1)], T(l, k // 4)[:, 128 * (k % 4):128 * (k % 4 + 1)],
                                                  ACT.Exp, bias=a_mx[l][:, k:k + 1])
                    mm.then_inc(a_e_r, 1)
                for l, n in LN:
                    m = i * 4 + (2 * s + l + 1)
                    act.wait_ge(a_pt_r, m)
                    nc.scalar.copy(a_PT[l][:, 0:512], T(l, 2)).then_inc(a_pta_r, 1)
            for l, n in LN:
                act.wait_ge(a_ot_r, n)
                nc.scalar.copy(a_oT[l], T(l, 2)[:, 0:128]).then_inc(a_oT_r, 1)

    def stage2_dve(v):
        with v.Fori(0, NP // 2) as i:
            LN = [(l, i * 2 + (l + 1)) for l in range(2)]
            for l, n in LN:
                v.wait_ge(a_qkv_r, n)
                nc.vector.tensor_scalar(a_k[l], T(l, 1)[:, 0:128], c("a_bk"), None, ALU.add).then_inc(a_k_r, 1)
            for s in range(2):
                for l, n in LN:
                    m = i * 4 + (2 * s + l + 1)
                    v.wait_ge(a_sc_r, m)
                    nc.vector.tensor_reduce(a_mx[l], T(l, 0, 2).rearrange("p (h k) -> p h k", h=8), X, ALU.max, negate=True).then_inc(a_mx_r, 1)
                for l, n in LN:
                    m = i * 4 + (2 * s + l + 1)
                    v.wait_ge(a_pt_r, m)
                    nc.vector.tensor_copy(a_PT[l][:, 512:1024], T(l, 3)).then_inc(a_ptv_r, 1)
                for l, n in LN:
                    m = i * 4 + (2 * s + l + 1)
                    v.wait_ge(a_av_r, m)
                    res = T(l, 0, 2).rearrange("p (b x) -> p b x", b=2)[:, :, 0:384].rearrange("p b (j y) -> p b j y", y=96)
                    rs = a_rs[l].rearrange("p (b j) -> p b j", b=2)
                    nc.vector.reciprocal(rs, res[:, :, :, 8]).then_inc(a_rs_r, 1)
                    v.wait_ge(a_rs_r, m)
                    nc.vector.tensor_tensor(a_o[l][:, 64 * s:64 * s + 64].rearrange("p (b j d) -> p b j d", b=2, j=4), res[:, :, :, 0:8],
                                            rs.unsqueeze(3).to_broadcast([128, 2, 4, 8]), ALU.mult).then_inc(a_o_r, 1)
            for l, n in LN:
                v.wait_ge(a_pr_r, n)
                hp = h[:, bass.ds(i * 4 + 2 * l, 2), :]
                nc.vector.tensor_tensor(hp, hp, T(l, 3)[:, 0:128].rearrange("p (b c) -> p b c", c=C), ALU.add).then_inc(a_h_r, 1)

    f_xs1 = lane(256, 192)
    f_w, f_wT = lane(512, 1024), lane(1536, 1024)
    f_tk, f_tT = lane(2560, 512), lane(3072, 512)
    f_uz = lane(3584, 1024)
    f_vw = lane(4608, 768)
    f_le, f_ebd, f_eT = lane(5376, 512), lane(5888, 1024), lane(6912, 1024)
    f_mx, f_rs, f_nr, f_lmx, f_zr = lane(7936, 16), lane(7952, 16), lane(7968, 8), lane(7976, 8), lane(7984, 8)
    f_zz, f_oT = f_le, xT
    fA, fB, fX = sb("fA", [128, 1024]), sb("fB", [128, 1024]), sb("fX", [128, 1024])
    fFT, fXT, fM, fV = big1[0:64, 0:512], big1[0:64, 512:1024], big1[0:64, 1024:1536], big1[0:64, 1536:2048]
    fGT, fsum, fti = big1[0:64, 2048:2112], big1[0:64, 2112:2128], sb("f_tinv", [128, 8])
    f_dve, f_pe = sem("3_setup_vector"), sem("3_setup_products")
    (f_xs_r, f_xs1_r, f_t_r, f_xT_r, f_lg_r, f_mx_r, f_sub_r, f_exp_r, f_sum_r, f_rs_r, f_w_r, f_wt_r, f_s_r, f_wT_r, f_nr_r, f_nr2_r,
     f_tk_r, f_tt_r, f_tT_r, f_u_r, f_vw_r, f_uz0_r, f_uz1_r, f_vwc_r, f_l_r, f_lmx_r, f_ls_r, f_e_r, f_et_r, f_eTa_r, f_eTv_r, f_z_r,
     f_zr_r, f_zz_r, f_o_r, f_oT_r, f_ot_r, f_h_r) = (sem("3_" + n) for n in (
         "rows", "rows_plus_1", "rowsT", "rowsT_copied", "logits", "max", "shifted", "exp", "sum", "rsum", "weights", "weightsT", "slices",
         "weightsT_copied", "norm", "rnorm", "tokens", "tokensT", "tokensT_copied", "keys_mixed", "values_mixed", "mixed_0", "mixed_1",
         "values_copied", "pairs", "pairs_max", "pairs_shifted", "pairs_exp", "pairsT", "pairsT_lo", "pairsT_hi", "slices_out", "rpairs",
         "slices_scaled", "outT", "outT_biased", "out", "h_written"))

    def heads(ap):
        return ap.rearrange("p (h c) -> p h c", h=8)

    def setup3_dve(v):
        k = [0]

        def step(ins):
            k[0] += 1
            ins.then_inc(f_dve, 1)
            v.wait_ge(f_dve, k[0])
        for t in (fA, fB, fX):
            step(nc.vector.memset(t[:, :], 0.0))
        step(nc.vector.tensor_scalar(fti[:, :], c("f_temp"), 0.1, 5.0, ALU.max, ALU.min))
        step(nc.vector.reciprocal(fti[:, :], fti[:, :]))
        for raw, b, to, at in (("f_fxT", "f_bfxT", fFT, 0), ("f_xT", "f_bxT", fXT, 8)):
            part = fsum[:, at:at + 8]
            step(nc.vector.tensor_reduce(part, heads(c(raw)[0:64]), X, ALU.add))
            step(nc.vector.tensor_tensor(part, c(b)[0:64], part, ALU.subtract))
            step(nc.vector.scalar_tensor_tensor(heads(to), part.unsqueeze(2).to_broadcast([64, 8, 64]), 1.0 / C, heads(c(raw)[0:64]),
                                                ALU.mult, ALU.add))
        v.wait_ge(f_pe, 1)
        step(nc.vector.tensor_copy(fGT, T(0, 0)[0:64, 0:64]))
        step(nc.vector.tensor_copy(fV, T(0, 1)[0:64, :]))
        bs = heads(fX[0:64, 0:512])
        step(nc.vector.scalar_tensor_tensor(bs, c("f_bslice")[0:64].unsqueeze(1).to_broadcast([64, 8, 64]), 1.0 / C,
                                            heads(T(0, 2)[0:64, :]), ALU.mult, ALU.add))
        step(nc.vector.tensor_tensor(bs, bs, fti[0:64, :].unsqueeze(2).to_broadcast([64, 8, 64]), ALU.mult))
        bs = heads(fX[64:128, 512:1024])
        step(nc.vector.scalar_tensor_tensor(bs, c("f_bslice")[64:128].unsqueeze(1).to_broadcast([64, 8, 64]), 1.0 / C,
                                            heads(T(0, 3)[64:128, :]), ALU.mult, ALU.add))
        step(nc.vector.tensor_tensor(bs, bs, fti[64:128, :].unsqueeze(2).to_broadcast([64, 8, 64]), ALU.mult))
        v.wait_ge(f_pe, 2)
        step(nc.vector.tensor_copy(fM, T(1, 0)[0:64, :]))
        v.wait_ge(f_pe, 3)
        for s in range(2):
            r = slice(64 * s, 64 * s + 64)
            step(nc.vector.tensor_scalar(fA[r, 512 * s:512 * (s + 1)], T(0, 0)[r, :], 64.0 ** -0.5, None, ALU.mult))
            step(nc.vector.tensor_copy(fB[r, 512 * s:512 * (s + 1)], T(0, 1)[r, :]))
        for l in range(2):
            step(nc.vector.memset(f_xs1[l], 1.0))
            step(nc.vector.memset(f_vw[l], 1.0))
            step(nc.vector.memset(f_uz[l], 0.0))
            step(nc.vector.memset(f_ebd[l], 0.0))
    SETUP3 = 30

    def setup3_pe(pe):
        pe.wait_ge(f_dve, 11)
        nc.tensor.matmul(T(0, 0)[0:64, 0:64], c("f_wkT")[0:64], c("f_wqT")[0:64], start=True, stop=True)
        nc.tensor.matmul(T(0, 1)[0:64, :], c("f_wvT")[0:64], c("f_out")[0:64], start=True, stop=True)
        for k in range(8):
            nc.tensor.matmul(T(0, 2)[0:64, 64 * k:64 * k + 64], fXT[:, 64 * k:64 * k + 64], c("f_slice")[0:64], start=True, stop=True)
        for k in range(8):
            m = nc.tensor.matmul(T(0, 3)[64:128, 64 * k:64 * k + 64], fXT[:, 64 * k:64 * k + 64], c("f_slice")[0:64], start=True, stop=True)
        m.then_inc(f_pe, 1)
        pe.wait_ge(f_dve, 17)
        nc.tensor.matmul(T(1, 0)[0:64, :], fGT, fFT, start=True, stop=True).then_inc(f_pe, 1)
        pe.wait_ge(f_dve, 18)
        for r in (slice(0, 64), slice(64, 128)):
            for k in range(8):
                q = slice(64 * k, 64 * k + 64)
                nc.tensor.matmul(T(0, 0)[r, q], fFT[:, q], fM[:, q], start=True, stop=True)
                m = nc.tensor.matmul(T(0, 1)[r, q], fFT[:, q], fV[:, q], start=True, stop=True)
        m.then_inc(f_pe, 1)

    def stage3_pool(pool):
        with pool.Fori(0, NP // 2) as i:
            LN = [(l, i * 2 + (l + 1)) for l in range(2)]
            for l, n in LN:
                pool.wait_ge(f_h_r, n)
                nc.gpsimd.tensor_tensor(xs[l].rearrange("p (b c) -> p b c", c=C), xc[:, bass.ds(i * 4 + 2 * l, 2), :],
                                        rstd_of(i * 4 + 2 * l, 2), ALU.mult).then_inc(f_xs_r, 1)
                pool.wait_ge(f_xs_r, n)
                nc.gpsimd.tensor_tensor(f_xs1[l].rearrange("p (s c) -> p s c", s=2)[:, :, 0:64], xs[l].rearrange("p (s c) -> p s c", s=2),
                                        one[:, 0:1].unsqueeze(1).to_broadcast([128, 2, 64]), ALU.add).then_inc(f_xs1_r, 1)
            for l, n in LN:
                pool.wait_ge(f_rs_r, n)
                w = f_w[l].rearrange("p (h g) -> p h g", g=64)
                nc.gpsimd.tensor_tensor(w, w, f_rs[l].unsqueeze(2).to_broadcast([128, 16, 64]), ALU.mult).then_inc(f_w_r, 1)

    def regions(l):
        return T(l, 0, 2).rearrange("p (b x) -> p b x", b=2)[:, :, 0:384].rearrange("p b (j y) -> p b j y", y=96)

    def stage3_pe(pe):
        with pe.Fori(0, NP // 2) as i:
            LN = [(l, i * 2 + (l + 1)) for l in range(2)]
            for l, n in LN:
                pe.wait_ge(f_xs_r, n)
                nc.tensor.transpose(T(l, 0)[:, 0:128], xs[l], eye).then_inc(f_t_r, 1)
            for l, n in LN:
                pe.wait_ge(f_xT_r, n)
                for s in range(2):
                    m = nc.tensor.matmul(T(l, s), xT[l], fX[:, 512 * s:512 * (s + 1)], start=True, stop=True)
                m.then_inc(f_lg_r, 1)
            for l, n in LN:
                pe.wait_ge(f_w_r, n)
                pe.wait_ge(f_xs1_r, n)
                for k in range(8):
                    m = nc.tensor.matmul(regions(l)[:, k // 4, k % 4, :], f_w[l][:, 128 * k:128 * k + 128],
                                         f_xs1[l][:, 96 * (k // 4):96 * (k // 4) + 96], start=True, stop=True)
                m.then_inc(f_s_r, 1)
                for k in range(8):
                    m = nc.tensor.transpose(T(l, 2 + k // 4)[:, 128 * (k % 4):128 * (k % 4) + 128], f_w[l][:, 128 * k:128 * k + 128], eye)
                m.then_inc(f_wt_r, 1)
            for l, n in LN:
                pe.wait_ge(f_tk_r, n)
                pe.wait_ge(f_wT_r, n)
                for k in range(4):
                    m = nc.tensor.transpose(T(l, 2)[:, 128 * k:128 * k + 128], f_tk[l][:, 128 * k:128 * k + 128], eye)
                m.then_inc(f_tt_r, 1)
            for l, n in LN:
                pe.wait_ge(f_tT_r, n)
                for s in range(2):
                    for k in range(8):
                        m = nc.tensor.matmul(T(l, 3)[64 * s:64 * s + 64, 64 * k:64 * k + 64], fA[:, 512 * s + 64 * k:512 * s + 64 * k + 64],
                                             f_tT[l][:, 64 * k:64 * k + 64], start=True, stop=True)
                m.then_inc(f_u_r, 1)
                for s in range(2):
                    for k in range(8):
                        o = 64 * (4 * s + k // 2)
                        m = nc.tensor.matmul(T(l, 1)[64 * (k % 2):64 * (k % 2) + 64, o:o + 64], f_tT[l][:, 64 * k:64 * k + 64],
                                             fB[:, 512 * s + 64 * k:512 * s + 64 * k + 64], start=True, stop=True)
                m.then_inc(f_vw_r, 1)
            for l, n in LN:
                pe.wait_ge(f_uz0_r, n)
                pe.wait_ge(f_uz1_r, n)
                for s in range(2):
                    for k in range(8):
                        o = 64 * (4 * s + k // 2)
                        m = nc.tensor.matmul(T(l, 0)[64 * (k % 2):64 * (k % 2) + 64, o:o + 64],
                                             f_uz[l][:, 512 * s + 64 * k:512 * s + 64 * k + 64], f_tT[l][:, 64 * k:64 * k + 64], start=True, stop=True)
                m.then_inc(f_l_r, 1)
            for l, n in LN:
                pe.wait_ge(f_e_r, n)
                for k in range(8):
                    m = nc.tensor.transpose(T(l, 2 + k // 4)[:, 128 * (k % 4):128 * (k % 4) + 128], f_ebd[l][:, 128 * k:128 * k + 128], eye)
                m.then_inc(f_et_r, 1)
            for l, n in LN:
                pe.wait_ge(f_eTa_r, n)
                pe.wait_ge(f_eTv_r, n)
                pe.wait_ge(f_vwc_r, n)
                for k in range(8):
                    m = nc.tensor.matmul(regions(l)[:, k // 4, k % 4, :], f_eT[l][:, 128 * k:128 * k + 128],
                                         f_vw[l][:, 96 * k:96 * k + 96], start=True, stop=True)
                m.then_inc(f_z_r, 1)
            for l, n in LN:
                pe.wait_ge(f_zz_r, n)
                for s in range(2):
                    for j in range(4):
                        k = 4 * s + j
                        m = nc.tensor.matmul(T(l, 2)[64 * s:64 * s + 64, 0:128], f_zz[l][:, 64 * k:64 * k + 64],
                                             f_wT[l][:, 128 * k:128 * k + 128], start=(j == 0), stop=(j == 3))
                m.then_inc(f_o_r, 1)
            for l, n in LN:
                pe.wait_ge(f_oT_r, n)
                nc.tensor.transpose(T(l, 3)[:, 0:128], f_oT[l], eye).then_inc(f_ot_r, 1)

    def stage3_act(act):
        with act.Fori(0, NP // 2) as i:
            LN = [(l, i * 2 + (l + 1)) for l in range(2)]
            for l, n in LN:
                act.wait_ge(f_t_r, n)
                nc.scalar.activation(xT[l], T(l, 0)[:, 0:128], ACT.Identity, bias=one[:, 0:1]).then_inc(f_xT_r, 1)
            for l, n in LN:
                act.wait_ge(f_sub_r, n)
                nc.scalar.activation(f_w[l], f_w[l], ACT.Exp).then_inc(f_exp_r, 1)
            for l, n in LN:
                act.wait_ge(f_wt_r, n)
                nc.scalar.copy(f_wT[l], T(l, 2, 2)).then_inc(f_wT_r, 1)
            for l, n in LN:
                act.wait_ge(f_tt_r, n)
                nc.scalar.copy(f_tT[l], T(l, 2)).then_inc(f_tT_r, 1)
            for l, n in LN:
                act.wait_ge(f_u_r, n)
                nc.scalar.copy(f_uz[l][0:64, 0:512], T(l, 3)[0:64, :]).then_inc(f_uz0_r, 1)
                act.wait_ge(f_vw_r, n)
                nc.scalar.copy(f_vw[l].rearrange("p (k y) -> p k y", y=96)[:, :, 0:64], T(l, 1).rearrange("p (k c) -> p k c", c=64)).then_inc(f_vwc_r, 1)
            for l, n in LN:
                act.wait_ge(f_ls_r, n)
                for r in (slice(0, 64), slice(64, 128)):
                    m = nc.scalar.activation(f_ebd[l][r, :].rearrange("p (k y) -> p k y", y=128)[:, :, r],
                                             f_le[l][r, :].rearrange("p (k c) -> p k c", c=64), ACT.Exp)
                m.then_inc(f_e_r, 1)
            for l, n in LN:
                act.wait_ge(f_et_r, n)
                nc.scalar.copy(f_eT[l][:, 0:512], T(l, 2)).then_inc(f_eTa_r, 1)
            for l, n in LN:
                act.wait_ge(f_o_r, n)
                nc.scalar.activation(f_oT[l], T(l, 2)[:, 0:128], ACT.Identity, bias=c("f_bout")).then_inc(f_oT_r, 1)

    def stage3_dve(v):
        with v.Fori(0, NP // 2) as i:
            LN = [(l, i * 2 + (l + 1)) for l in range(2)]
            for l, n in LN:
                v.wait_ge(f_lg_r, n)
                lg = T(l, 0, 2).rearrange("p (h g) -> p h g", g=64)
                nc.vector.tensor_reduce(f_mx[l], lg, X, ALU.max).then_inc(f_mx_r, 1)
                v.wait_ge(f_mx_r, n)
                nc.vector.tensor_tensor(f_w[l].rearrange("p (h g) -> p h g", g=64), lg, f_mx[l].unsqueeze(2).to_broadcast([128, 16, 64]),
                                        ALU.subtract).then_inc(f_sub_r, 1)
            for l, n in LN:
                v.wait_ge(f_exp_r, n)
                nc.vector.tensor_reduce(f_rs[l], f_w[l].rearrange("p (h g) -> p h g", g=64), X, ALU.add).then_inc(f_sum_r, 1)
                v.wait_ge(f_sum_r, n)
                nc.vector.reciprocal(f_rs[l], f_rs[l]).then_inc(f_rs_r, 1)
            for l, n in LN:
                v.wait_ge(f_s_r, n)
                nr = f_nr[l].rearrange("p (s j) -> p s j", s=2)
                nc.vector.tensor_scalar(nr, regions(l)[:, :, :, 64], 1e-5, None, ALU.add).then_inc(f_nr_r, 1)
                v.wait_ge(f_nr_r, n)
                nc.vector.reciprocal(f_nr[l], f_nr[l]).then_inc(f_nr2_r, 1)
                v.wait_ge(f_nr2_r, n)
                nc.vector.tensor_tensor(f_tk[l].rearrange("p (j s c) -> p s j c", j=4, s=2), regions(l)[:, :, :, 0:64],
                                        nr.unsqueeze(3).to_broadcast([128, 2, 4, 64]), ALU.mult).then_inc(f_tk_r, 1)
            for l, n in LN:
                v.wait_ge(f_u_r, n)
                nc.vector.tensor_copy(f_uz[l][64:128, 512:1024], T(l, 3)[64:128, :]).then_inc(f_uz1_r, 1)
            for l, n in LN:
                v.wait_ge(f_l_r, n)
                nc.vector.tensor_reduce(f_lmx[l], T(l, 0).rearrange("p (k c) -> p k c", c=64), X, ALU.max).then_inc(f_lmx_r, 1)
                v.wait_ge(f_lmx_r, n)
                nc.vector.tensor_tensor(f_le[l].rearrange("p (k c) -> p k c", c=64), T(l, 0).rearrange("p (k c) -> p k c", c=64),
                                        f_lmx[l].unsqueeze(2).to_broadcast([128, 8, 64]), ALU.subtract).then_inc(f_ls_r, 1)
            for l, n in LN:
                v.wait_ge(f_et_r, n)
                nc.vector.tensor_copy(f_eT[l][:, 512:1024], T(l, 3)).then_inc(f_eTv_r, 1)
            for l, n in LN:
                v.wait_ge(f_z_r, n)
                zr = f_zr[l].rearrange("p (s j) -> p s j", s=2)
                nc.vector.reciprocal(zr, regions(l)[:, :, :, 64]).then_inc(f_zr_r, 1)
                v.wait_ge(f_zr_r, n)
                nc.vector.tensor_tensor(f_zz[l].rearrange("p (s j c) -> p s j c", s=2, j=4), regions(l)[:, :, :, 0:64],
                                        zr.unsqueeze(3).to_broadcast([128, 2, 4, 64]), ALU.mult).then_inc(f_zz_r, 1)
            for l, n in LN:
                v.wait_ge(f_ot_r, n)
                hp = h[:, bass.ds(i * 4 + 2 * l, 2), :]
                nc.vector.tensor_tensor(hp, hp, T(l, 3)[:, 0:128].rearrange("p (b c) -> p b c", c=C), ALU.add).then_inc(f_h_r, 1)

    xg = big1[:, :].rearrange("p (t b) -> p t b", b=B)
    ys = big2[:, :].rearrange("p (t b) -> p t b", b=B)
    r_x1, r_res = sem("4_normed"), sem("4_residual")
    r_dup, r_t, r_xgf, r_xgr = sem("4_rows"), sem("4_rowsT"), sem("4_forward"), sem("4_reverse")
    dup = [squares[k][:, 0:512].rearrange("p (b d c) -> p b d c", b=4, d=2) for k in range(2)]
    NJ4 = B // 4

    def stage4_norm_dve(v):
        for b in range(4):
            v.wait_ge(ln_rstd, 8 + b + 1)
            nc.vector.tensor_tensor(blk(xc, b), blk(xc, b), blk(rstd, b).unsqueeze(2).to_broadcast([128, 16, C]), ALU.mult).then_inc(r_x1, 1)
            v.wait_ge(r_x1, b + 1)
            nc.vector.tensor_tensor(blk(h, b), blk(h, b), blk(xc, b), ALU.add).then_inc(r_res, 1)
        v.wait_ge(r_res, 4)
        norm_dve(v, 3, xc)

    def stage4_pool(pool):
        with pool.Fori(0, NJ4 // 2) as i:
            for l in range(2):
                n = i * 2 + (l + 1)
                pool.wait_ge(r_t, n)
                nc.gpsimd.tensor_tensor(dup[l], xc[:, bass.ds(i * 8 + 4 * l, 4), :].unsqueeze(2).to_broadcast([128, 4, 2, C]),
                                        rstd[:, bass.ds(i * 8 + 4 * l, 4)].unsqueeze(2).unsqueeze(3).to_broadcast([128, 4, 2, C]),
                                        ALU.mult).then_inc(r_dup, 1)

    def stage4_pe(pe):
        with pe.Fori(0, NJ4 // 2) as i:
            for l in range(2):
                n = i * 2 + (l + 1)
                pe.wait_ge(r_dup, n)
                pe.wait_ge(r_xgf, n)
                pe.wait_ge(r_xgr, n)
                for b in range(4):
                    m = nc.tensor.transpose(T(l, 0)[:, 128 * b:128 * b + 128], squares[l][:, 128 * b:128 * b + 128], eye)
                m.then_inc(r_t, 1)

    def stage4_act(act):
        with act.Fori(0, NJ4 // 2) as i:
            for l in range(2):
                act.wait_ge(r_t, i * 2 + (l + 3))
                nc.scalar.activation(xg[0:64, :, bass.ds(i * 8 + 4 * l, 4)].rearrange("p t b -> p b t"),
                                     T(l, 0)[0:64, :].rearrange("p (b t) -> p b t", b=4), ACT.Identity,
                                     bias=c("g_lnb")[0:64], scale=c("g_lng")[0:64]).then_inc(r_xgf, 1)

    def stage4_dve(v):
        with v.Fori(0, NJ4 // 2) as i:
            for l in range(2):
                v.wait_ge(r_t, i * 2 + (l + 3))
                nc.vector.tensor_scalar(xg[64:128, :, bass.ds(i * 8 + 4 * l, 4)].rearrange("p t b -> p b t"),
                                        T(l, 0)[64:128, :].rearrange("p (b t) -> p b t", b=4)[:, :, ::-1],
                                        c("g_lng")[64:128], c("g_lnb")[64:128], ALU.mult, ALU.add).then_inc(r_xgr, 1)

    UN = 16
    g_bias, g_nbz = sb("g_bias", [128, 3]), sb("g_nbz", [128, 1])
    g_set, g_r, g_z, g_omz, g_t, g_t2, g_n, g_a, g_b, g_hs = (
        [sb(f"g_{n}{u}", [128, B]) for u in range(2)] for n in ("set", "r", "z", "omz", "t", "t2", "n", "a", "b", "h"))
    (g_setup, g_rp, g_hp, g_zp, g_rr, g_zr, g_tr, g_t2r, g_nr, g_ar, g_br, g_hr, g_yr) = (sem("5_" + n) for n in (
        "setup", "r_sum", "hn_sum", "z_sum", "r", "z", "gated", "n_sum", "n", "a", "b", "h", "stored"))

    GS = 8

    def gru_x(gate, half, group, first):
        w = 64 * GS // 2
        nc.tensor.matmul(T(group, gate)[:, w * half:w * (half + 1)], c("g_ih", 128 * gate, 128 * gate + 128),
                         big1[:, bass.ds(first * B + w * half, w)], start=(half == 0), stop=True, skip_group_check=True)

    def gru_products(to, gate, state, start):
        for d in range(2):
            m = nc.tensor.matmul(to[64 * d:64 * d + 64, :], c("g_hh", 128 * gate + 64 * d, 128 * gate + 64 * d + 64), state[:, :],
                                 start=start, stop=True, skip_group_check=True)
        return m

    def gru_pe(pe):
        def steps(i, last):
            for st in range(UN):
                u, group, col = st % 2, st // GS, B * (st % GS)
                n = i * UN + st
                R, Z = (T(group, k)[:, col:col + B] for k in range(2))
                HN = T(u, 3)[:, 0:B]
                pe.wait_ge(g_br, n + 1)
                gru_products(R, 0, g_b[1 - u], False)
                gru_products(HN, 2, g_b[1 - u], True)
                pe.wait_ge(g_ar, n + 1)
                gru_products(R, 0, g_a[1 - u], False).then_inc(g_rp, 1)
                gru_products(HN, 2, g_a[1 - u], False).then_inc(g_hp, 1)
                pe.wait_ge(g_hr, n + 1)
                gru_products(Z, 1, g_hs[1 - u], False).then_inc(g_zp, 1)
                if st % GS < 6 and not (last and group == 1):
                    gru_x(st % GS // 2, st % 2, 1 - group, i * UN + GS * (group + 1))
        for gate in range(3):
            for half in range(2):
                gru_x(gate, half, 0, 0)
        with pe.Fori(0, L // UN - 1) as i:
            steps(i, False)
        steps(L // UN - 1, True)

    def gru_act(act):
        with act.Fori(0, L // UN) as i:
            for st in range(UN):
                u, n = st % 2, i * UN + (st + 1)
                group, col = st // GS, B * (st % GS)
                act.wait_ge(g_rp, n)
                nc.scalar.activation(g_r[u][:, :], T(group, 0)[:, col:col + B], ACT.Sigmoid, bias=g_bias[:, 0:1]).then_inc(g_rr, 1)
                act.wait_ge(g_zp, n)
                nc.scalar.activation(g_z[u][:, :], T(group, 1)[:, col:col + B], ACT.Sigmoid, bias=g_bias[:, 1:2])
                nc.scalar.activation(g_omz[u][:, :], T(group, 1)[:, col:col + B], ACT.Sigmoid, bias=g_nbz[:, 0:1], scale=-1.0).then_inc(g_zr, 1)
                act.wait_ge(g_t2r, n)
                nc.scalar.activation(g_n[u][:, :], g_t2[u][:, :], ACT.Tanh, bias=c("g_bih", 2, 3)).then_inc(g_nr, 1)

    def gru_dve(v):
        with v.Fori(0, L // UN) as i:
            for st in range(UN):
                u, n = st % 2, i * UN + (st + 1)
                group, col = st // GS, B * (st % GS)
                v.wait_ge(g_hp, n)
                v.wait_ge(g_rr, n)
                nc.vector.scalar_tensor_tensor(g_t[u][:, :], T(u, 3)[:, 0:B], c("g_bhh", 2, 3), g_r[u][:, :], ALU.add, ALU.mult).then_inc(g_tr, 1)
                v.wait_ge(g_tr, n)
                nc.vector.tensor_tensor(g_t2[u][:, :], T(group, 2)[:, col:col + B], g_t[u][:, :], ALU.add).then_inc(g_t2r, 1)
                v.wait_ge(g_zr, n)
                v.wait_ge(g_hr, n)
                v.wait_ge(g_yr, n)
                nc.vector.tensor_tensor(g_b[u][:, :], g_z[u][:, :], g_hs[1 - u][:, :], ALU.mult).then_inc(g_br, 1)
                v.wait_ge(g_nr, n)
                nc.vector.tensor_tensor(g_a[u][:, :], g_omz[u][:, :], g_n[u][:, :], ALU.mult).then_inc(g_ar, 1)
                v.wait_ge(g_ar, n + 1)
                nc.vector.tensor_tensor(g_hs[u][:, :], g_a[u][:, :], g_b[u][:, :], ALU.add).then_inc(g_hr, 1)

    def gru_pool(pool):
        with pool.Fori(0, L // UN) as i:
            for st in range(UN):
                u = st % 2
                t = i * UN + st
                pool.wait_ge(g_ar, t + 2)
                nc.gpsimd.tensor_tensor(big2[0:64, bass.ds(t * B, B)], g_a[u][0:64, :], g_b[u][0:64, :], ALU.add)
                nc.gpsimd.tensor_tensor(big2[64:128, bass.ds((i * (-UN) + (L - 1 - st)) * B, B)], g_a[u][64:128, :], g_b[u][64:128, :],
                                        ALU.add).then_inc(g_yr, 1)

    gg = [big1[0:64, 512 * l:512 * (l + 1)] for l in range(2)]
    cb = [big1[:, 1024 + 512 * l:1024 + 512 * (l + 1)] for l in range(2)]
    o_p, o_g, o_c, o_r, o_o, o_h = (sem("6_" + n) for n in ("products", "gate", "gated", "reverse", "projected", "h_written"))

    def stage6_pe(pe):
        with pe.Fori(0, NJ4 // 2) as i:
            LN = [(l, i * 2 + (l + 1)) for l in range(2)]
            for l, n in LN:
                pe.wait_ge(o_h, n)
                rhs = ys[:, :, bass.ds(i * 8 + 4 * l, 4)].rearrange("p t b -> p b t")
                nc.tensor.matmul(T(l, 0)[0:64, :], c("g_gate"), rhs, start=True, stop=True)
                nc.tensor.matmul(T(l, 1)[0:64, :], c("g_diff"), rhs, start=True, stop=True).then_inc(o_p, 1)
            for l, n in LN:
                pe.wait_ge(o_c, n)
                pe.wait_ge(o_r, n)
                nc.tensor.matmul(T(l, 2)[:, 0:256], eye, c("g_bout"), start=True, stop=False)
                for b in range(4):
                    m = nc.tensor.matmul(T(l, 2)[:, 64 * b:64 * b + 64], cb[l][:, 128 * b:128 * b + 128], c("g_out"), start=False, stop=(b == 3))
                m.then_inc(o_o, 1)

    def stage6_act(act):
        with act.Fori(0, NJ4 // 2) as i:
            for l in range(2):
                n = i * 2 + (l + 1)
                act.wait_ge(o_p, n)
                nc.scalar.activation(gg[l], T(l, 0)[0:64, :], ACT.Sigmoid, bias=c("g_bgate")[0:64]).then_inc(o_g, 1)
                nc.scalar.activation(cb[l][64:128, :].rearrange("p (b t) -> p b t", b=4),
                                     ys[64:128, :, bass.ds(i * 8 + 4 * l, 4)].rearrange("p t b -> p b t"), ACT.Identity).then_inc(o_r, 1)

    def stage6_dve(v):
        with v.Fori(0, NJ4 // 2) as i:
            LN = [(l, i * 2 + (l + 1)) for l in range(2)]
            for l, n in LN:
                v.wait_ge(o_g, n)
                nc.vector.tensor_tensor(cb[l][0:64, :], T(l, 1)[0:64, :], gg[l], ALU.mult).then_inc(o_c, 1)
            for l, n in LN:
                v.wait_ge(o_o, n)
                hp = h[:, bass.ds(i * 8 + 4 * l, 4), :]
                nc.vector.tensor_tensor(hp, hp, T(l, 2)[:, 0:256].rearrange("p (b c) -> p b c", c=C), ALU.add).then_inc(o_h, 1)

    NJ7 = B // 8
    m_xs = [big1[:, 512 * k:512 * (k + 1)] for k in range(2)]
    m_xT = [big1[:, 1024 + 512 * k:1024 + 512 * (k + 1)] for k in range(2)]
    m_y = [big1[:, 2048 + 512 * k:2048 + 512 * (k + 1)] for k in range(2)]
    m_red = [big1[:, 3072 + 512 * k:3072 + 512 * (k + 1)] for k in range(2)]
    hid = [big2[:, 4096 * k:4096 * (k + 1)] for k in range(2)]

    def small(at, cols):
        return [big1[:, 4096 + 1024 * k + at:4096 + 1024 * k + at + cols] for k in range(2)]
    m_lg, m_m8, m_i8 = small(0, 64), small(64, 64), small(128, 64)
    m_if, m_d, m_w1, m_w2 = small(192, 16), small(208, 8), small(216, 8), small(224, 8)
    m_e1, m_e2, m_c1, m_c2, m_comb = small(256, 64), small(320, 64), small(384, 64), small(448, 64), small(512, 64)
    (m_xs_r, m_t_r, m_xT_r, m_lg_r, m_d_r, m_ex_r, m_comb_r, m_step, m_hp, m_ra, m_rv, m_yp, m_add, m_mul, m_rd, m_h_r) = (
        sem("7_" + n) for n in ("rows", "rowsT", "rowsT_copied", "gate_logits", "top_diff", "top_exp", "combine", "gate_steps", "hidden",
                                "relu_even", "relu_odd", "expert_out", "biased", "weighted", "reduced", "h_written"))
    STEPS7 = 27

    def stage7_pool(pool):
        with pool.Fori(0, NJ7 // 2) as i:
            for l in range(2):
                J = i * 2 + l
                pool.wait_ge(m_t_r, J + 1)
                nc.gpsimd.tensor_tensor(m_xs[l].rearrange("p (b c) -> p b c", c=C), xc[:, bass.ds(i * 16 + 8 * l, 8), :],
                                        rstd_of(i * 16 + 8 * l, 8), ALU.mult).then_inc(m_xs_r, 1)
                pool.wait_ge(m_comb_r, J + 1)
                for s in range(2):
                    for p in range(4):
                        pool.wait_ge(m_add, J * 8 + (4 * s + p + 3))
                        y = m_y[p % 2].rearrange("p (e c) -> p e c", e=8)
                        nc.gpsimd.tensor_tensor(y, y, m_comb[l][:, 8 * (2 * p + s):8 * (2 * p + s) + 8].unsqueeze(2).to_broadcast([128, 8, C]),
                                                ALU.mult).then_inc(m_mul, 1)

    def stage7_pe(pe):
        with pe.Fori(0, NJ7 // 2) as i:
            for l in range(2):
                J = i * 2 + l
                pe.wait_ge(m_xs_r, J + 1)
                pe.wait_ge(m_xT_r, J + 1)
                for p in range(4):
                    m = nc.tensor.transpose(T(0, 0)[:, 128 * p:128 * p + 128], m_xs[l][:, 128 * p:128 * p + 128], eye)
                m.then_inc(m_t_r, 1)
                pe.wait_ge(m_xT_r, J + 2)
                for p in range(4):
                    m = nc.tensor.matmul(T(0, 1)[:, 16 * p:16 * p + 16], m_xT[l][:, 128 * p:128 * p + 128], c("m_g"), start=True, stop=True)
                m.then_inc(m_lg_r, 1)
                for s in range(2):
                    for e in range(8):
                        pe.wait_ge(m_ra if e % 2 == 0 else m_rv, J * 8 + (4 * s + e // 2 + 1))
                        nc.tensor.matmul(T(0, 2 + e % 2), c("m_w1", 128 * (8 * s + e), 128 * (8 * s + e + 1)), m_xT[l],
                                         start=True, stop=True).then_inc(m_hp, 1)
                for s in range(2):
                    pe.wait_ge(m_ra, J * 8 + (4 * s + 5))
                    pe.wait_ge(m_rv, J * 8 + (4 * s + 5))
                    for p in range(4):
                        pe.wait_ge(m_add, J * 8 + (4 * s + p + 1))
                        for e in range(8):
                            o = 512 * (2 * (p % 2) + e // 4) + 96 * (e % 4)
                            m = nc.tensor.matmul(pt[1][:, o:o + 96], hid[s][:, 512 * e + 128 * p:512 * e + 128 * p + 128],
                                                 c("m_w2", 64 * e, 64 * e + 96), start=True, stop=True)
                        m.then_inc(m_yp, 1)

    def stage7_act(act):
        with act.Fori(0, NJ7 // 2) as i:
            for l in range(2):
                J = i * 2 + l
                act.wait_ge(m_t_r, J + 3)
                nc.scalar.copy(m_xT[l], T(0, 0)).then_inc(m_xT_r, 1)
                act.wait_ge(m_d_r, J + 1)
                nc.scalar.activation(m_d[l], m_d[l], ACT.Exp).then_inc(m_ex_r, 1)
                for s in range(2):
                    act.wait_ge(m_yp, J * 8 + (4 * s + 4))
                    for e in range(0, 8, 2):
                        act.wait_ge(m_hp, J * 16 + (8 * s + e + 1))
                        nc.scalar.activation(hid[s][:, 512 * e:512 * (e + 1)], T(0, 2), ACT.Relu, bias=c("m_b1", e, e + 1)).then_inc(m_ra, 1)

    def stage7_dve(v):
        def reduce(i, l, s, p):
            v.wait_ge(m_mul, (i * 2 + l) * 8 + (4 * s + p + 1))
            b = 2 * p + s
            nc.vector.tensor_reduce(m_red[l][:, 64 * b:64 * b + 64], m_y[p % 2].rearrange("p (e c) -> p c e", e=8), X, ALU.add).then_inc(m_rd, 1)
        with v.Fori(0, NJ7 // 2) as i:
            for l in range(2):
                J = i * 2 + l
                k = [0]

                def step(ins, ordered=True):
                    k[0] += 1
                    ins.then_inc(m_step, 1)
                    if ordered:
                        v.wait_ge(m_step, J * STEPS7 + k[0])
                v.wait_ge(m_lg_r, J + 1)
                step(nc.vector.tensor_tensor(m_lg[l], T(0, 1)[:, 0:64], m_bg[:, :], ALU.add))
                step(nc.vector.memset(spare[:, 30:31], 0.0), ordered=False)
                for b in range(8):
                    step(nc.vector.max(m_m8[l][:, 8 * b:8 * b + 8], m_lg[l][:, 8 * b:8 * b + 8]), ordered=(b == 7))
                step(nc.vector.memset(spare[:, 31:32], 0.0), ordered=False)
                for b in range(8):
                    step(nc.vector.max_index(m_i8[l][:, 8 * b:8 * b + 8].bitcast(U32), m_m8[l][:, 8 * b:8 * b + 8],
                                             m_lg[l][:, 8 * b:8 * b + 8]), ordered=(b == 7))
                top = m_m8[l].rearrange("p (b k) -> p b k", k=8)
                nc.vector.tensor_tensor(m_d[l], top[:, :, 1], top[:, :, 0], ALU.subtract).then_inc(m_d_r, 1)
                step(nc.vector.tensor_copy(m_if[l].rearrange("p (b k) -> p b k", k=2),
                                           m_i8[l].bitcast(U32).rearrange("p (b k) -> p b k", k=8)[:, :, 0:2]))
                which = m_if[l].rearrange("p (b k) -> p b k", k=2)
                iota = c("iota").unsqueeze(1).to_broadcast([128, 8, 8])

                def e8(t):
                    return t.rearrange("p (b e) -> p b e", e=8)
                step(nc.vector.tensor_tensor(e8(m_e1[l]), iota, which[:, :, 0:1].to_broadcast([128, 8, 8]), ALU.is_equal), ordered=False)
                step(nc.vector.tensor_tensor(e8(m_e2[l]), iota, which[:, :, 1:2].to_broadcast([128, 8, 8]), ALU.is_equal))
                v.wait_ge(m_ex_r, J + 1)
                step(nc.vector.tensor_scalar(m_w1[l], m_d[l], 1.0, None, ALU.add))
                step(nc.vector.reciprocal(m_w1[l], m_w1[l]))
                step(nc.vector.tensor_tensor(m_w2[l], m_d[l], m_w1[l], ALU.mult), ordered=False)
                step(nc.vector.tensor_tensor(e8(m_c1[l]), e8(m_e1[l]), m_w1[l].unsqueeze(2).to_broadcast([128, 8, 8]), ALU.mult))
                step(nc.vector.tensor_tensor(e8(m_c2[l]), e8(m_e2[l]), m_w2[l].unsqueeze(2).to_broadcast([128, 8, 8]), ALU.mult))
                nc.vector.tensor_tensor(m_comb[l], m_c1[l], m_c2[l], ALU.add).then_inc(m_comb_r, 1)
                assert k[0] == 19 + 8, k[0]
                for s in range(2):
                    v.wait_ge(m_yp, J * 8 + (4 * s + 4))
                    for e in range(1, 8, 2):
                        v.wait_ge(m_hp, J * 16 + (8 * s + e + 1))
                        nc.vector.tensor_scalar(hid[s][:, 512 * e:512 * (e + 1)], T(0, 3), c("m_b1", e, e + 1), 0.0, ALU.add, ALU.max).then_inc(m_rv, 1)
                for s in range(2):
                    for p in range(4):
                        v.wait_ge(m_yp, J * 8 + (4 * s + p + 9))
                        v.wait_ge(m_rd, J * 8 + (4 * s + p + 1))
                        y = pt[1][:, 1024 * (p % 2):1024 * (p % 2) + 1024].rearrange("p (b x) -> p b x", b=2)[:, :, 0:384]
                        nc.vector.tensor_tensor(m_y[p % 2].rearrange("p (b j c) -> p b j c", b=2, j=4),
                                                y.rearrange("p b (j y) -> p b j y", y=96)[:, :, :, 0:64],
                                                c("m_b2").rearrange("p (b j c) -> p b j c", b=2, j=4), ALU.add).then_inc(m_add, 1)
                        if p:
                            reduce(i, l, s, p - 1)
                    reduce(i, l, s, 3)
                v.wait_ge(m_rd, J * 8 + 10)
                hp = h[:, bass.ds(i * 16 + 8 * l, 8), :]
                nc.vector.tensor_tensor(hp, hp, m_red[l].rearrange("p (b c) -> p b c", c=C), ALU.add).then_inc(m_h_r, 1)

    m_bg, m_bg_r = sb("m_bgs", [128, 64]), sem("7_gate_bias")

    with nc.Block() as block:
        @block.sync
        def _(sp):
            sp.dma_start(cst[:, :], consts).then_inc(loaded, 16)
            for i in range(JA // 2):
                if i >= 2:
                    sp.wait_ge(c1_max, 8 * (i - 1) + 2)
                for t in range(3):
                    sp.dma_start(xin[i % 2][32 * t:32 * (t + 1), :], xp[i, :, t:t + LEN]).then_inc(x_loaded[i % 2], 16)
            with sp.Fori(0, NJ7) as j:
                sp.wait_ge(m_h_r, j + 1)
                sp.dma_start(out[bass.ds(j * 8, 8), :, :].rearrange("b l c -> l b c"), h[:, bass.ds(j * 8, 8), :]).then_inc(stored, 16)
            sp.wait_ge(stored, 16 * NJ7)

        @block.gpsimd
        def _(pool):
            nc.gpsimd.memset(half_neg[:, :], -0.5).then_inc(bn_var, 1)
            nc.gpsimd.memset(one[:, :], 1.0).then_inc(one_set, 1)
            pool.wait_ge(loaded, 16)
            nc.gpsimd.tensor_scalar(bn_s[:, :], c("bn_v"), EPS, None, ALU.add).then_inc(bn_var, 1)
            pool.wait_ge(bn_var, 2)
            nc.gpsimd.tensor_tensor(bn_s[:, :], bn_s[:, :], half_neg[:, 0:1].to_broadcast([128, 83]), ALU.pow).then_inc(bn_rs, 1)
            norm_pool(pool, 0)
            pool.wait_ge(ln_rstd, 4)
            stage2_pool(pool)
            norm_pool(pool, 1)
            pool.wait_ge(ln_rstd, 8)
            pool.wait_ge(f_dve, SETUP3)
            stage3_pool(pool)
            norm_pool(pool, 2)
            norm_pool(pool, 3)
            pool.wait_ge(ln_rstd, 16)
            stage4_pool(pool)
            pool.wait_ge(f_h_r, NP + 2)
            gru_pool(pool)
            norm_pool(pool, 4)
            pool.wait_ge(ln_rstd, 20)
            stage7_pool(pool)

        @block.vector
        def _(v):
            for k in range(2):
                nc.vector.memset(h1[k], 0.0).then_inc(pads_zero, 1)
            nc.vector.memset(h3g, 0.0).then_inc(pads_zero, 1)
            for k, (credited, n) in enumerate(((c1_max, 2), (c2_max, 2), (h1_ready, 2), (h2_ready, 2), (b_h3, 2), (b_h, 1), (b_c3, 1), (a_h_r, 2), (f_h_r, 2),
                                               (r_t, 2), (r_xgf, 2), (r_xgr, 2), (g_yr, 2), (o_h, 2), (m_t_r, 2), (m_xT_r, 1),
                                               (m_ra, 1), (m_rv, 1), (m_add, 2), (m_yp, 8), (m_rd, 2))):
                nc.vector.memset(spare[:, k:k + 1], 0.0).then_inc(credited, n)
            v.wait_ge(loaded, 16)
            nc.vector.tensor_copy(eye16[:, :], eye).then_inc(eye_cast, 1)
            nc.vector.tensor_scalar(gbv[:, :], c("bv"), c("gamma"), None, ALU.mult).then_inc(gbv_ready, 1)
            v.wait_ge(bn_rs, 1)
            nc.vector.tensor_tensor(bn_s[:, :], bn_s[:, :], c("bn_g"), ALU.mult).then_inc(bn_scale, 1)
            nc.vector.tensor_tensor(bn_t[:, :], c("bn_b"), c("bn_m"), ALU.subtract).then_inc(bn_scale, 1)
            v.wait_ge(bn_scale, 2)
            nc.vector.tensor_tensor(bn_t[:, :], bn_t[:, :], bn_s[:, 80:83], ALU.mult).then_inc(bn_shift, 1)
            v.wait_ge(bn_shift, 1)
            nc.vector.tensor_tensor(bn_t[:, :], bn_t[:, :], c("bn_be"), ALU.add).then_inc(bn_shift, 1)
            nc.vector.tensor_tensor(w1s[:, :].rearrange("p (a c) -> p a c", c=16), c("w1").rearrange("p (a c) -> p a c", c=16),
                                    bn_s[:, 0:16].unsqueeze(1).to_broadcast([128, 16, 16]), ALU.mult)
            w2v = c("w2").rearrange("p (a c) -> p a c", c=64)
            nc.vector.tensor_tensor(w2v, w2v, bn_s[:, 16:80].unsqueeze(1).to_broadcast([128, 24, 64]), ALU.mult).then_inc(w_scaled, 1)
            nc.vector.tensor_copy(bias16[0][:, :], c("a_bias")).then_inc(a_split, 1)
            v.wait_ge(a_split, 1)
            nc.vector.tensor_tensor(bias_left, c("a_bias"), bias16[0][:, :], ALU.subtract).then_inc(a_split, 1)
            v.wait_ge(a_split, 2)
            nc.vector.tensor_copy(bias16[1][:, :], bias_left).then_inc(a_split, 1)
            v.wait_ge(a_split, 3)
            nc.vector.tensor_tensor(bias_left, bias_left, bias16[1][:, :], ALU.subtract).then_inc(a_split, 1)
            v.wait_ge(a_split, 4)
            nc.vector.tensor_copy(bias16[2][:, :], bias_left).then_inc(a_split, 1)
            nc.vector.tensor_scalar(a_bqs[:, :], c("a_bq"), HD ** -0.5, None, ALU.mult).then_inc(a_split, 1)
            v.wait_ge(a_pb_ps, 1)
            nc.vector.tensor_tensor(a_pb[:, :], T(1, 3)[:, 0:128], c("a_bp"), ALU.add).then_inc(a_pb_r, 1)
            stage1a_dve(v)
            stage1b_dve(v)
            v.wait_ge(b_h, IB + 1)
            for l in range(2):
                nc.vector.memset(a_v[l], 1.0).then_inc(a_ones, 1)
            norm_dve(v, 0, h)
            stage2_dve(v)
            v.wait_ge(a_h_r, NP + 2)
            norm_dve(v, 1, h)
            setup3_dve(v)
            stage3_dve(v)
            for u in range(2):
                nc.vector.memset(g_hs[u][:, :], 0.0).then_inc(g_setup, 1)
            nc.vector.memset(g_a[1][:, :], 0.0).then_inc(g_ar, 1)
            nc.vector.memset(g_b[1][:, :], 0.0).then_inc(g_br, 1)
            nc.vector.tensor_tensor(g_bias[:, :], c("g_bih"), c("g_bhh"), ALU.add).then_inc(g_setup, 1)
            nc.vector.tensor_tensor(m_bg[:, :], c("m_bg"), c("m_bias"), ALU.add).then_inc(m_bg_r, 1)
            v.wait_ge(g_setup, 3)
            nc.vector.tensor_scalar(g_nbz[:, :], g_bias[:, 1:2], -1.0, None, ALU.mult).then_inc(g_hr, 1)
            v.wait_ge(f_h_r, NP + 2)
            norm_dve(v, 2, h)
            stage4_norm_dve(v)
            stage4_dve(v)
            gru_dve(v)
            stage6_dve(v)
            v.wait_ge(o_h, NJ4 + 2)
            norm_dve(v, 4, h)
            v.wait_ge(m_bg_r, 1)
            stage7_dve(v)

        @block.tensor
        def _(pe):
            pe.wait_ge(loaded, 16)
            nc.tensor.matmul(T(1, 3)[:, 0:128], c("a_bv"), c("a_p"), start=True, stop=True).then_inc(a_pb_ps, 1)
            stage1a_pe(pe)
            pe.wait_ge(h2_ready, JA + 2)
            stage1b_pe(pe)
            pe.wait_ge(a_split, 6)
            pe.wait_ge(a_pb_r, 1)
            pe.wait_ge(b_h, IB + 1)
            stage2_pe(pe)
            setup3_pe(pe)
            pe.wait_ge(f_dve, SETUP3)
            stage3_pe(pe)
            pe.wait_ge(f_h_r, NP + 2)
            stage4_pe(pe)
            pe.wait_ge(r_xgf, NJ4 + 2)
            pe.wait_ge(r_xgr, NJ4 + 2)
            gru_pe(pe)
            pe.wait_ge(g_yr, L + 2)
            pe.wait_ge(g_hr, L + 1)
            stage6_pe(pe)
            pe.wait_ge(o_h, NJ4 + 2)
            stage7_pe(pe)

        @block.scalar
        def _(act):
            stage1a_act(act)
            stage1b_act(act)
            norm_act(act, 0)
            act.wait_ge(a_ones, 2)
            act.wait_ge(a_split, 6)
            stage2_act(act)
            norm_act(act, 1)
            act.wait_ge(f_dve, SETUP3)
            act.wait_ge(one_set, 1)
            stage3_act(act)
            norm_act(act, 2)
            norm_act(act, 3)
            act.wait_ge(f_h_r, NP + 2)
            stage4_act(act)
            act.wait_ge(g_setup, 3)
            act.wait_ge(g_hr, 1)
            gru_act(act)
            stage6_act(act)
            norm_act(act, 4)
            stage7_act(act)


def lay_out(w):
    big = np.zeros((128, WIDTH), np.float32)

    def put(name, a):
        a = np.asarray(a, np.float32)
        o, n = AT[name]
        assert a.shape[1] == n, (name, a.shape, n)
        big[:a.shape[0], o:o + n] = a

    def col(a):
        return np.asarray(a).reshape(-1, 1)

    def rows(a):
        return np.broadcast_to(np.asarray(a).reshape(1, -1), (128, np.asarray(a).size))

    def diag2(a):
        z = np.zeros((128, 2 * a.shape[1]), np.float32)
        z[:64, :a.shape[1]] = a
        z[64:, a.shape[1]:] = a
        return z

    put("eye", np.eye(128))
    w1 = np.zeros((3, 2, 16, 2, 8, 16), np.float32)
    for b in range(16):
        w1[:, :, b, b // 8, b % 8, :] = w["L0_tok_w1"].transpose(2, 1, 0)
    put("w1", w1.reshape(96, 256))
    w2 = np.zeros((4, 2, 16, 4, 3, 2, 64), np.float32)
    for p in range(4):
        for s in range(2):
            w2[p, s, :, p, :, s, :] = w["L0_tok_w2"].transpose(1, 2, 0)
    put("w2", w2.reshape(128, 12 * 128))
    w3 = np.zeros((2, 64, 2, 4, 128), np.float32)
    for s in range(2):
        w3[s, :, s] = w["L0_tok_w3"].transpose(1, 2, 0)
    put("w3", w3.reshape(128, 8 * 128))
    for n, part in (("v", "v"), ("g", "g")):
        a1, a2, a3 = (np.asarray(w[f"L0_tok_{part}{k}"]) for k in (1, 2, 3))
        put("bn_" + n, np.concatenate([rows(a1), rows(a2), col(np.tile(a1, 8)), col(np.tile(a2, 2)), col(a3)], 1))
    for n, part in (("b", "b"), ("m", "m"), ("be", "be")):
        a1, a2, a3 = (np.asarray(w[f"L0_tok_{part}{k}"]) for k in (1, 2, 3))
        put("bn_" + n, np.concatenate([col(np.tile(a1, 8)), col(np.tile(a2, 2)), col(a3)], 1))
    zq, zk = np.zeros((2, 64, 2, 2, 64), np.float32), np.zeros((2, 64, 2, 64), np.float32)
    zbq, zbk = np.zeros((2, 64, 2), np.float32), np.zeros((2, 64, 1), np.float32)
    for s in range(2):
        zq[s, :, s, s, :8] = w["L0_tok_wq"].T
        zk[s, :, s, :8] = w["L0_tok_wk"].T
        zbq[s, :8, s] = w["L0_tok_bq"]
        zbk[s, :8, 0] = w["L0_tok_bk"]
    put("wq", zq.reshape(128, 256))
    put("wk", zk.reshape(128, 128))
    put("bq", zbq.reshape(128, 2))
    put("bk", zbk.reshape(128, 1))
    put("wv", diag2(w["L0_tok_wv"].T))
    put("bv", col(np.tile(w["L0_tok_bv"], 2)))
    put("gamma", col(np.broadcast_to(w["L0_tok_gamma"], (128,))))
    lay_out_more(w, put, col, rows, diag2)
    return big


def lay_out_more(w, put, col, rows, diag2):
    qkv = w["L0_attn_qkv_weight"]
    qkv_b = w["L0_attn_qkv_bias"]
    for k, n in enumerate(("a_q", "a_k", "a_v")):
        put(n, diag2(qkv[64 * k:64 * (k + 1)].T))
    put("a_bq", col(np.tile(qkv_b[0:64], 2)))
    put("a_bk", col(np.tile(qkv_b[64:128], 2)))
    put("a_bv", np.broadcast_to(col(np.tile(qkv_b[128:192], 2)), (128, 128)))
    put("a_p", diag2(w["L0_attn_proj_weight"].T))
    put("a_bp", rows(np.tile(w["L0_attn_proj_bias"], 2)))
    mask = np.zeros((2, 8, 8, 2, 8), np.float32)
    for s in range(2):
        for k in range(8):
            mask[s, k, :, s, k] = 1.0
    put("a_mask", mask.reshape(128, 16))
    table = w["L0_attn_bias_table"].T
    put("a_bias", np.stack([table[:, q:q + 128][:, ::-1] for q in range(128)]).reshape(128, 1024))
    def headT(a):
        return a.reshape(64, 8, 64).transpose(2, 1, 0).reshape(64, 512)
    put("f_fxT", headT(w["L0_ffn_W_fx"]))
    put("f_xT", headT(w["L0_ffn_W_x"]))
    put("f_bfxT", w["L0_ffn_b_fx"].reshape(8, 64).T)
    put("f_bxT", w["L0_ffn_b_x"].reshape(8, 64).T)
    put("f_slice", w["L0_ffn_W_slice"])
    put("f_bslice", rows(w["L0_ffn_b_slice"]))
    for n in "qkv":
        put(f"f_w{n}T", w[f"L0_ffn_W_{n}"].T)
    put("f_out", w["L0_ffn_W_out"].reshape(8, 64, 64).transpose(1, 0, 2).reshape(64, 512))
    put("f_bout", col(np.tile(w["L0_ffn_b_out"], 2)))
    put("f_temp", rows(w["L0_ffn_temperature"]))
    a = "L1_attn_"
    put("g_lng", col(np.tile(w[a + "ln_g"], 2)))
    put("g_lnb", col(np.tile(w[a + "ln_b"], 2)))
    for n in ("ih", "hh"):
        z = np.zeros((2, 64, 3, 2, 64), np.float32)
        zb = np.zeros((2, 64, 3), np.float32)
        for d, way in enumerate(("fwd", "rev")):
            z[d, :, :, d] = w[f"{a}{way}_w_{n}"].reshape(3, 64, 64).transpose(2, 0, 1)
            zb[d] = w[f"{a}{way}_b_{n}"].reshape(3, 64).T
        put("g_" + n, z.reshape(128, 384))
        put("g_b" + n, zb.reshape(128, 3))
    put("g_gate", w[a + "gate_w"].T)
    put("g_bgate", col(w[a + "gate_b"]))
    put("g_diff", np.concatenate([np.eye(64), -np.eye(64)]))
    put("g_out", np.tile(w[a + "out_w"].T, (2, 1)))
    put("g_bout", rows(np.tile(w[a + "out_b"], 4)))
    put("m_g", diag2(w["L1_ffn_Wg"]))
    put("m_bg", rows(np.tile(w["L1_ffn_bg"], 8)))
    put("m_bias", rows(np.tile(w["L1_ffn_bias"], 8)))
    z = np.zeros((2, 64, 2, 8, 128), np.float32)
    for s in range(2):
        z[s, :, s] = w["L1_ffn_W1"].transpose(1, 0, 2)
    put("m_w1", z.reshape(128, 2048))
    put("m_b1", w["L1_ffn_b1"].T)
    put("m_w2", np.concatenate([w["L1_ffn_W2"].transpose(1, 0, 2).reshape(128, 512), np.zeros((128, 32), np.float32)], 1))
    put("m_b2", rows(w["L1_ffn_b2"]))
    put("iota", rows(np.arange(8)))


def kernel(**inputs):
    import concourse.bacc as bacc
    from concourse.bass_utils import run_bass_kernel_spmd

    w = {k: np.asarray(v) for k, v in inputs.items()}
    xp = np.zeros((4, 2, 16, LEN + 2), np.float32)
    xp[:, :, :, 1:LEN + 1] = w["x"].reshape(4, 16, 2, LEN).transpose(0, 2, 1, 3)
    arrays = {"x_dram": xp.reshape(4, 32, LEN + 2), "consts_dram": lay_out(w)}
    nc = bacc.Bacc("TRN2", target_bir_lowering=False, num_devices=1)
    args = [nc.dram_tensor(n, a.shape, F32, kind="ExternalInput").ap() for n, a in arrays.items()]
    out = nc.dram_tensor("out_dram", (B, L, C), F32, kind="ExternalOutput").ap()
    build(nc, *args, out)
    return run_bass_kernel_spmd(nc, [arrays], core_ids=[0]).results[0]["out_dram"]
```

```python
import numpy as np
import concourse.bass as bass
from concourse import mybir

F32 = mybir.dt.float32
BF16 = mybir.dt.bfloat16
U32 = mybir.dt.uint32
ALU = mybir.AluOpType
ACT = mybir.ActivationFunctionType
X = mybir.AxisListType.X
EPS = 1e-5
B, L, C = 64, 128, 64
NP = B // 2
HEADS, HD = 8, 8
G = 64
E = 8
LEN = 4096

PARTS = [
    ("eye", 128),
    ("w1", 2 * 128), ("w2", 12 * 128), ("w3", 8 * 128),
    ("bn_v", 83), ("bn_g", 83), ("bn_b", 3), ("bn_m", 3), ("bn_be", 3),
    ("wq", 256), ("wk", 128), ("bq", 2), ("bk", 1), ("wv", 128), ("bv", 1), ("gamma", 1),
    ("a_q", 128), ("a_k", 128), ("a_bq", 1), ("a_bk", 1), ("a_mask", 16), ("a_v", 128), ("a_bv", 128), ("a_p", 128), ("a_bp", 128),
    ("a_bias", HEADS * 128),
    ("f_fxT", 512), ("f_bfxT", 8), ("f_xT", 512), ("f_bxT", 8), ("f_slice", 64), ("f_bslice", 64),
    ("f_wqT", 64), ("f_wkT", 64), ("f_wvT", 64), ("f_out", 512), ("f_bout", 1), ("f_temp", 8),
    ("g_lng", 1), ("g_lnb", 1), ("g_ih", 3 * 128), ("g_hh", 3 * 128), ("g_bih", 3), ("g_bhh", 3),
    ("g_gate", 64), ("g_bgate", 1), ("g_diff", 64), ("g_out", 64), ("g_bout", 256),
    ("m_g", 16), ("m_bg", 64), ("m_bias", 64), ("m_w1", 16 * 128), ("m_b1", 8), ("m_w2", 512 + 32), ("m_b2", 512), ("iota", 8),
]
AT, WIDTH = {}, 0
for _n, _w in PARTS:
    AT[_n] = (WIDTH, _w)
    WIDTH += _w


def build(nc, xp, consts, out):
    def sb(name, shape, dt=F32):
        return nc.alloc_sbuf_tensor(name, shape, dt)

    def sem(name):
        return nc.alloc_semaphore(name)

    cst = sb("cst", [128, WIDTH])

    def c(name, a=0, b=None):
        o, w = AT[name]
        return cst[:, o + a:o + (w if b is None else b)]

    eye = c("eye")
    h = sb("h", [128, B, C])
    xc = sb("xc", [128, B, C])
    big1 = sb("big1", [128, 2 * LEN])
    big2 = sb("big2", [128, 2 * LEN])
    pt = [nc.alloc_psum_tensor(f"bank{l}", [128, 4 * 512], F32) for l in range(2)]

    def T(l, k, n=1):
        return pt[l][:, 512 * k:512 * (k + n)]

    xin = [big1[0:96, 0:LEN], big1[0:96, LEN:2 * LEN]]
    bn_s = sb("bn_s", [128, 83])
    bn_t = sb("bn_t", [128, 3])
    w1s = sb("w1s", [128, 2 * 128])
    half_neg = sb("half_neg", [128, 1])
    spare = sb("spare", [128, 32])
    one, one_set = sb("one", [128, 1]), sem("one_set")
    h1raw = [big2[:, 512 * k:512 * (k + 1)] for k in range(2)]
    h1 = [big2[:, 1024 + 520 * k:1024 + 520 * k + 514] for k in range(2)]
    h2raw = [big2[:, 2100 + 512 * k:2100 + 512 * (k + 1)] for k in range(2)]
    h2all = xc[:, :, :].rearrange("p (q s) c -> p q (s c)", s=2)

    loaded = sem("consts_loaded")
    x_loaded = [sem("x_loaded0"), sem("x_loaded1")]
    bn_var, bn_rs, bn_scale, bn_shift = sem("bn_var"), sem("bn_rsqrt"), sem("bn_scale"), sem("bn_shift")
    w_scaled, pads_zero = sem("conv_weights_scaled"), sem("pads_zero")
    c1_sum, c1_max, h1_ready = sem("conv1_sum"), sem("conv1_max"), sem("h1_ready")
    c2_sum, c2_max, h2_ready = sem("conv2_sum"), sem("conv2_max"), sem("h2_ready")
    stored = sem("out_stored")
    b_copy, b_proj, b_q, b_k, b_v = (sem("1b_" + n) for n in ("h2_copied", "projected", "q_ready", "k_ready", "v_ready"))
    b_energy, b_max, b_exp, b_rs, b_norm = (sem("1b_" + n) for n in ("energy", "max", "exp", "rsum", "normed"))
    b_pT, b_pTc, b_att, b_h3, b_c3, b_h = (sem("1b_" + n) for n in ("pT", "pT_copied", "attended", "h3_ready", "conv3", "h_written"))
    gbv_ready = sem("gamma_bv_ready")
    gbv = sb("gbv", [128, 1])

    def buf(name, cols, dt=F32):
        return [sb(f"{name}{l}", [128, cols], dt) for l in range(2)]

    def big2_lane(at, cols):
        return [big2[:, at + cols * l:at + cols * (l + 1)] for l in range(2)]
    h2p = big2_lane(3200, 128)
    bq_s, bk_s = big2_lane(5800, 256), big2_lane(3712, 128)
    bvT = big2_lane(3968, 128)
    bP, bPT = big2_lane(4224, 256), big2_lane(4736, 256)
    bmx, bsum, brs = big2_lane(5248, 2), big2_lane(5252, 2), big2_lane(5256, 2)
    h3g = big2[:, 5260:5260 + 4 * 130].rearrange("p (r n) -> p r n", r=4)

    JA = 8

    def stage1a_pe(pe):
        pe.wait_ge(w_scaled, 1)
        pe.wait_ge(pads_zero, 3)
        with pe.Fori(0, JA // 4) as ii:
            for w, g in ((0, 0), (0, 1), (1, 0), (1, 1)):
                j = ii * 4 + (2 * w + g)
                if g == 0:
                    pe.wait_ge(x_loaded[w], ii * 48 + 48)
                for q in range(4):
                    pe.wait_ge(c1_max, (j * 4) + (q + 1))
                    for k in range(2):
                        m = nc.tensor.matmul(T(0, 2 * (q % 2) + k), w1s[0:96, 128 * g:128 * (g + 1)],
                                             xin[w][:, (2 * q + k) * 512:(2 * q + k + 1) * 512], start=True, stop=True)
                    m.then_inc(c1_sum, 1)
                pe.wait_ge(h1_ready, j + 3)
                for p in range(4):
                    pe.wait_ge(c2_max, (j * 4) + (p + 1))
                    for t in range(3):
                        m = nc.tensor.matmul(T(1, p % 2), w2s(p, t), h1[g][:, t:t + 512], start=(t == 0), stop=(t == 2))
                    m.then_inc(c2_sum, 1)

    def w2s(p, t):
        return c("w2", (3 * p + t) * 128, (3 * p + t + 1) * 128)

    def stage1a_dve(v):
        with v.Fori(0, JA // 2) as i:
            for g in range(2):
                j = i * 2 + g
                v.wait_ge(h1_ready, j + 1)
                for q in range(4):
                    v.wait_ge(c1_sum, (j * 4) + (q + 1))
                    nc.vector.tensor_reduce(h1raw[g][:, 128 * q:128 * (q + 1)],
                                            T(0, 2 * (q % 2), 2).rearrange("p (n k) -> p n k", k=8), X, ALU.max).then_inc(c1_max, 1)
                v.wait_ge(h2_ready, j + 1)
                for p in range(4):
                    v.wait_ge(c2_sum, (j * 4) + (p + 1))
                    nc.vector.tensor_reduce(h2raw[g][:, 128 * p:128 * (p + 1)],
                                            T(1, p % 2).rearrange("p (n k) -> p n k", k=4), X, ALU.max).then_inc(c2_max, 1)

    def stage1a_act(act):
        act.wait_ge(bn_shift, 2)
        act.wait_ge(pads_zero, 3)
        with act.Fori(0, JA // 2) as i:
            for g in range(2):
                j = i * 2 + g
                act.wait_ge(c1_max, j * 4 + 6)
                nc.scalar.activation(h1[g][:, 1:513], h1raw[g], ACT.Relu, bias=bn_t[:, 0:1]).then_inc(h1_ready, 1)
                act.wait_ge(c2_max, j * 4 + 6)
                nc.scalar.activation(h2all[:, bass.ds(4 * j, 4), :], h2raw[g].rearrange("p (r n) -> p r n", r=4),
                                     ACT.Relu, bias=bn_t[:, 1:2]).then_inc(h2_ready, 1)

    IB = NP // 4

    def stage1b_pe(pe):
        with pe.Fori(0, IB) as i:
            for rr in (0, 2):
                R = [(r, r % 2, i * 4 + (r + 1)) for r in (rr, rr + 1)]
                for r, l, n in R:
                    pe.wait_ge(b_copy, n)
                    if r == 0:
                        pe.wait_ge(b_h, i + 1)
                    for s in range(2):
                        nc.tensor.matmul(T(l, 0)[:, 128 * s:128 * (s + 1)], c("wq", 128 * s, 128 * (s + 1)), h2p[l], start=True, stop=True)
                    nc.tensor.matmul(T(l, 2)[:, 256:384], c("wk"), h2p[l], start=True, stop=True)
                    nc.tensor.matmul(T(l, 1)[:, 0:128], h2p[l], c("wv"), start=True, stop=True).then_inc(b_proj, 1)
                for r, l, n in R:
                    pe.wait_ge(b_q, n)
                    pe.wait_ge(b_k, n)
                    for s in range(2):
                        m = nc.tensor.matmul(T(l, 2)[:, 128 * s:128 * (s + 1)], bq_s[l][:, 128 * s:128 * (s + 1)],
                                             bk_s[l], start=True, stop=True)
                    m.then_inc(b_energy, 1)
                for r, l, n in R:
                    pe.wait_ge(b_norm, n)
                    for s in range(2):
                        m = nc.tensor.transpose(T(l, 3)[:, 128 * s:128 * (s + 1)], bP[l][:, 128 * s:128 * (s + 1)], eye)
                    m.then_inc(b_pT, 1)
                for r, l, n in R:
                    pe.wait_ge(b_pTc, n)
                    pe.wait_ge(b_v, n)
                    for s in range(2):
                        m = nc.tensor.matmul(T(l, 1)[64 * s:64 * s + 64, 128:256], bvT[l][:, 64 * s:64 * s + 64],
                                             bPT[l][:, 128 * s:128 * (s + 1)], start=True, stop=True)
                    m.then_inc(b_att, 1)
            pe.wait_ge(b_h3, i * 4 + 6)
            for s in range(2):
                for t in range(4):
                    m = nc.tensor.matmul(T(0, 0)[:, 256 * s:256 * (s + 1)], c("w3", (4 * s + t) * 128, (4 * s + t + 1) * 128),
                                         h3g[:, :, t:t + 127:2], start=(t == 0), stop=(t == 3))
            m.then_inc(b_c3, 1)

    def stage1b_dve(v):
        v.wait_ge(h2_ready, JA + 2)
        with v.Fori(0, IB) as i:
            for rr in (0, 2):
                R = [(r, r % 2, i * 4 + (r + 1)) for r in (rr, rr + 1)]
                for r, l, n in R:
                    v.wait_ge(b_h3, i * 4 + (r + 1))
                    nc.vector.tensor_copy(h2p[l], h2all[:, i * 4 + r, :]).then_inc(b_copy, 1)
                for r, l, n in R:
                    v.wait_ge(b_proj, n)
                    nc.vector.tensor_scalar(bk_s[l], T(l, 2)[:, 256:384], c("bk"), None, ALU.add).then_inc(b_k, 1)
                for r, l, n in R:
                    v.wait_ge(b_energy, n)
                    nc.vector.tensor_reduce(bmx[l], T(l, 2)[:, 0:256].rearrange("p (s n) -> p s n", s=2), X, ALU.max,
                                            negate=True).then_inc(b_max, 1)
                for r, l, n in R:
                    v.wait_ge(b_exp, n)
                    nc.vector.reciprocal(brs[l], bsum[l]).then_inc(b_rs, 1)
                for r, l, n in R:
                    v.wait_ge(b_rs, n)
                    for s in range(2):
                        m = nc.vector.tensor_scalar(bP[l][:, 128 * s:128 * (s + 1)], bP[l][:, 128 * s:128 * (s + 1)],
                                                    brs[l][:, s:s + 1], c("gamma"), ALU.mult, ALU.mult)
                    m.then_inc(b_norm, 1)
                for r, l, n in R:
                    v.wait_ge(b_att, n)
                    if r == 0:
                        v.wait_ge(b_c3, i + 1)
                    nc.vector.scalar_tensor_tensor(h3g[:, r, 1:129], T(l, 1)[:, 128:256], gbv[:, 0:1], h2p[l],
                                                   ALU.add, ALU.add).then_inc(b_h3, 1)

    def stage1b_act(act):
        with act.Fori(0, IB) as i:
            for rr in (0, 2):
                R = [(r, r % 2, i * 4 + (r + 1)) for r in (rr, rr + 1)]
                for r, l, n in R:
                    act.wait_ge(b_proj, n)
                    for s in range(2):
                        m = nc.scalar.activation(bq_s[l][:, 128 * s:128 * (s + 1)], T(l, 0)[:, 128 * s:128 * (s + 1)],
                                                 ACT.Identity, bias=c("bq", s, s + 1))
                    m.then_inc(b_q, 1)
                    nc.scalar.copy(bvT[l], T(l, 1)[:, 0:128]).then_inc(b_v, 1)
                for r, l, n in R:
                    act.wait_ge(b_max, n)
                    nc.scalar.activation(bP[l][:, 0:128], T(l, 2)[:, 0:128], ACT.Exp, bias=bmx[l][:, 0:1], accum_out=bsum[l][:, 0:1])
                    nc.scalar.activation(bP[l][:, 128:256], T(l, 2)[:, 128:256], ACT.Exp, bias=bmx[l][:, 1:2],
                                         accum_out=bsum[l][:, 1:2]).then_inc(b_exp, 1)
                for r, l, n in R:
                    act.wait_ge(b_pT, n)
                    nc.scalar.copy(bPT[l], T(l, 3)[:, 0:256]).then_inc(b_pTc, 1)
            act.wait_ge(b_c3, i + 2)
            nc.scalar.activation(h[:, bass.ds(8 * i, 8), :].rearrange("p (r s) c -> p s r c", s=2),
                                 T(0, 0).rearrange("p (s r c) -> p s r c", s=2, r=4), ACT.Identity,
                                 bias=bn_t[:, 2:3], scale=bn_s[:, 82:83]).then_inc(b_h, 1)

    rowsum, rowsq, rstd = sb("rowsum", [128, B]), sb("rowsq", [128, B]), sb("rstd", [128, B])
    eps_var = sb("eps_var", [128, B])
    squares = [sb(f"squares{k}", [128, 16 * C]) for k in range(2)]
    ln_sum, ln_cent, ln_sq, ln_var, ln_eps, ln_rstd = (sem("ln_" + n) for n in ("sum", "centred", "squared", "var", "eps", "rstd"))

    def blk(t, b):
        return t[:, 16 * b:16 * (b + 1)]

    def norm_dve(v, k, src):
        def variance(b):
            v.wait_ge(ln_sq, 4 * k + b + 1)
            nc.vector.tensor_reduce(blk(rowsq, b), squares[b % 2][:, :].rearrange("p (b c) -> p b c", c=C), X, ALU.add).then_inc(ln_var, 1)
        for b in range(4):
            nc.vector.tensor_reduce(blk(rowsum, b), blk(src, b), X, ALU.add).then_inc(ln_sum, 1)
            if b:
                variance(b - 1)
            v.wait_ge(ln_sum, 4 * k + b + 1)
            nc.vector.scalar_tensor_tensor(blk(xc, b), blk(rowsum, b).unsqueeze(2).to_broadcast([128, 16, C]), -1.0 / C,
                                           blk(src, b), ALU.mult, ALU.add).then_inc(ln_cent, 1)
        variance(3)

    def norm_act(act, k):
        for b in range(4):
            act.wait_ge(ln_cent, 4 * k + b + 1)
            if b >= 2:
                act.wait_ge(ln_var, 4 * k + b - 1)
            nc.scalar.activation(squares[b % 2][:, :].rearrange("p (b c) -> p b c", c=C), blk(xc, b), ACT.Square).then_inc(ln_sq, 1)

    def norm_pool(pool, k):
        for b in range(4):
            pool.wait_ge(ln_var, 4 * k + b + 1)
            nc.gpsimd.tensor_scalar(blk(eps_var, b), blk(rowsq, b), 1.0 / C, EPS, ALU.mult, ALU.add).then_inc(ln_eps, 1)
            pool.wait_ge(ln_eps, 4 * k + b + 1)
            nc.gpsimd.tensor_tensor(blk(rstd, b), blk(eps_var, b), half_neg[:, 0:1].to_broadcast([128, 16]), ALU.pow).then_inc(ln_rstd, 1)

    def rstd_of(first, n):
        return rstd[:, bass.ds(first, n)].unsqueeze(2).to_broadcast([128, n, C])

    big = [big1, big2]

    def lane(at, cols):
        return [big[l][:, at:at + cols] for l in range(2)]
    xs, xT, a_q, a_k = lane(0, 128), lane(128, 128), lane(256, 128), lane(384, 128)
    a_v = lane(512, 2 * 168)
    a_kz = lane(1024, 2048)
    a_o, a_oT = lane(5136, 128), lane(5264, 128)

    def four(at, cols):
        return [big[k // 2][:, at + cols * (k % 2):at + cols * (k % 2 + 1)] for k in range(4)]
    a_P, a_PT, a_mx, a_rs = four(3072, 512), four(4096, 512), four(5120, 4), four(5128, 4)
    a_bqs, a_pb = sb("a_bqs", [128, 1]), sb("a_pb", [128, 128])
    (a_xs_r, a_t_r, a_xT_r, a_qkv_r, a_q_r, a_v_r, a_k_r, a_kz_r, a_sc_r, a_mx_r, a_e_r, a_pt_r, a_ptc_r, a_av_r, a_rs_r,
     a_o_r, a_ot_r, a_oT_r, a_pr_r, a_h_r) = (sem("2_" + n) for n in (
         "rows", "rowsT", "rowsT_copied", "qkv", "q_ready", "v_ready", "k_ready", "k_spread", "scores", "max", "exp", "pT", "pT_copied",
         "attended", "rsum", "heads_out", "outT", "outT_copied", "projected", "h_written"))
    a_setup, a_pb_ps, a_pb_r, a_ones = sem("2_constants"), sem("2_pb_product"), sem("2_pb"), sem("2_ones")

    N2 = NP // 2

    def bank(b):
        return T(b // 4, b % 4)

    def back(i, t, d):
        return (i, t - d) if t >= d else (i - 1, t - d + 8)

    def exists(i, d, last=N2 - 1):
        return not isinstance(i, int) or 0 <= i + d <= last

    def pipelined(engine, slot):
        for t in range(8):
            slot(0, t)
        with engine.Fori(1, N2 - 1) as i:
            for t in range(8):
                slot(i, t)
        for t in range(8):
            slot(N2 - 1, t)
        for t in range(5):
            slot(N2, t)

    def stage2_pool(pool):
        def rows(i, l, first=False):
            n = i * 2 + (l + 1)
            if not first:
                pool.wait_ge(a_t_r, n - 2)
            nc.gpsimd.tensor_tensor(xs[l].rearrange("p (b c) -> p b c", c=C), xc[:, bass.ds(i * 4 + 2 * l, 2), :],
                                    rstd_of(i * 4 + 2 * l, 2), ALU.mult).then_inc(a_xs_r, 1)

        def spread(i, l):
            for u in range(4):
                pool.wait_ge(a_k_r, i * 2 + (l + 1))
                nc.gpsimd.tensor_tensor(a_kz[l][:, 512 * u:512 * (u + 1)].rearrange("p (h k) -> p h k", h=4),
                                        a_k[l].unsqueeze(1).to_broadcast([128, 4, 128]),
                                        c("a_mask", 4 * u, 4 * u + 4).unsqueeze(2).to_broadcast([128, 4, 128]), ALU.mult).then_inc(a_kz_r, 1)

        rows(0, 0, True)
        rows(0, 1, True)
        spread(0, 0)
        with pool.Fori(1, N2) as i:
            rows(i, 0)
            spread(i - 1, 1)
            rows(i, 1)
            spread(i, 0)
        spread(N2 - 1, 1)

    def stage2_pe(pe):
        def rows(i, l):
            pe.wait_ge(a_xs_r, i * 2 + (l + 1))
            if l or exists(i, -1):
                pe.wait_ge(a_v_r, i * 2 + l)
            pe.wait_ge(a_oT_r, i * 2 + (l + 1))
            nc.tensor.transpose(bank(2)[:, 0:128], xs[l], eye).then_inc(a_t_r, 1)

        def qkv(i, l):
            pe.wait_ge(a_xT_r, i * 2 + (l + 1))
            pe.wait_ge(a_h_r, i * 2 + (l + 1))
            nc.tensor.matmul(bank(2)[:, 128:256], c("a_q"), xT[l], start=True, stop=True)
            nc.tensor.matmul(bank(3)[:, 0:128], c("a_k"), xT[l], start=True, stop=True)
            nc.tensor.matmul(bank(2)[:, 256:384], xT[l], c("a_v"), start=True, stop=True).then_inc(a_qkv_r, 1)

        def slot(i, t):
            l, u = t // 4, t % 4
            if exists(i, 0):
                if u == 0:
                    pe.wait_ge(a_q_r, i * 2 + (l + 1))
                pe.wait_ge(a_kz_r, i * 8 + (t + 1))
                if t >= 2 or exists(i, -1):
                    pe.wait_ge(a_mx_r, i * 8 + (t - 1))
                nc.tensor.matmul(bank(t % 2), a_q[l], a_kz[l][:, 512 * u:512 * (u + 1)], start=True, stop=True).then_inc(a_sc_r, 1)
            if u == 0 and exists(i, l, N2 - 1):
                rows(i + l, 1 - l)
            if u == 1 and exists(i, l, N2 - 1):
                qkv(i + l, 1 - l)
            ib, tb = back(i, t, 2)
            if exists(ib, 0):
                pe.wait_ge(a_e_r, ib * 8 + (tb + 1))
                if tb >= 4 or exists(ib, -1):
                    pe.wait_ge(a_o_r, ib * 8 + (tb - 3))
                for k in range(4):
                    m = nc.tensor.transpose(bank(4 + tb % 4)[:, 128 * k:128 * (k + 1)], a_P[tb % 4][:, 128 * k:128 * (k + 1)], eye)
                m.then_inc(a_pt_r, 1)
            if u == 3:
                ij, lj = (i, 0) if l else (i - 1, 1)
                if exists(ij, 0):
                    if exists(i, l):
                        pe.wait_ge(a_v_r, i * 2 + (l + 2))
                    pe.wait_ge(a_o_r, ij * 8 + (4 * lj + 4))
                    nc.tensor.transpose(bank(2)[:, 384:512], a_o[lj], eye).then_inc(a_ot_r, 1)
            if u == 0 and exists(i, -1, N2 - 1):
                pe.wait_ge(a_oT_r, i * 2 + (l + 2))
                pe.wait_ge(a_h_r, i * 2 + (l + 1))
                nc.tensor.matmul(bank(3)[:, 128:256], a_oT[l], c("a_p"), start=True, stop=False)
                nc.tensor.matmul(bank(3)[:, 128:256], eye, a_pb[:, :], start=False, stop=True).then_inc(a_pr_r, 1)
            ib, tb = back(i, t, 3)
            if exists(ib, 0):
                pe.wait_ge(a_ptc_r, ib * 8 + (tb + 1))
                if tb % 4 == 0:
                    pe.wait_ge(a_v_r, ib * 2 + (tb // 4 + 1))
                at = 168 * (tb % 4 // 2) + 36 * (tb % 2)
                for k in range(4):
                    m = nc.tensor.matmul(bank(4 + tb % 4)[:, 96 * k:96 * (k + 1)], a_PT[tb % 4][:, 128 * k:128 * (k + 1)],
                                         a_v[tb // 4][:, at + 9 * k:at + 9 * k + 96], start=True, stop=True)
                m.then_inc(a_av_r, 1)
        rows(0, 0)
        qkv(0, 0)
        pipelined(pe, slot)

    def stage2_act(act):
        def rows(i, l):
            act.wait_ge(a_t_r, i * 2 + (l + 1))
            nc.scalar.copy(xT[l], bank(2)[:, 0:128]).then_inc(a_xT_r, 1)

        def queries(i, l):
            act.wait_ge(a_qkv_r, i * 2 + (l + 1))
            nc.scalar.activation(a_q[l], bank(2)[:, 128:256], ACT.Identity, bias=a_bqs[:, 0:1], scale=-HD ** -0.5).then_inc(a_q_r, 1)

        def values(i, l):
            if not isinstance(i, int) or i:
                act.wait_ge(a_av_r, i * 8 + (4 * l - 4))
            for s in range(2):
                m = nc.scalar.copy(a_v[l][:, 168 * s:168 * s + 72].rearrange("p (h d) -> p h d", h=8)[:, :, 0:8],
                                   bank(2)[:, 256 + 64 * s:320 + 64 * s].rearrange("p (h d) -> p h d", h=8))
            m.then_inc(a_v_r, 1)

        def slot(i, t):
            l, u = t // 4, t % 4
            if u == 0 and exists(i, l, N2 - 1):
                rows(i + l, 1 - l)
            ib, tb = back(i, t, 1)
            if exists(ib, 0):
                act.wait_ge(a_mx_r, ib * 8 + (tb + 1))
                for k in range(4):
                    P = a_P[tb % 4][:, 128 * k:128 * (k + 1)]
                    m = nc.scalar.activation(P, P, ACT.Exp, bias=a_mx[tb % 4][:, k:k + 1], scale=-1.0)
                m.then_inc(a_e_r, 1)
            if u == 1 and exists(i, l, N2 - 1):
                queries(i + l, 1 - l)
            if u == 3 and exists(i, l, N2 - 1):
                values(i + l, 1 - l)
            if u == 3:
                ij, lj = (i, 0) if l else (i - 1, 1)
                if exists(ij, 0):
                    act.wait_ge(a_ot_r, ij * 2 + (lj + 1))
                    nc.scalar.copy(a_oT[lj], bank(2)[:, 384:512]).then_inc(a_oT_r, 1)
        rows(0, 0)
        queries(0, 0)
        values(0, 0)
        pipelined(act, slot)

    def stage2_dve(v):
        def keys(i, l):
            v.wait_ge(a_qkv_r, i * 2 + (l + 1))
            nc.vector.tensor_scalar(a_k[l], bank(3)[:, 0:128], c("a_bk"), None, ALU.add).then_inc(a_k_r, 1)

        def slot(i, t):
            l, u = t // 4, t % 4
            if exists(i, 0):
                v.wait_ge(a_sc_r, i * 8 + (t + 1))
                nc.vector.memset(spare[:, 24 + t:25 + t], 0.0)
                for k in range(4):
                    m = nc.vector.tensor_tensor_reduce(a_P[t % 4][:, 128 * k:128 * (k + 1)], bank(t % 2)[:, 128 * k:128 * (k + 1)],
                                                       c("a_bias", 512 * (u % 2) + 128 * k, 512 * (u % 2) + 128 * (k + 1)), 1.0, 3e38,
                                                       ALU.add, ALU.min, a_mx[t % 4][:, k:k + 1])
                m.then_inc(a_mx_r, 1)
            if u == 1 and exists(i, l, N2 - 1):
                keys(i + l, 1 - l)
            ib, tb = back(i, t, 2)
            if exists(ib, 0):
                v.wait_ge(a_pt_r, ib * 8 + (tb + 1))
                nc.vector.tensor_copy(a_PT[tb % 4], bank(4 + tb % 4)).then_inc(a_ptc_r, 1)
            if u == 0 and exists(i, -1, N2 - 1):
                v.wait_ge(a_pr_r, i * 2 + (l - 1))
                hp = h[:, bass.ds(i * 4 + (2 * l - 4), 2), :]
                nc.vector.tensor_tensor(hp, hp, bank(3)[:, 128:256].rearrange("p (b c) -> p b c", c=C), ALU.add).then_inc(a_h_r, 1)
            ib, tb = back(i, t, 3)
            if exists(ib, 0):
                v.wait_ge(a_av_r, ib * 8 + (tb + 1))
                res = bank(4 + tb % 4)[:, 0:384].rearrange("p (j y) -> p j y", y=96)
                nc.vector.reciprocal(a_rs[tb % 4], res[:, :, 8]).then_inc(a_rs_r, 1)
                v.wait_ge(a_rs_r, ib * 8 + (tb + 1))
                at = 32 * (tb % 4)
                nc.vector.tensor_tensor(a_o[tb // 4][:, at:at + 32].rearrange("p (j d) -> p j d", j=4), res[:, :, 0:8],
                                        a_rs[tb % 4].unsqueeze(2).to_broadcast([128, 4, 8]), ALU.mult).then_inc(a_o_r, 1)
        keys(0, 0)
        pipelined(v, slot)

    f_xs1 = lane(256, 192)
    f_w, f_wT = lane(512, 1024), lane(1536, 1024)
    f_tk, f_tT = lane(2560, 512), lane(3072, 512)
    f_uz = lane(3584, 1024)
    f_vw, f_oT = lane(4608, 512), lane(5120, 128)
    f_le, f_ebd, f_y = lane(5376, 512), lane(5888, 1024), lane(6912, 1024)
    f_mx, f_rs, f_nr, f_lmx, f_zr = lane(7936, 16), lane(7952, 16), lane(7968, 8), lane(7976, 8), lane(7984, 8)
    fA, fB, fX = sb("fA", [128, 1024]), sb("fB", [128, 1024]), sb("fX", [128, 1024])
    fFT, fXT, fM, fV = big1[0:64, 0:512], big1[0:64, 512:1024], big1[0:64, 1024:1536], big1[0:64, 1536:2048]
    fGT, fsum, fti = big1[0:64, 2048:2112], big1[0:64, 2112:2128], sb("f_tinv", [128, 8])
    f_dve, f_pe = sem("3_setup_vector"), sem("3_setup_products")
    (f_xs_r, f_xs1_r, f_t_r, f_xT_r, f_lg_r, f_mx_r, f_sub_r, f_exp_r, f_sum_r, f_rs_r, f_w_r, f_wt_r, f_s_r, f_wT_r, f_nr_r, f_nr2_r,
     f_tk_r, f_tt_r, f_tT_r, f_u_r, f_vw_r, f_uz0_r, f_uz1_r, f_vwc_r, f_l_r, f_lmx_r, f_ls_r, f_e_r, f_es_r, f_er_r, f_eb_r,
     f_y_r, f_ya_r, f_yv_r, f_o_r, f_oT_r, f_ot_r, f_h_r) = (sem("3_" + n) for n in (
         "rows", "rows_plus_1", "rowsT", "rowsT_copied", "logits", "max", "shifted", "exp", "sum", "rsum", "weights", "weightsT", "slices",
         "weightsT_copied", "norm", "rnorm", "tokens", "tokensT", "tokensT_copied", "keys_mixed", "values_mixed", "mixed_0", "mixed_1",
         "values_copied", "pairs", "pairs_max", "pairs_shifted", "pairs_exp", "pairs_sum", "pairs_rsum", "pairs_scaled",
         "attended", "attended_lo", "attended_hi", "outT", "outT_biased", "out", "h_written"))

    def heads(ap):
        return ap.rearrange("p (h c) -> p h c", h=8)

    def setup3_dve(v):
        k = [0]

        def step(ins):
            k[0] += 1
            ins.then_inc(f_dve, 1)
            v.wait_ge(f_dve, k[0])
        for t in (fA, fB, fX):
            step(nc.vector.memset(t[:, :], 0.0))
        step(nc.vector.tensor_scalar(fti[:, :], c("f_temp"), 0.1, 5.0, ALU.max, ALU.min))
        step(nc.vector.reciprocal(fti[:, :], fti[:, :]))
        for raw, b, to, at in (("f_fxT", "f_bfxT", fFT, 0), ("f_xT", "f_bxT", fXT, 8)):
            part = fsum[:, at:at + 8]
            step(nc.vector.tensor_reduce(part, heads(c(raw)[0:64]), X, ALU.add))
            step(nc.vector.tensor_tensor(part, c(b)[0:64], part, ALU.subtract))
            step(nc.vector.scalar_tensor_tensor(heads(to), part.unsqueeze(2).to_broadcast([64, 8, 64]), 1.0 / C, heads(c(raw)[0:64]),
                                                ALU.mult, ALU.add))
        v.wait_ge(f_pe, 1)
        step(nc.vector.tensor_copy(fGT, T(0, 0)[0:64, 0:64]))
        step(nc.vector.tensor_copy(fV, T(0, 1)[0:64, :]))
        bs = heads(fX[0:64, 0:512])
        step(nc.vector.scalar_tensor_tensor(bs, c("f_bslice")[0:64].unsqueeze(1).to_broadcast([64, 8, 64]), 1.0 / C,
                                            heads(T(0, 2)[0:64, :]), ALU.mult, ALU.add))
        step(nc.vector.tensor_tensor(bs, bs, fti[0:64, :].unsqueeze(2).to_broadcast([64, 8, 64]), ALU.mult))
        bs = heads(fX[64:128, 512:1024])
        step(nc.vector.scalar_tensor_tensor(bs, c("f_bslice")[64:128].unsqueeze(1).to_broadcast([64, 8, 64]), 1.0 / C,
                                            heads(T(0, 3)[64:128, :]), ALU.mult, ALU.add))
        step(nc.vector.tensor_tensor(bs, bs, fti[64:128, :].unsqueeze(2).to_broadcast([64, 8, 64]), ALU.mult))
        v.wait_ge(f_pe, 2)
        step(nc.vector.tensor_copy(fM, T(1, 0)[0:64, :]))
        v.wait_ge(f_pe, 3)
        for s in range(2):
            r = slice(64 * s, 64 * s + 64)
            step(nc.vector.tensor_scalar(fA[r, 512 * s:512 * (s + 1)], T(0, 0)[r, :], 64.0 ** -0.5, None, ALU.mult))
            step(nc.vector.tensor_copy(fB[r, 512 * s:512 * (s + 1)], T(0, 1)[r, :]))
        for l in range(2):
            step(nc.vector.memset(f_xs1[l], 1.0))
            step(nc.vector.memset(f_uz[l], 0.0))
            step(nc.vector.memset(f_ebd[l], 0.0))
    SETUP3 = 28

    def setup3_pe(pe):
        pe.wait_ge(f_dve, 11)
        nc.tensor.matmul(T(0, 0)[0:64, 0:64], c("f_wkT")[0:64], c("f_wqT")[0:64], start=True, stop=True)
        nc.tensor.matmul(T(0, 1)[0:64, :], c("f_wvT")[0:64], c("f_out")[0:64], start=True, stop=True)
        for k in range(8):
            nc.tensor.matmul(T(0, 2)[0:64, 64 * k:64 * k + 64], fXT[:, 64 * k:64 * k + 64], c("f_slice")[0:64], start=True, stop=True)
        for k in range(8):
            m = nc.tensor.matmul(T(0, 3)[64:128, 64 * k:64 * k + 64], fXT[:, 64 * k:64 * k + 64], c("f_slice")[0:64], start=True, stop=True)
        m.then_inc(f_pe, 1)
        pe.wait_ge(f_dve, 17)
        nc.tensor.matmul(T(1, 0)[0:64, :], fGT, fFT, start=True, stop=True).then_inc(f_pe, 1)
        pe.wait_ge(f_dve, 18)
        for r in (slice(0, 64), slice(64, 128)):
            for k in range(8):
                q = slice(64 * k, 64 * k + 64)
                nc.tensor.matmul(T(0, 0)[r, q], fFT[:, q], fM[:, q], start=True, stop=True)
                m = nc.tensor.matmul(T(0, 1)[r, q], fFT[:, q], fV[:, q], start=True, stop=True)
        m.then_inc(f_pe, 1)

    def job(i, l, d):
        i2, l2 = i + (l + d) // 2, (l + d) % 2
        return i2, l2, i2 * 2 + (l2 + 1)

    def pipelined3(engine, slot):
        for l in range(2):
            slot(0, l)
        with engine.Fori(1, N2 - 1) as i:
            for l in range(2):
                slot(i, l)
        for l in range(2):
            slot(N2 - 1, l)
        for l in range(2):
            slot(N2, l)

    def regions():
        return T(0, 2, 2).rearrange("p (b x) -> p b x", b=2)[:, :, 0:384].rearrange("p b (j y) -> p b j y", y=96)

    def stage3_pool(pool):
        def rows(i, l, n, first=False):
            if not first:
                pool.wait_ge(f_t_r, n - 2)
            nc.gpsimd.tensor_tensor(xs[l].rearrange("p (b c) -> p b c", c=C), xc[:, bass.ds(i * 4 + 2 * l, 2), :],
                                    rstd_of(i * 4 + 2 * l, 2), ALU.mult).then_inc(f_xs_r, 1)

        def rows_plus_1(i, l, n):
            pool.wait_ge(f_xs_r, n)
            pool.wait_ge(f_s_r, n)
            nc.gpsimd.tensor_tensor(f_xs1[l].rearrange("p (s c) -> p s c", s=2)[:, :, 0:64], xs[l].rearrange("p (s c) -> p s c", s=2),
                                    one[:, 0:1].unsqueeze(1).to_broadcast([128, 2, 64]), ALU.add).then_inc(f_xs1_r, 1)

        def weights(i, l, n):
            pool.wait_ge(f_rs_r, n)
            w = f_w[l].rearrange("p (h g) -> p h g", g=64)
            nc.gpsimd.tensor_tensor(w, w, f_rs[l].unsqueeze(2).to_broadcast([128, 16, 64]), ALU.mult).then_inc(f_w_r, 1)

        def slot(i, l):
            a, b = job(i, l, 1), job(i, l, 2)
            if exists(b[0], 0):
                pool.wait_ge(f_xs1_r, b[2] - 2)
                rows(*b)
            if exists(a[0], 0):
                rows_plus_1(*a)
                weights(*a)
        for l in range(2):
            rows(0, l, l + 1, first=True)
        rows_plus_1(0, 0, 1)
        weights(0, 0, 1)
        pipelined3(pool, slot)

    def stage3_pe(pe):
        def rows(i, l, n):
            if not isinstance(n, int) or n > 1:
                pe.wait_ge(f_sub_r, n - 1)
            pe.wait_ge(f_xs_r, n)
            nc.tensor.transpose(T(0, 0)[:, 0:128], xs[l], eye).then_inc(f_t_r, 1)

        def logits(i, l, n):
            pe.wait_ge(f_xT_r, n)
            for s in range(2):
                m = nc.tensor.matmul(T(0, s), xT[l], fX[:, 512 * s:512 * (s + 1)], start=True, stop=True)
            m.then_inc(f_lg_r, 1)

        def slices(i, l, n):
            pe.wait_ge(f_w_r, n)
            pe.wait_ge(f_xs1_r, n)
            if l or exists(i, -1):
                pe.wait_ge(f_vwc_r, n - 1)
            for k in range(8):
                m = nc.tensor.matmul(regions()[:, k // 4, k % 4, :], f_w[l][:, 128 * k:128 * k + 128],
                                     f_xs1[l][:, 96 * (k // 4):96 * (k // 4) + 96], start=True, stop=True)
            m.then_inc(f_s_r, 1)
            for k in range(8):
                m = nc.tensor.transpose(T(1, k // 4)[:, 128 * (k % 4):128 * (k % 4) + 128], f_w[l][:, 128 * k:128 * k + 128], eye)
            m.then_inc(f_wt_r, 1)

        def tokensT(i, l, n):
            pe.wait_ge(f_tk_r, n)
            pe.wait_ge(f_h_r, n)
            for k in range(4):
                m = nc.tensor.transpose(T(1, 2)[:, 128 * k:128 * k + 128], f_tk[l][:, 128 * k:128 * k + 128], eye)
            m.then_inc(f_tt_r, 1)

        def mixed(i, l, n):
            pe.wait_ge(f_tT_r, n)
            for s in range(2):
                for k in range(8):
                    m = nc.tensor.matmul(T(0, 2)[64 * s:64 * s + 64, 64 * k:64 * k + 64], fA[:, 512 * s + 64 * k:512 * s + 64 * k + 64],
                                         f_tT[l][:, 64 * k:64 * k + 64], start=True, stop=True)
            m.then_inc(f_u_r, 1)
            for s in range(2):
                for k in range(8):
                    o = 64 * (4 * s + k // 2)
                    m = nc.tensor.matmul(T(0, 3)[64 * (k % 2):64 * (k % 2) + 64, o:o + 64], f_tT[l][:, 64 * k:64 * k + 64],
                                         fB[:, 512 * s + 64 * k:512 * s + 64 * k + 64], start=True, stop=True)
            m.then_inc(f_vw_r, 1)

        def pairs(i, l, n):
            pe.wait_ge(f_uz0_r, n)
            pe.wait_ge(f_uz1_r, n)
            for s in range(2):
                for k in range(8):
                    o = 64 * (4 * s + k // 2)
                    m = nc.tensor.matmul(T(1, 3)[64 * (k % 2):64 * (k % 2) + 64, o:o + 64],
                                         f_uz[l][:, 512 * s + 64 * k:512 * s + 64 * k + 64], f_tT[l][:, 64 * k:64 * k + 64], start=True, stop=True)
            m.then_inc(f_l_r, 1)

        def attended(i, l, n):
            pe.wait_ge(f_eb_r, n)
            for k in range(8):
                m = nc.tensor.matmul(T(1, k // 4)[:, 128 * (k % 4):128 * (k % 4) + 128], f_ebd[l][:, 128 * k:128 * k + 128],
                                     f_wT[l][:, 128 * k:128 * k + 128], start=True, stop=True)
            m.then_inc(f_y_r, 1)

        def outT(i, l, n):
            pe.wait_ge(f_ya_r, n)
            pe.wait_ge(f_yv_r, n)
            for s in range(2):
                for j in range(4):
                    k = 4 * s + j
                    m = nc.tensor.matmul(T(1, 2)[64 * s:64 * s + 64, 0:128], f_vw[l][:, 64 * k:64 * k + 64],
                                         f_y[l][:, 128 * k:128 * k + 128], start=(j == 0), stop=(j == 3))
            m.then_inc(f_o_r, 1)

        def out(i, l, n):
            pe.wait_ge(f_oT_r, n)
            nc.tensor.transpose(T(1, 2)[:, 128:256], f_oT[l], eye).then_inc(f_ot_r, 1)

        def slot(i, l):
            z, a, b, y = job(i, l, 0), job(i, l, 1), job(i, l, 2), job(i, l, -1)
            if exists(z[0], 0):
                slices(*z)
            if exists(a[0], 0):
                logits(*a)
            if exists(z[0], 0):
                tokensT(*z)
                pe.wait_ge(f_wT_r, z[2])
            if exists(y[0], 0):
                attended(*y)
            if exists(z[0], 0):
                mixed(*z)
            if exists(y[0], 0):
                outT(*y)
            if exists(z[0], 0):
                pairs(*z)
            if exists(y[0], 0):
                out(*y)
            if exists(b[0], 0):
                rows(*b)
        rows(0, 0, 1)
        logits(0, 0, 1)
        rows(0, 1, 2)
        pipelined3(pe, slot)

    def stage3_act(act):
        def rowsT(i, l, n):
            act.wait_ge(f_t_r, n)
            nc.scalar.activation(xT[l], T(0, 0)[:, 0:128], ACT.Identity, bias=one[:, 0:1]).then_inc(f_xT_r, 1)

        def exp(i, l, n):
            act.wait_ge(f_sub_r, n)
            nc.scalar.activation(f_w[l], f_w[l], ACT.Exp).then_inc(f_exp_r, 1)

        def slot(i, l):
            (zi, zl, z), a, b, (yi, yl, y) = job(i, l, 0), job(i, l, 1), job(i, l, 2), job(i, l, -1)
            if exists(yi, 0):
                act.wait_ge(f_ls_r, y)
                nc.scalar.activation(f_le[yl], f_le[yl], ACT.Exp).then_inc(f_e_r, 1)
            if exists(zi, 0):
                act.wait_ge(f_wt_r, z)
                nc.scalar.copy(f_wT[zl], T(1, 0, 2)).then_inc(f_wT_r, 1)
                act.wait_ge(f_tt_r, z)
                nc.scalar.copy(f_tT[zl], T(1, 2)).then_inc(f_tT_r, 1)
            if exists(yi, 0):
                act.wait_ge(f_y_r, y)
                nc.scalar.copy(f_y[yl][:, 0:512], T(1, 0)).then_inc(f_ya_r, 1)
            if exists(a[0], 0):
                exp(*a)
            if exists(zi, 0):
                act.wait_ge(f_u_r, z)
                nc.scalar.copy(f_uz[zl][0:64, 0:512], T(0, 2)[0:64, :]).then_inc(f_uz0_r, 1)
                act.wait_ge(f_vw_r, z)
                nc.scalar.copy(f_vw[zl], T(0, 3)).then_inc(f_vwc_r, 1)
            if exists(yi, 0):
                act.wait_ge(f_o_r, y)
                nc.scalar.activation(f_oT[yl], T(1, 2)[:, 0:128], ACT.Identity, bias=c("f_bout")).then_inc(f_oT_r, 1)
            if exists(b[0], 0):
                rowsT(*b)
        rowsT(0, 0, 1)
        exp(0, 0, 1)
        rowsT(0, 1, 2)
        pipelined3(act, slot)

    def stage3_dve(v):
        def shifted(i, l, n):
            v.wait_ge(f_lg_r, n)
            lg = T(0, 0, 2).rearrange("p (h g) -> p h g", g=64)
            nc.vector.tensor_reduce(f_mx[l], lg, X, ALU.max).then_inc(f_mx_r, 1)
            v.wait_ge(f_mx_r, n)
            nc.vector.tensor_tensor(f_w[l].rearrange("p (h g) -> p h g", g=64), lg, f_mx[l].unsqueeze(2).to_broadcast([128, 16, 64]),
                                    ALU.subtract).then_inc(f_sub_r, 1)

        def rsum(i, l, n):
            v.wait_ge(f_exp_r, n)
            nc.vector.tensor_reduce(f_rs[l], f_w[l].rearrange("p (h g) -> p h g", g=64), X, ALU.add).then_inc(f_sum_r, 1)
            v.wait_ge(f_sum_r, n)
            nc.vector.reciprocal(f_rs[l], f_rs[l]).then_inc(f_rs_r, 1)

        def tokens(i, l, n):
            v.wait_ge(f_s_r, n + 2)
            nr = f_nr[l].rearrange("p (s j) -> p s j", s=2)
            nc.vector.tensor_scalar(nr, regions()[:, :, :, 64], 1e-5, None, ALU.add).then_inc(f_nr_r, 1)
            v.wait_ge(f_nr_r, n)
            nc.vector.reciprocal(f_nr[l], f_nr[l]).then_inc(f_nr2_r, 1)
            v.wait_ge(f_nr2_r, n)
            nc.vector.tensor_tensor(f_tk[l].rearrange("p (j s c) -> p s j c", j=4, s=2), regions()[:, :, :, 0:64],
                                    nr.unsqueeze(3).to_broadcast([128, 2, 4, 64]), ALU.mult).then_inc(f_tk_r, 1)

        def pairs_shifted(i, l, n):
            v.wait_ge(f_l_r, n)
            pairs = T(1, 3).rearrange("p (k c) -> p k c", c=64)
            nc.vector.tensor_reduce(f_lmx[l], pairs, X, ALU.max).then_inc(f_lmx_r, 1)
            v.wait_ge(f_lmx_r, n)
            nc.vector.tensor_tensor(f_le[l].rearrange("p (k c) -> p k c", c=64), pairs,
                                    f_lmx[l].unsqueeze(2).to_broadcast([128, 8, 64]), ALU.subtract).then_inc(f_ls_r, 1)

        def pairs_scaled(i, l, n):
            e = f_le[l].rearrange("p (k c) -> p k c", c=64)
            v.wait_ge(f_e_r, n)
            nc.vector.tensor_reduce(f_zr[l], e, X, ALU.add).then_inc(f_es_r, 1)
            v.wait_ge(f_es_r, n)
            nc.vector.reciprocal(f_zr[l], f_zr[l]).then_inc(f_er_r, 1)
            v.wait_ge(f_er_r, n)
            for r in (slice(0, 64), slice(64, 128)):
                m = nc.vector.tensor_tensor(f_ebd[l][r, :].rearrange("p (k y) -> p k y", y=128)[:, :, r], e[r],
                                            f_zr[l][r, :].unsqueeze(2).to_broadcast([64, 8, 64]), ALU.mult)
            m.then_inc(f_eb_r, 1)

        def slot(i, l):
            z, a, y, (xi, xl, x) = job(i, l, 0), job(i, l, 1), job(i, l, -1), job(i, l, -2)
            if exists(y[0], 0):
                pairs_shifted(*y)
            if exists(xi, 0):
                v.wait_ge(f_ot_r, x)
                hp = h[:, bass.ds(xi * 4 + 2 * xl, 2), :]
                nc.vector.tensor_tensor(hp, hp, T(1, 2)[:, 128:256].rearrange("p (b c) -> p b c", c=C), ALU.add).then_inc(f_h_r, 1)
            if exists(z[0], 0):
                tokens(*z)
            if exists(y[0], 0):
                pairs_scaled(*y)
            if exists(a[0], 0):
                shifted(*a)
            if exists(y[0], 0):
                v.wait_ge(f_y_r, y[2])
                nc.vector.tensor_copy(f_y[y[1]][:, 512:1024], T(1, 1)).then_inc(f_yv_r, 1)
            if exists(z[0], 0):
                v.wait_ge(f_u_r, z[2])
                nc.vector.tensor_copy(f_uz[z[1]][64:128, 512:1024], T(0, 2)[64:128, :]).then_inc(f_uz1_r, 1)
            if exists(a[0], 0):
                rsum(*a)
        shifted(0, 0, 1)
        rsum(0, 0, 1)
        pipelined3(v, slot)

    xg = big1[:, :].rearrange("p (t b) -> p t b", b=B)
    ys = big2[:, :].rearrange("p (t b) -> p t b", b=B)
    r_x1, r_res = sem("4_normed"), sem("4_residual")
    r_dup, r_t, r_xgf, r_xgr = sem("4_rows"), sem("4_rowsT"), sem("4_forward"), sem("4_reverse")
    dup = [squares[k][:, 0:512].rearrange("p (b d c) -> p b d c", b=4, d=2) for k in range(2)]
    NJ4 = B // 4

    def stage4_norm_dve(v):
        for b in range(4):
            v.wait_ge(ln_rstd, 8 + b + 1)
            nc.vector.tensor_tensor(blk(xc, b), blk(xc, b), blk(rstd, b).unsqueeze(2).to_broadcast([128, 16, C]), ALU.mult).then_inc(r_x1, 1)
            v.wait_ge(r_x1, b + 1)
            nc.vector.tensor_tensor(blk(h, b), blk(h, b), blk(xc, b), ALU.add).then_inc(r_res, 1)
        v.wait_ge(r_res, 4)
        norm_dve(v, 3, xc)

    def stage4_pool(pool):
        with pool.Fori(0, NJ4 // 2) as i:
            for l in range(2):
                n = i * 2 + (l + 1)
                pool.wait_ge(r_t, n)
                nc.gpsimd.tensor_tensor(dup[l], xc[:, bass.ds(i * 8 + 4 * l, 4), :].unsqueeze(2).to_broadcast([128, 4, 2, C]),
                                        rstd[:, bass.ds(i * 8 + 4 * l, 4)].unsqueeze(2).unsqueeze(3).to_broadcast([128, 4, 2, C]),
                                        ALU.mult).then_inc(r_dup, 1)

    def stage4_pe(pe):
        with pe.Fori(0, NJ4 // 2) as i:
            for l in range(2):
                n = i * 2 + (l + 1)
                pe.wait_ge(r_dup, n)
                pe.wait_ge(r_xgf, n)
                pe.wait_ge(r_xgr, n)
                for b in range(4):
                    m = nc.tensor.transpose(T(l, 0)[:, 128 * b:128 * b + 128], squares[l][:, 128 * b:128 * b + 128], eye)
                m.then_inc(r_t, 1)

    def stage4_act(act):
        with act.Fori(0, NJ4 // 2) as i:
            for l in range(2):
                act.wait_ge(r_t, i * 2 + (l + 3))
                nc.scalar.activation(xg[0:64, :, bass.ds(i * 8 + 4 * l, 4)].rearrange("p t b -> p b t"),
                                     T(l, 0)[0:64, :].rearrange("p (b t) -> p b t", b=4), ACT.Identity,
                                     bias=c("g_lnb")[0:64], scale=c("g_lng")[0:64]).then_inc(r_xgf, 1)

    def stage4_dve(v):
        with v.Fori(0, NJ4 // 2) as i:
            for l in range(2):
                v.wait_ge(r_t, i * 2 + (l + 3))
                nc.vector.tensor_scalar(xg[64:128, :, bass.ds(i * 8 + 4 * l, 4)].rearrange("p t b -> p b t"),
                                        T(l, 0)[64:128, :].rearrange("p (b t) -> p b t", b=4)[:, :, ::-1],
                                        c("g_lng")[64:128], c("g_lnb")[64:128], ALU.mult, ALU.add).then_inc(r_xgr, 1)

    UN = 16
    g_bias, g_nbz = sb("g_bias", [128, 3]), sb("g_nbz", [128, 1])
    g_set, g_r, g_z, g_omz, g_t, g_t2, g_n, g_a, g_b, g_hs = (
        [sb(f"g_{n}{u}", [128, B]) for u in range(2)] for n in ("set", "r", "z", "omz", "t", "t2", "n", "a", "b", "h"))
    (g_setup, g_rp, g_hp, g_zp, g_rr, g_zr, g_tr, g_t2r, g_nr, g_ar, g_br, g_hr, g_yr) = (sem("5_" + n) for n in (
        "setup", "r_sum", "hn_sum", "z_sum", "r", "z", "gated", "n_sum", "n", "a", "b", "h", "stored"))

    GS = 8

    def gru_x(gate, half, group, first):
        w = 64 * GS // 2
        nc.tensor.matmul(T(group, gate)[:, w * half:w * (half + 1)], c("g_ih", 128 * gate, 128 * gate + 128),
                         big1[:, bass.ds(first * B + w * half, w)], start=(half == 0), stop=True, skip_group_check=True)

    def gru_products(to, gate, state, start):
        for d in range(2):
            m = nc.tensor.matmul(to[64 * d:64 * d + 64, :], c("g_hh", 128 * gate + 64 * d, 128 * gate + 64 * d + 64), state[:, :],
                                 start=start, stop=True, skip_group_check=True)
        return m

    def gru_pe(pe):
        def steps(i, last):
            for st in range(UN):
                u, group, col = st % 2, st // GS, B * (st % GS)
                n = i * UN + st
                R, Z = (T(group, k)[:, col:col + B] for k in range(2))
                HN = T(u, 3)[:, 0:B]
                pe.wait_ge(g_br, n + 1)
                gru_products(R, 0, g_b[1 - u], False)
                gru_products(HN, 2, g_b[1 - u], True)
                pe.wait_ge(g_ar, n + 1)
                gru_products(R, 0, g_a[1 - u], False).then_inc(g_rp, 1)
                gru_products(HN, 2, g_a[1 - u], False).then_inc(g_hp, 1)
                pe.wait_ge(g_hr, n + 1)
                gru_products(Z, 1, g_hs[1 - u], False).then_inc(g_zp, 1)
                if st % GS < 6 and not (last and group == 1):
                    gru_x(st % GS // 2, st % 2, 1 - group, i * UN + GS * (group + 1))
        for gate in range(3):
            for half in range(2):
                gru_x(gate, half, 0, 0)
        with pe.Fori(0, L // UN - 1) as i:
            steps(i, False)
        steps(L // UN - 1, True)

    def gru_act(act):
        with act.Fori(0, L // UN) as i:
            for st in range(UN):
                u, n = st % 2, i * UN + (st + 1)
                group, col = st // GS, B * (st % GS)
                act.wait_ge(g_rp, n)
                nc.scalar.activation(g_r[u][:, :], T(group, 0)[:, col:col + B], ACT.Sigmoid, bias=g_bias[:, 0:1]).then_inc(g_rr, 1)
                act.wait_ge(g_zp, n)
                nc.scalar.activation(g_z[u][:, :], T(group, 1)[:, col:col + B], ACT.Sigmoid, bias=g_bias[:, 1:2])
                nc.scalar.activation(g_omz[u][:, :], T(group, 1)[:, col:col + B], ACT.Sigmoid, bias=g_nbz[:, 0:1], scale=-1.0).then_inc(g_zr, 1)
                act.wait_ge(g_t2r, n)
                nc.scalar.activation(g_n[u][:, :], g_t2[u][:, :], ACT.Tanh, bias=c("g_bih", 2, 3)).then_inc(g_nr, 1)

    def gru_dve(v):
        with v.Fori(0, L // UN) as i:
            for st in range(UN):
                u, n = st % 2, i * UN + (st + 1)
                group, col = st // GS, B * (st % GS)
                v.wait_ge(g_hp, n)
                v.wait_ge(g_rr, n)
                nc.vector.scalar_tensor_tensor(g_t[u][:, :], T(u, 3)[:, 0:B], c("g_bhh", 2, 3), g_r[u][:, :], ALU.add, ALU.mult).then_inc(g_tr, 1)
                v.wait_ge(g_tr, n)
                nc.vector.tensor_tensor(g_t2[u][:, :], T(group, 2)[:, col:col + B], g_t[u][:, :], ALU.add).then_inc(g_t2r, 1)
                v.wait_ge(g_zr, n)
                v.wait_ge(g_hr, n)
                v.wait_ge(g_yr, n)
                nc.vector.tensor_tensor(g_b[u][:, :], g_z[u][:, :], g_hs[1 - u][:, :], ALU.mult).then_inc(g_br, 1)
                v.wait_ge(g_nr, n)
                nc.vector.tensor_tensor(g_a[u][:, :], g_omz[u][:, :], g_n[u][:, :], ALU.mult).then_inc(g_ar, 1)
                v.wait_ge(g_ar, n + 1)
                nc.vector.tensor_tensor(g_hs[u][:, :], g_a[u][:, :], g_b[u][:, :], ALU.add).then_inc(g_hr, 1)

    def gru_pool(pool):
        with pool.Fori(0, L // UN) as i:
            for st in range(UN):
                u = st % 2
                t = i * UN + st
                pool.wait_ge(g_ar, t + 2)
                nc.gpsimd.tensor_tensor(big2[0:64, bass.ds(t * B, B)], g_a[u][0:64, :], g_b[u][0:64, :], ALU.add)
                nc.gpsimd.tensor_tensor(big2[64:128, bass.ds((i * (-UN) + (L - 1 - st)) * B, B)], g_a[u][64:128, :], g_b[u][64:128, :],
                                        ALU.add).then_inc(g_yr, 1)

    gg = [big1[0:64, 512 * l:512 * (l + 1)] for l in range(2)]
    cb = [big1[:, 1024 + 512 * l:1024 + 512 * (l + 1)] for l in range(2)]
    o_p, o_g, o_c, o_r, o_o, o_h = (sem("6_" + n) for n in ("products", "gate", "gated", "reverse", "projected", "h_written"))

    def stage6_pe(pe):
        with pe.Fori(0, NJ4 // 2) as i:
            LN = [(l, i * 2 + (l + 1)) for l in range(2)]
            for l, n in LN:
                pe.wait_ge(o_h, n)
                rhs = ys[:, :, bass.ds(i * 8 + 4 * l, 4)].rearrange("p t b -> p b t")
                nc.tensor.matmul(T(l, 0)[0:64, :], c("g_gate"), rhs, start=True, stop=True)
                nc.tensor.matmul(T(l, 1)[0:64, :], c("g_diff"), rhs, start=True, stop=True).then_inc(o_p, 1)
            for l, n in LN:
                pe.wait_ge(o_c, n)
                pe.wait_ge(o_r, n)
                nc.tensor.matmul(T(l, 2)[:, 0:256], eye, c("g_bout"), start=True, stop=False)
                for b in range(4):
                    m = nc.tensor.matmul(T(l, 2)[:, 64 * b:64 * b + 64], cb[l][:, 128 * b:128 * b + 128], c("g_out"), start=False, stop=(b == 3))
                m.then_inc(o_o, 1)

    def stage6_act(act):
        with act.Fori(0, NJ4 // 2) as i:
            for l in range(2):
                n = i * 2 + (l + 1)
                act.wait_ge(o_p, n)
                nc.scalar.activation(gg[l], T(l, 0)[0:64, :], ACT.Sigmoid, bias=c("g_bgate")[0:64]).then_inc(o_g, 1)
                nc.scalar.activation(cb[l][64:128, :].rearrange("p (b t) -> p b t", b=4),
                                     ys[64:128, :, bass.ds(i * 8 + 4 * l, 4)].rearrange("p t b -> p b t"), ACT.Identity).then_inc(o_r, 1)

    def stage6_dve(v):
        with v.Fori(0, NJ4 // 2) as i:
            LN = [(l, i * 2 + (l + 1)) for l in range(2)]
            for l, n in LN:
                v.wait_ge(o_g, n)
                nc.vector.tensor_tensor(cb[l][0:64, :], T(l, 1)[0:64, :], gg[l], ALU.mult).then_inc(o_c, 1)
            for l, n in LN:
                v.wait_ge(o_o, n)
                hp = h[:, bass.ds(i * 8 + 4 * l, 4), :]
                nc.vector.tensor_tensor(hp, hp, T(l, 2)[:, 0:256].rearrange("p (b c) -> p b c", c=C), ALU.add).then_inc(o_h, 1)

    NJ7 = B // 8
    m_xs = [big1[:, 512 * k:512 * (k + 1)] for k in range(2)]
    m_xT = [big1[:, 1024 + 512 * k:1024 + 512 * (k + 1)] for k in range(2)]
    m_y = [big1[:, 2048 + 512 * k:2048 + 512 * (k + 1)] for k in range(2)]
    m_red = [big1[:, 3072 + 512 * k:3072 + 512 * (k + 1)] for k in range(2)]
    hid = [big2[:, 4096 * k:4096 * (k + 1)] for k in range(2)]

    def small(at, cols):
        return [big1[:, 4096 + 1024 * k + at:4096 + 1024 * k + at + cols] for k in range(2)]
    m_lg, m_m8, m_i8 = small(0, 64), small(64, 64), small(128, 64)
    m_if, m_d, m_w1, m_w2 = small(192, 16), small(208, 8), small(216, 8), small(224, 8)
    m_e1, m_e2, m_c1, m_c2, m_comb = small(256, 64), small(320, 64), small(384, 64), small(448, 64), small(512, 64)
    (m_xs_r, m_t_r, m_xT_r, m_lg_r, m_d_r, m_ex_r, m_comb_r, m_step, m_hp, m_ra, m_rv, m_yp, m_add, m_mul, m_rd, m_h_r) = (
        sem("7_" + n) for n in ("rows", "rowsT", "rowsT_copied", "gate_logits", "top_diff", "top_exp", "combine", "gate_steps", "hidden",
                                "relu_even", "relu_odd", "expert_out", "biased", "weighted", "reduced", "h_written"))
    STEPS7 = 27

    def stage7_pool(pool):
        with pool.Fori(0, NJ7 // 2) as i:
            for l in range(2):
                J = i * 2 + l
                pool.wait_ge(m_t_r, J + 1)
                nc.gpsimd.tensor_tensor(m_xs[l].rearrange("p (b c) -> p b c", c=C), xc[:, bass.ds(i * 16 + 8 * l, 8), :],
                                        rstd_of(i * 16 + 8 * l, 8), ALU.mult).then_inc(m_xs_r, 1)
                pool.wait_ge(m_comb_r, J + 1)
                for s in range(2):
                    for p in range(4):
                        pool.wait_ge(m_add, J * 8 + (4 * s + p + 3))
                        y = m_y[p % 2].rearrange("p (e c) -> p e c", e=8)
                        nc.gpsimd.tensor_tensor(y, y, m_comb[l][:, 8 * (2 * p + s):8 * (2 * p + s) + 8].unsqueeze(2).to_broadcast([128, 8, C]),
                                                ALU.mult).then_inc(m_mul, 1)

    def stage7_pe(pe):
        with pe.Fori(0, NJ7 // 2) as i:
            for l in range(2):
                J = i * 2 + l
                pe.wait_ge(m_xs_r, J + 1)
                pe.wait_ge(m_xT_r, J + 1)
                for p in range(4):
                    m = nc.tensor.transpose(T(0, 0)[:, 128 * p:128 * p + 128], m_xs[l][:, 128 * p:128 * p + 128], eye)
                m.then_inc(m_t_r, 1)
                pe.wait_ge(m_xT_r, J + 2)
                for p in range(4):
                    m = nc.tensor.matmul(T(0, 1)[:, 16 * p:16 * p + 16], m_xT[l][:, 128 * p:128 * p + 128], c("m_g"), start=True, stop=True)
                m.then_inc(m_lg_r, 1)
                for s in range(2):
                    for e in range(8):
                        pe.wait_ge(m_ra if e % 2 == 0 else m_rv, J * 8 + (4 * s + e // 2 + 1))
                        nc.tensor.matmul(T(0, 2 + e % 2), c("m_w1", 128 * (8 * s + e), 128 * (8 * s + e + 1)), m_xT[l],
                                         start=True, stop=True).then_inc(m_hp, 1)
                for s in range(2):
                    pe.wait_ge(m_ra, J * 8 + (4 * s + 5))
                    pe.wait_ge(m_rv, J * 8 + (4 * s + 5))
                    for p in range(4):
                        pe.wait_ge(m_add, J * 8 + (4 * s + p + 1))
                        for e in range(8):
                            o = 512 * (2 * (p % 2) + e // 4) + 96 * (e % 4)
                            m = nc.tensor.matmul(pt[1][:, o:o + 96], hid[s][:, 512 * e + 128 * p:512 * e + 128 * p + 128],
                                                 c("m_w2", 64 * e, 64 * e + 96), start=True, stop=True)
                        m.then_inc(m_yp, 1)

    def stage7_act(act):
        with act.Fori(0, NJ7 // 2) as i:
            for l in range(2):
                J = i * 2 + l
                act.wait_ge(m_t_r, J + 3)
                nc.scalar.copy(m_xT[l], T(0, 0)).then_inc(m_xT_r, 1)
                act.wait_ge(m_d_r, J + 1)
                nc.scalar.activation(m_d[l], m_d[l], ACT.Exp).then_inc(m_ex_r, 1)
                for s in range(2):
                    act.wait_ge(m_yp, J * 8 + (4 * s + 4))
                    for e in range(0, 8, 2):
                        act.wait_ge(m_hp, J * 16 + (8 * s + e + 1))
                        nc.scalar.activation(hid[s][:, 512 * e:512 * (e + 1)], T(0, 2), ACT.Relu, bias=c("m_b1", e, e + 1)).then_inc(m_ra, 1)

    def stage7_dve(v):
        def reduce(i, l, s, p):
            v.wait_ge(m_mul, (i * 2 + l) * 8 + (4 * s + p + 1))
            b = 2 * p + s
            nc.vector.tensor_reduce(m_red[l][:, 64 * b:64 * b + 64], m_y[p % 2].rearrange("p (e c) -> p c e", e=8), X, ALU.add).then_inc(m_rd, 1)
        with v.Fori(0, NJ7 // 2) as i:
            for l in range(2):
                J = i * 2 + l
                k = [0]

                def step(ins, ordered=True):
                    k[0] += 1
                    ins.then_inc(m_step, 1)
                    if ordered:
                        v.wait_ge(m_step, J * STEPS7 + k[0])
                v.wait_ge(m_lg_r, J + 1)
                step(nc.vector.tensor_tensor(m_lg[l], T(0, 1)[:, 0:64], m_bg[:, :], ALU.add))
                step(nc.vector.memset(spare[:, 30:31], 0.0), ordered=False)
                for b in range(8):
                    step(nc.vector.max(m_m8[l][:, 8 * b:8 * b + 8], m_lg[l][:, 8 * b:8 * b + 8]), ordered=(b == 7))
                step(nc.vector.memset(spare[:, 31:32], 0.0), ordered=False)
                for b in range(8):
                    step(nc.vector.max_index(m_i8[l][:, 8 * b:8 * b + 8].bitcast(U32), m_m8[l][:, 8 * b:8 * b + 8],
                                             m_lg[l][:, 8 * b:8 * b + 8]), ordered=(b == 7))
                top = m_m8[l].rearrange("p (b k) -> p b k", k=8)
                nc.vector.tensor_tensor(m_d[l], top[:, :, 1], top[:, :, 0], ALU.subtract).then_inc(m_d_r, 1)
                step(nc.vector.tensor_copy(m_if[l].rearrange("p (b k) -> p b k", k=2),
                                           m_i8[l].bitcast(U32).rearrange("p (b k) -> p b k", k=8)[:, :, 0:2]))
                which = m_if[l].rearrange("p (b k) -> p b k", k=2)
                iota = c("iota").unsqueeze(1).to_broadcast([128, 8, 8])

                def e8(t):
                    return t.rearrange("p (b e) -> p b e", e=8)
                step(nc.vector.tensor_tensor(e8(m_e1[l]), iota, which[:, :, 0:1].to_broadcast([128, 8, 8]), ALU.is_equal), ordered=False)
                step(nc.vector.tensor_tensor(e8(m_e2[l]), iota, which[:, :, 1:2].to_broadcast([128, 8, 8]), ALU.is_equal))
                v.wait_ge(m_ex_r, J + 1)
                step(nc.vector.tensor_scalar(m_w1[l], m_d[l], 1.0, None, ALU.add))
                step(nc.vector.reciprocal(m_w1[l], m_w1[l]))
                step(nc.vector.tensor_tensor(m_w2[l], m_d[l], m_w1[l], ALU.mult), ordered=False)
                step(nc.vector.tensor_tensor(e8(m_c1[l]), e8(m_e1[l]), m_w1[l].unsqueeze(2).to_broadcast([128, 8, 8]), ALU.mult))
                step(nc.vector.tensor_tensor(e8(m_c2[l]), e8(m_e2[l]), m_w2[l].unsqueeze(2).to_broadcast([128, 8, 8]), ALU.mult))
                nc.vector.tensor_tensor(m_comb[l], m_c1[l], m_c2[l], ALU.add).then_inc(m_comb_r, 1)
                assert k[0] == 19 + 8, k[0]
                for s in range(2):
                    v.wait_ge(m_yp, J * 8 + (4 * s + 4))
                    for e in range(1, 8, 2):
                        v.wait_ge(m_hp, J * 16 + (8 * s + e + 1))
                        nc.vector.tensor_scalar(hid[s][:, 512 * e:512 * (e + 1)], T(0, 3), c("m_b1", e, e + 1), 0.0, ALU.add, ALU.max).then_inc(m_rv, 1)
                for s in range(2):
                    for p in range(4):
                        v.wait_ge(m_yp, J * 8 + (4 * s + p + 9))
                        v.wait_ge(m_rd, J * 8 + (4 * s + p + 1))
                        y = pt[1][:, 1024 * (p % 2):1024 * (p % 2) + 1024].rearrange("p (b x) -> p b x", b=2)[:, :, 0:384]
                        nc.vector.tensor_tensor(m_y[p % 2].rearrange("p (b j c) -> p b j c", b=2, j=4),
                                                y.rearrange("p b (j y) -> p b j y", y=96)[:, :, :, 0:64],
                                                c("m_b2").rearrange("p (b j c) -> p b j c", b=2, j=4), ALU.add).then_inc(m_add, 1)
                        if p:
                            reduce(i, l, s, p - 1)
                    reduce(i, l, s, 3)
                v.wait_ge(m_rd, J * 8 + 10)
                hp = h[:, bass.ds(i * 16 + 8 * l, 8), :]
                nc.vector.tensor_tensor(hp, hp, m_red[l].rearrange("p (b c) -> p b c", c=C), ALU.add).then_inc(m_h_r, 1)

    m_bg, m_bg_r = sb("m_bgs", [128, 64]), sem("7_gate_bias")

    with nc.Block() as block:
        @block.sync
        def _(sp):
            sp.dma_start(cst[:, :], consts).then_inc(loaded, 16)
            for i in range(JA // 2):
                if i >= 2:
                    sp.wait_ge(c1_max, 8 * (i - 1) + 2)
                for t in range(3):
                    sp.dma_start(xin[i % 2][32 * t:32 * (t + 1), :], xp[i, :, t:t + LEN]).then_inc(x_loaded[i % 2], 16)
            with sp.Fori(0, NJ7) as j:
                sp.wait_ge(m_h_r, j + 1)
                sp.dma_start(out[bass.ds(j * 8, 8), :, :].rearrange("b l c -> l b c"), h[:, bass.ds(j * 8, 8), :]).then_inc(stored, 16)
            sp.wait_ge(stored, 16 * NJ7)

        @block.gpsimd
        def _(pool):
            nc.gpsimd.memset(half_neg[:, :], -0.5).then_inc(bn_var, 1)
            nc.gpsimd.memset(one[:, :], 1.0).then_inc(one_set, 1)
            pool.wait_ge(loaded, 16)
            nc.gpsimd.tensor_scalar(bn_s[:, :], c("bn_v"), EPS, None, ALU.add).then_inc(bn_var, 1)
            pool.wait_ge(bn_var, 2)
            nc.gpsimd.tensor_tensor(bn_s[:, :], bn_s[:, :], half_neg[:, 0:1].to_broadcast([128, 83]), ALU.pow).then_inc(bn_rs, 1)
            norm_pool(pool, 0)
            pool.wait_ge(ln_rstd, 4)
            stage2_pool(pool)
            norm_pool(pool, 1)
            pool.wait_ge(ln_rstd, 8)
            pool.wait_ge(f_dve, SETUP3)
            stage3_pool(pool)
            norm_pool(pool, 2)
            norm_pool(pool, 3)
            pool.wait_ge(ln_rstd, 16)
            stage4_pool(pool)
            pool.wait_ge(f_h_r, NP + 2)
            gru_pool(pool)
            norm_pool(pool, 4)
            pool.wait_ge(ln_rstd, 20)
            stage7_pool(pool)

        @block.vector
        def _(v):
            for k in range(2):
                nc.vector.memset(h1[k], 0.0).then_inc(pads_zero, 1)
            nc.vector.memset(h3g, 0.0).then_inc(pads_zero, 1)
            for k, (credited, n) in enumerate(((c1_max, 2), (c2_max, 2), (h1_ready, 2), (h2_ready, 2), (b_h3, 2), (b_h, 1), (b_c3, 1), (a_h_r, 3), (a_oT_r, 3), (f_h_r, 2), (f_s_r, 2),
                                               (r_t, 2), (r_xgf, 2), (r_xgr, 2), (g_yr, 2), (o_h, 2), (m_t_r, 2), (m_xT_r, 1),
                                               (m_ra, 1), (m_rv, 1), (m_add, 2), (m_yp, 8), (m_rd, 2))):
                nc.vector.memset(spare[:, k:k + 1], 0.0).then_inc(credited, n)
            v.wait_ge(loaded, 16)
            nc.vector.tensor_scalar(gbv[:, :], c("bv"), c("gamma"), None, ALU.mult).then_inc(gbv_ready, 1)
            v.wait_ge(bn_rs, 1)
            nc.vector.tensor_tensor(bn_s[:, :], bn_s[:, :], c("bn_g"), ALU.mult).then_inc(bn_scale, 1)
            nc.vector.tensor_tensor(bn_t[:, :], c("bn_b"), c("bn_m"), ALU.subtract).then_inc(bn_scale, 1)
            v.wait_ge(bn_scale, 2)
            nc.vector.tensor_tensor(bn_t[:, :], bn_t[:, :], bn_s[:, 80:83], ALU.mult).then_inc(bn_shift, 1)
            v.wait_ge(bn_shift, 1)
            nc.vector.tensor_tensor(bn_t[:, :], bn_t[:, :], c("bn_be"), ALU.add).then_inc(bn_shift, 1)
            nc.vector.tensor_tensor(w1s[:, :].rearrange("p (a c) -> p a c", c=16), c("w1").rearrange("p (a c) -> p a c", c=16),
                                    bn_s[:, 0:16].unsqueeze(1).to_broadcast([128, 16, 16]), ALU.mult)
            w2v = c("w2").rearrange("p (a c) -> p a c", c=64)
            nc.vector.tensor_tensor(w2v, w2v, bn_s[:, 16:80].unsqueeze(1).to_broadcast([128, 24, 64]), ALU.mult).then_inc(w_scaled, 1)
            nc.vector.tensor_scalar(c("a_bias"), c("a_bias"), -1.0, None, ALU.mult).then_inc(a_setup, 1)
            nc.vector.tensor_scalar(a_bqs[:, :], c("a_bq"), -HD ** -0.5, None, ALU.mult).then_inc(a_setup, 1)
            v.wait_ge(a_pb_ps, 1)
            nc.vector.tensor_tensor(a_pb[:, :], T(1, 3)[:, 0:128], c("a_bp"), ALU.add).then_inc(a_pb_r, 1)
            stage1a_dve(v)
            stage1b_dve(v)
            v.wait_ge(b_h, IB + 1)
            for l in range(2):
                nc.vector.memset(a_v[l], 1.0).then_inc(a_ones, 1)
            norm_dve(v, 0, h)
            v.wait_ge(a_setup, 2)
            stage2_dve(v)
            v.wait_ge(a_h_r, NP + 3)
            norm_dve(v, 1, h)
            setup3_dve(v)
            stage3_dve(v)
            for u in range(2):
                nc.vector.memset(g_hs[u][:, :], 0.0).then_inc(g_setup, 1)
            nc.vector.memset(g_a[1][:, :], 0.0).then_inc(g_ar, 1)
            nc.vector.memset(g_b[1][:, :], 0.0).then_inc(g_br, 1)
            nc.vector.tensor_tensor(g_bias[:, :], c("g_bih"), c("g_bhh"), ALU.add).then_inc(g_setup, 1)
            nc.vector.tensor_tensor(m_bg[:, :], c("m_bg"), c("m_bias"), ALU.add).then_inc(m_bg_r, 1)
            v.wait_ge(g_setup, 3)
            nc.vector.tensor_scalar(g_nbz[:, :], g_bias[:, 1:2], -1.0, None, ALU.mult).then_inc(g_hr, 1)
            v.wait_ge(f_h_r, NP + 2)
            norm_dve(v, 2, h)
            stage4_norm_dve(v)
            stage4_dve(v)
            gru_dve(v)
            stage6_dve(v)
            v.wait_ge(o_h, NJ4 + 2)
            norm_dve(v, 4, h)
            v.wait_ge(m_bg_r, 1)
            stage7_dve(v)

        @block.tensor
        def _(pe):
            pe.wait_ge(loaded, 16)
            nc.tensor.matmul(T(1, 3)[:, 0:128], c("a_bv"), c("a_p"), start=True, stop=True).then_inc(a_pb_ps, 1)
            stage1a_pe(pe)
            pe.wait_ge(h2_ready, JA + 2)
            stage1b_pe(pe)
            pe.wait_ge(a_pb_r, 1)
            pe.wait_ge(b_h, IB + 1)
            stage2_pe(pe)
            setup3_pe(pe)
            pe.wait_ge(f_dve, SETUP3)
            stage3_pe(pe)
            pe.wait_ge(f_h_r, NP + 2)
            stage4_pe(pe)
            pe.wait_ge(r_xgf, NJ4 + 2)
            pe.wait_ge(r_xgr, NJ4 + 2)
            gru_pe(pe)
            pe.wait_ge(g_yr, L + 2)
            pe.wait_ge(g_hr, L + 1)
            stage6_pe(pe)
            pe.wait_ge(o_h, NJ4 + 2)
            stage7_pe(pe)

        @block.scalar
        def _(act):
            stage1a_act(act)
            stage1b_act(act)
            norm_act(act, 0)
            act.wait_ge(a_ones, 2)
            act.wait_ge(a_setup, 2)
            stage2_act(act)
            norm_act(act, 1)
            act.wait_ge(f_dve, SETUP3)
            act.wait_ge(one_set, 1)
            stage3_act(act)
            norm_act(act, 2)
            norm_act(act, 3)
            act.wait_ge(f_h_r, NP + 2)
            stage4_act(act)
            act.wait_ge(g_setup, 3)
            act.wait_ge(g_hr, 1)
            gru_act(act)
            stage6_act(act)
            norm_act(act, 4)
            stage7_act(act)


def lay_out(w):
    big = np.zeros((128, WIDTH), np.float32)

    def put(name, a):
        a = np.asarray(a, np.float32)
        o, n = AT[name]
        assert a.shape[1] == n, (name, a.shape, n)
        big[:a.shape[0], o:o + n] = a

    def col(a):
        return np.asarray(a).reshape(-1, 1)

    def rows(a):
        return np.broadcast_to(np.asarray(a).reshape(1, -1), (128, np.asarray(a).size))

    def diag2(a):
        z = np.zeros((128, 2 * a.shape[1]), np.float32)
        z[:64, :a.shape[1]] = a
        z[64:, a.shape[1]:] = a
        return z

    put("eye", np.eye(128))
    w1 = np.zeros((3, 2, 16, 2, 8, 16), np.float32)
    for b in range(16):
        w1[:, :, b, b // 8, b % 8, :] = w["L0_tok_w1"].transpose(2, 1, 0)
    put("w1", w1.reshape(96, 256))
    w2 = np.zeros((4, 2, 16, 4, 3, 2, 64), np.float32)
    for p in range(4):
        for s in range(2):
            w2[p, s, :, p, :, s, :] = w["L0_tok_w2"].transpose(1, 2, 0)
    put("w2", w2.reshape(128, 12 * 128))
    w3 = np.zeros((2, 64, 2, 4, 128), np.float32)
    for s in range(2):
        w3[s, :, s] = w["L0_tok_w3"].transpose(1, 2, 0)
    put("w3", w3.reshape(128, 8 * 128))
    for n, part in (("v", "v"), ("g", "g")):
        a1, a2, a3 = (np.asarray(w[f"L0_tok_{part}{k}"]) for k in (1, 2, 3))
        put("bn_" + n, np.concatenate([rows(a1), rows(a2), col(np.tile(a1, 8)), col(np.tile(a2, 2)), col(a3)], 1))
    for n, part in (("b", "b"), ("m", "m"), ("be", "be")):
        a1, a2, a3 = (np.asarray(w[f"L0_tok_{part}{k}"]) for k in (1, 2, 3))
        put("bn_" + n, np.concatenate([col(np.tile(a1, 8)), col(np.tile(a2, 2)), col(a3)], 1))
    zq, zk = np.zeros((2, 64, 2, 2, 64), np.float32), np.zeros((2, 64, 2, 64), np.float32)
    zbq, zbk = np.zeros((2, 64, 2), np.float32), np.zeros((2, 64, 1), np.float32)
    for s in range(2):
        zq[s, :, s, s, :8] = w["L0_tok_wq"].T
        zk[s, :, s, :8] = w["L0_tok_wk"].T
        zbq[s, :8, s] = w["L0_tok_bq"]
        zbk[s, :8, 0] = w["L0_tok_bk"]
    put("wq", zq.reshape(128, 256))
    put("wk", zk.reshape(128, 128))
    put("bq", zbq.reshape(128, 2))
    put("bk", zbk.reshape(128, 1))
    put("wv", diag2(w["L0_tok_wv"].T))
    put("bv", col(np.tile(w["L0_tok_bv"], 2)))
    put("gamma", col(np.broadcast_to(w["L0_tok_gamma"], (128,))))
    lay_out_more(w, put, col, rows, diag2)
    return big


def lay_out_more(w, put, col, rows, diag2):
    qkv = w["L0_attn_qkv_weight"]
    qkv_b = w["L0_attn_qkv_bias"]
    for k, n in enumerate(("a_q", "a_k", "a_v")):
        put(n, diag2(qkv[64 * k:64 * (k + 1)].T))
    put("a_bq", col(np.tile(qkv_b[0:64], 2)))
    put("a_bk", col(np.tile(qkv_b[64:128], 2)))
    put("a_bv", np.broadcast_to(col(np.tile(qkv_b[128:192], 2)), (128, 128)))
    put("a_p", diag2(w["L0_attn_proj_weight"].T))
    put("a_bp", rows(np.tile(w["L0_attn_proj_bias"], 2)))
    mask = np.zeros((2, 8, 8, 2, 8), np.float32)
    for s in range(2):
        for k in range(8):
            mask[s, k, :, s, k] = 1.0
    put("a_mask", mask.reshape(128, 16))
    table = w["L0_attn_bias_table"].T
    put("a_bias", np.stack([table[:, q:q + 128][:, ::-1] for q in range(128)]).reshape(128, 1024))
    def headT(a):
        return a.reshape(64, 8, 64).transpose(2, 1, 0).reshape(64, 512)
    put("f_fxT", headT(w["L0_ffn_W_fx"]))
    put("f_xT", headT(w["L0_ffn_W_x"]))
    put("f_bfxT", w["L0_ffn_b_fx"].reshape(8, 64).T)
    put("f_bxT", w["L0_ffn_b_x"].reshape(8, 64).T)
    put("f_slice", w["L0_ffn_W_slice"])
    put("f_bslice", rows(w["L0_ffn_b_slice"]))
    for n in "qkv":
        put(f"f_w{n}T", w[f"L0_ffn_W_{n}"].T)
    put("f_out", w["L0_ffn_W_out"].reshape(8, 64, 64).transpose(1, 0, 2).reshape(64, 512))
    put("f_bout", col(np.tile(w["L0_ffn_b_out"], 2)))
    put("f_temp", rows(w["L0_ffn_temperature"]))
    a = "L1_attn_"
    put("g_lng", col(np.tile(w[a + "ln_g"], 2)))
    put("g_lnb", col(np.tile(w[a + "ln_b"], 2)))
    for n in ("ih", "hh"):
        z = np.zeros((2, 64, 3, 2, 64), np.float32)
        zb = np.zeros((2, 64, 3), np.float32)
        for d, way in enumerate(("fwd", "rev")):
            z[d, :, :, d] = w[f"{a}{way}_w_{n}"].reshape(3, 64, 64).transpose(2, 0, 1)
            zb[d] = w[f"{a}{way}_b_{n}"].reshape(3, 64).T
        put("g_" + n, z.reshape(128, 384))
        put("g_b" + n, zb.reshape(128, 3))
    put("g_gate", w[a + "gate_w"].T)
    put("g_bgate", col(w[a + "gate_b"]))
    put("g_diff", np.concatenate([np.eye(64), -np.eye(64)]))
    put("g_out", np.tile(w[a + "out_w"].T, (2, 1)))
    put("g_bout", rows(np.tile(w[a + "out_b"], 4)))
    put("m_g", diag2(w["L1_ffn_Wg"]))
    put("m_bg", rows(np.tile(w["L1_ffn_bg"], 8)))
    put("m_bias", rows(np.tile(w["L1_ffn_bias"], 8)))
    z = np.zeros((2, 64, 2, 8, 128), np.float32)
    for s in range(2):
        z[s, :, s] = w["L1_ffn_W1"].transpose(1, 0, 2)
    put("m_w1", z.reshape(128, 2048))
    put("m_b1", w["L1_ffn_b1"].T)
    put("m_w2", np.concatenate([w["L1_ffn_W2"].transpose(1, 0, 2).reshape(128, 512), np.zeros((128, 32), np.float32)], 1))
    put("m_b2", rows(w["L1_ffn_b2"]))
    put("iota", rows(np.arange(8)))


def kernel(**inputs):
    import concourse.bacc as bacc
    from concourse.bass_utils import run_bass_kernel_spmd

    w = {k: np.asarray(v) for k, v in inputs.items()}
    xp = np.zeros((4, 2, 16, LEN + 2), np.float32)
    xp[:, :, :, 1:LEN + 1] = w["x"].reshape(4, 16, 2, LEN).transpose(0, 2, 1, 3)
    arrays = {"x_dram": xp.reshape(4, 32, LEN + 2), "consts_dram": lay_out(w)}
    nc = bacc.Bacc("TRN2", target_bir_lowering=False, num_devices=1)
    args = [nc.dram_tensor(n, a.shape, F32, kind="ExternalInput").ap() for n, a in arrays.items()]
    out = nc.dram_tensor("out_dram", (B, L, C), F32, kind="ExternalOutput").ap()
    build(nc, *args, out)
    return run_bass_kernel_spmd(nc, [arrays], core_ids=[0]).results[0]["out_dram"]
```

```python
import numpy as np
import concourse.bass as bass
from concourse import mybir

F32 = mybir.dt.float32
U32 = mybir.dt.uint32
ALU = mybir.AluOpType
ACT = mybir.ActivationFunctionType
X = mybir.AxisListType.X
EPS = 1e-5
B, L, C = 64, 128, 64
NP = B // 2
HEADS, HD = 8, 8
G = 64
E = 8
LEN = 4096

PARTS = [
    ("bn_v", 83), ("bn_g", 83), ("bn_b", 3), ("bn_m", 3), ("bn_be", 3), ("w1", 2 * 128), ("w2", 128),
    ("eye", 128), ("w3", 8 * 128),
    ("wq", 256), ("wk", 128), ("bq", 2), ("bk", 1), ("wv", 128), ("bv", 1), ("gamma", 1),
    ("a_q", 128), ("a_k", 128), ("a_bq", 1), ("a_bk", 1), ("a_mask", 16), ("a_v", 128), ("a_bv", 128), ("a_p", 128), ("a_bp", 128),
    ("a_bias", HEADS * 128),
    ("f_fxT", 512), ("f_bfxT", 8), ("f_xT", 512), ("f_bxT", 8), ("f_slice", 64), ("f_bslice", 64),
    ("f_wqT", 64), ("f_wkT", 64), ("f_wvT", 64), ("f_out", 512), ("f_bout", 1), ("f_temp", 8),
    ("g_lng", 1), ("g_lnb", 1), ("g_ih", 3 * 128), ("g_hh", 3 * 128), ("g_bih", 3), ("g_bhh", 3),
    ("g_gate", 64), ("g_diff", 64), ("g_bgate", 1), ("g_out", 64), ("g_bout", 256),
    ("m_g", 16), ("m_bg", 64), ("m_bias", 64), ("m_w1", 16 * 128), ("m_b1", 8), ("m_w2", 512 + 32), ("m_b2", 512), ("iota", 8),
]
AT, WIDTH = {}, 0
for _n, _w in PARTS:
    AT[_n] = (WIDTH, _w)
    WIDTH += _w


def build(nc, xp, consts, out):
    def sb(name, shape, dt=F32):
        return nc.alloc_sbuf_tensor(name, shape, dt)

    def sem(name):
        return nc.alloc_semaphore(name)

    cst = sb("cst", [128, WIDTH])

    def c(name, a=0, b=None):
        o, w = AT[name]
        return cst[:, o + a:o + (w if b is None else b)]

    eye = c("eye")
    h = sb("h", [128, B, C])
    xc = sb("xc", [128, B, C])
    big1 = sb("big1", [128, 2 * LEN])
    big2 = sb("big2", [128, 2 * LEN])
    pt = [nc.alloc_psum_tensor(f"bank{l}", [128, 4 * 512], F32) for l in range(2)]

    def T(l, k, n=1):
        return pt[l][:, 512 * k:512 * (k + n)]

    xin = [big1[0:96, 0:LEN], big1[0:96, LEN:2 * LEN]]
    bn_s = sb("bn_s", [128, 83])
    bn_t = sb("bn_t", [128, 3])
    w1s = sb("w1s", [128, 2 * 128])
    half_neg, eps = sb("half_neg", [128, 1]), sb("eps", [128, 1])
    spare = sb("spare", [128, 32])
    one, one_set = sb("one", [128, 1]), sem("one_set")
    h1raw = [big2[:, 512 * k:512 * (k + 1)] for k in range(2)]
    h2raw = [big2[:, 1024 + 512 * k:1024 + 512 * (k + 1)] for k in range(2)]
    taps = big2[0:96, 2048:2048 + 8 * 512].rearrange("p (k n) -> p k n", k=8)
    h2all = xc[:, :, :].rearrange("p (q s) c -> p q (s c)", s=2)

    conv_loaded, loaded = sem("conv_consts_loaded"), sem("consts_loaded")
    x_loaded = [sem("x_loaded0"), sem("x_loaded1")]
    bn_var, bn_rs, bn_scale, bn_shift = sem("bn_var"), sem("bn_rsqrt"), sem("bn_scale"), sem("bn_shift")
    w_scaled, pads_zero = sem("conv_weights_scaled"), sem("pads_zero")
    c1_sum, c1_max, h1_ready = sem("conv1_sum"), sem("conv1_max"), sem("h1_ready")
    c2_sum, c2_max, h2_ready = sem("conv2_sum"), sem("conv2_max"), sem("h2_ready")
    stored = sem("out_stored")
    b_copy, b_proj, b_q, b_k, b_v = (sem("1b_" + n) for n in ("h2_copied", "projected", "q_ready", "k_ready", "v_ready"))
    b_energy, b_max, b_exp, b_rs, b_norm = (sem("1b_" + n) for n in ("energy", "max", "exp", "rsum", "normed"))
    b_pT, b_pTc, b_att, b_h3, b_c3, b_h = (sem("1b_" + n) for n in ("pT", "pT_copied", "attended", "h3_ready", "conv3", "h_written"))
    gbv_ready = sem("gamma_bv_ready")
    gbv = sb("gbv", [128, 1])

    def big2_bufs(at, cols, n=2):
        return [big2[:, at + cols * k:at + cols * (k + 1)] for k in range(n)]
    h2p, bk_s = big2_bufs(0, 128), big2_bufs(256, 128)
    bq_s, bP, bPT = big2_bufs(512, 256), big2_bufs(1024, 256), big2_bufs(1536, 256)
    bvT = big2_bufs(2048, 128, 4)
    bmx, bsum, brs = big2_bufs(2560, 2), big2_bufs(2564, 2), big2_bufs(2568, 2)
    h3g = [t.rearrange("p (r n) -> p r n", r=4) for t in big2_bufs(2572, 4 * 130)]

    JA = 8

    def turns(engine, per, turn):
        with engine.Fori(0, JA // per - 1) as i:
            for g in range(per):
                turn(i, g)
        for g in range(per):
            turn(JA // per - 1, g)

    def stage1a_pe(pe):
        def conv1(ii, k):
            j, w, g = ii * 4 + k, k // 2, k % 2
            if g == 0:
                pe.wait_ge(x_loaded[w], ii * 48 + 48)
            for q in range(4):
                pe.wait_ge(c1_max, (j * 4) + (q + 1))
                for b in range(2):
                    m = nc.tensor.matmul(T(0, 2 * (q % 2) + b), w1s[0:96, 128 * g:128 * (g + 1)],
                                         xin[w][:, (2 * q + b) * 512:(2 * q + b + 1) * 512], start=True, stop=True)
                m.then_inc(c1_sum, 1)

        def turn(ii, k):
            if k < 3:
                conv1(ii, k + 1)
            elif not isinstance(ii, int) or ii < JA // 4 - 1:
                conv1(ii + 1, 0)
            else:
                pe.wait_ge(c1_max, JA * 4 + 2)
                pe.wait_ge(loaded, 16)
                setup3_first_pe(pe)
            j = ii * 4 + k
            for p in range(4):
                pe.wait_ge(h1_ready, j * 4 + (p + 9))
                pe.wait_ge(c2_max, (j * 4) + (p + 1))
                nc.tensor.matmul(T(1, p), c("w2")[0:96], taps[:, 4 * (k % 2) + p, :], start=True, stop=True).then_inc(c2_sum, 1)
        pe.wait_ge(w_scaled, 1)
        conv1(0, 0)
        pe.wait_ge(w_scaled, 2)
        turns(pe, 4, turn)

    def stage1a_dve(v):
        def max1(i, g):
            j = i * 2 + g
            v.wait_ge(h1_ready, j * 4 + 4)
            for q in range(4):
                v.wait_ge(c1_sum, (j * 4) + (q + 1))
                nc.vector.tensor_reduce(h1raw[g][:, 128 * q:128 * (q + 1)],
                                        T(0, 2 * (q % 2), 2).rearrange("p (n k) -> p n k", k=8), X, ALU.max).then_inc(c1_max, 1)

        def turn(i, g):
            if g == 0:
                max1(i, 1)
                if isinstance(i, int) and i == JA // 2 - 1:
                    v.wait_ge(loaded, 16)
                    setup3_rows_dve(v)
                    nc.vector.tensor_scalar(a_bqs[:, :], c("a_bq"), -HD ** -0.5, None, ALU.mult).then_inc(a_setup, 1)
                    nc.vector.tensor_scalar(c("a_bias"), c("a_bias"), -1.0, None, ALU.mult).then_inc(a_setup, 1)
            elif not isinstance(i, int) or i < JA // 2 - 1:
                max1(i + 1, 0)
            else:
                setup3_middle_dve(v)
            j = i * 2 + g
            v.wait_ge(h2_ready, j + 1)
            for p in range(4):
                v.wait_ge(c2_sum, (j * 4) + (p + 1))
                nc.vector.tensor_reduce(h2raw[g][:, 128 * p:128 * (p + 1)],
                                        T(1, p).rearrange("p (n k) -> p n k", k=4), X, ALU.max).then_inc(c2_max, 1)
        max1(0, 0)
        v.wait_ge(bn_rs, 3)
        nc.vector.tensor_tensor(bn_s[:, 16:80], bn_s[:, 16:80], c("bn_g", 16, 80), ALU.mult).then_inc(bn_scale, 1)
        v.wait_ge(bn_scale, 4)
        w2v = c("w2").rearrange("p (a c) -> p a c", c=64)
        nc.vector.tensor_tensor(w2v, w2v, bn_s[:, 16:80].unsqueeze(1).to_broadcast([128, 2, 64]), ALU.mult).then_inc(w_scaled, 1)
        turns(v, 2, turn)

    def stage1a_act(act):
        def relu1(i, g):
            act.wait_ge(c1_max, i * 8 + (g * 4 + 6))
            for p in range(4):
                raw, to, bias = h1raw[g][32 * p:32 * (p + 1), :], taps[:, 4 * g + p, :], bn_t[32 * p:32 * (p + 1), 0:1]
                nc.scalar.activation(to[0:32, 1:512], raw[:, 0:511], ACT.Relu, bias=bias)
                nc.scalar.activation(to[32:64, :], raw, ACT.Relu, bias=bias)
                nc.scalar.activation(to[64:96, 0:511], raw[:, 1:512], ACT.Relu, bias=bias).then_inc(h1_ready, 1)

        def turn(i, g):
            if g == 0:
                relu1(i, 1)
            elif not isinstance(i, int) or i < JA // 2 - 1:
                relu1(i + 1, 0)
            act.wait_ge(c2_max, i * 8 + (g * 4 + 8))
            nc.scalar.activation(h2all[:, bass.ds(i * 8 + 4 * g, 4), :], h2raw[g].rearrange("p (r n) -> p r n", r=4),
                                 ACT.Relu, bias=bn_t[:, 1:2]).then_inc(h2_ready, 1)
        act.wait_ge(bn_shift, 2)
        act.wait_ge(pads_zero, 2)
        relu1(0, 0)
        turns(act, 2, turn)

    NG = NP // 4

    rowsum, rowsq, rstd = sb("rowsum", [128, B]), sb("rowsq", [128, B]), sb("rstd", [128, B])
    eps_var = sb("eps_var", [128, B])
    squares = [sb(f"squares{k}", [128, 16 * C]) for k in range(2)]
    ln_sum, ln_cent, ln_sq, ln_var, ln_eps, ln_rstd = (sem("ln_" + n) for n in ("sum", "centred", "squared", "var", "eps", "rstd"))
    LN = [0, NG, NG + NP // 2, NG + NP // 2 + NP, NG + NP // 2 + NP + B // 8]

    def part(t, first, n):
        return t[:, bass.ds(first, n)]

    def centre(v, num, first, n, src):
        nc.vector.tensor_reduce(part(rowsum, first, n), part(src, first, n), X, ALU.add).then_inc(ln_sum, 1)
        v.wait_ge(ln_sum, num)
        nc.vector.scalar_tensor_tensor(part(xc, first, n), part(rowsum, first, n).unsqueeze(2).to_broadcast([128, n, C]), -1.0 / C,
                                       part(src, first, n), ALU.mult, ALU.add).then_inc(ln_cent, 1)

    def square(act, num, first, n, parity):
        act.wait_ge(ln_cent, num)
        act.wait_ge(ln_var, num)
        nc.scalar.activation(squares[parity][:, 0:C * n].rearrange("p (b c) -> p b c", c=C), part(xc, first, n), ACT.Square,
                             scale=C ** -0.5).then_inc(ln_sq, 1)

    def variance(v, num, first, n, parity):
        v.wait_ge(ln_sq, num)
        nc.vector.tensor_reduce(part(rowsq, first, n), squares[parity][:, 0:C * n].rearrange("p (b c) -> p b c", c=C), X, ALU.add).then_inc(ln_var, 1)

    def rsqrt(pool, num, first, n):
        pool.wait_ge(ln_var, num + 2)
        nc.gpsimd.tensor_tensor(part(eps_var, first, n), part(rowsq, first, n), eps[:, 0:1].to_broadcast([128, n]), ALU.add).then_inc(ln_eps, 1)
        pool.wait_ge(ln_eps, num)
        nc.gpsimd.tensor_tensor(part(rstd, first, n), part(eps_var, first, n), half_neg[:, 0:1].to_broadcast([128, n]), ALU.pow).then_inc(ln_rstd, 1)

    def stage1b_pool(pool):
        pool.wait_ge(h2_ready, JA + 2)
        for l in range(2):
            nc.gpsimd.memset(f_xs1[l], 1.0).then_inc(f_still, 1)
            nc.gpsimd.memset(f_uz[l], 0.0).then_inc(f_still, 1)
            nc.gpsimd.memset(f_ebd[l], 0.0).then_inc(f_still, 1)
        with pool.Fori(0, N1) as i:
            for par in range(2):
                rsqrt(pool, i * 2 + (par + 1), i * 16 + 8 * par, 8)

    def rstd_of(first, n):
        return rstd[:, bass.ds(first, n)].unsqueeze(2).to_broadcast([128, n, C])

    N1 = NP // 8

    def bank(b):
        return T(b // 4, b % 4)

    def there(i, n):
        return not isinstance(i, int) or 0 <= i < n

    def back8(i, t, d):
        i, t = i + (t - d) // 8, (t - d) % 8
        return i, t, i * 8 + (t + 1)

    def pipelined1(engine, slot):
        for t in range(8):
            slot(0, t)
        with engine.Fori(1, N1 - 1) as i:
            for t in range(8):
                slot(i, t)
        for i in (N1 - 1, N1):
            for t in range(8):
                slot(i, t)

    def stage1b_pe(pe):
        def slot(i, t):
            ig, tg, _ = back8(i, t, 7)
            if there(ig, N1):
                g, part, par = ig * 2 + (tg // 4 + 1), tg % 4, tg // 4
                if part == 0:
                    pe.wait_ge(b_h3, g * 4 + 1)
                    pe.wait_ge(b_h, g)
                for k in (2 * part, 2 * part + 1):
                    m = nc.tensor.matmul(bank(7)[:, 256 * (k // 4):256 * (k // 4 + 1)], c("w3", k * 128, (k + 1) * 128),
                                         h3g[par][:, :, k % 4:k % 4 + 127:2], start=(k % 4 == 0), stop=(k % 4 == 3))
                if part == 3:
                    m.then_inc(b_c3, 1)
            if there(i, N1):
                n = i * 8 + (t + 1)
                pe.wait_ge(b_copy, n)
                if t >= 2 or not isinstance(i, int) or i:
                    pe.wait_ge(b_v, n - 2)
                if t or not isinstance(i, int) or i:
                    pe.wait_ge(b_k, n - 1)
                q = bank(t % 2)
                for k in range(2):
                    nc.tensor.matmul(q[:, 128 * k:128 * (k + 1)], c("wq", 128 * k, 128 * (k + 1)), h2p[t % 2], start=True, stop=True)
                nc.tensor.matmul(bank(2)[:, 0:128], c("wk"), h2p[t % 2], start=True, stop=True)
                nc.tensor.matmul(q[:, 256:384], h2p[t % 2], c("wv"), start=True, stop=True).then_inc(b_proj, 1)
            ij, tj, n = back8(i, t, 1)
            if there(ij, N1):
                pe.wait_ge(b_q, n)
                pe.wait_ge(b_k, n)
                for k in range(2):
                    m = nc.tensor.matmul(bank(3 + tj % 2)[:, 128 * k:128 * (k + 1)], bq_s[tj % 2][:, 128 * k:128 * (k + 1)],
                                         bk_s[tj % 2], start=True, stop=True)
                m.then_inc(b_energy, 1)
            ij, tj, n = back8(i, t, 3)
            if there(ij, N1):
                pe.wait_ge(b_pTc, n)
                pe.wait_ge(b_v, n)
                pe.wait_ge(b_h3, n)
                for k in range(2):
                    m = nc.tensor.matmul(bank(6)[64 * k:64 * k + 64, 0:128], bvT[tj % 4][:, 64 * k:64 * k + 64],
                                         bPT[tj % 2][:, 128 * k:128 * (k + 1)], start=True, stop=True)
                m.then_inc(b_att, 1)
            ij, tj, n = back8(i, t, 2)
            if there(ij, N1):
                pe.wait_ge(b_norm, n)
                for k in range(2):
                    m = nc.tensor.transpose(bank(5)[:, 128 * k:128 * (k + 1)], bP[tj % 2][:, 128 * k:128 * (k + 1)], eye)
                m.then_inc(b_pT, 1)
        pipelined1(pe, slot)

    def stage1b_dve(v):
        def copy(i, t, first=False):
            n = i * 8 + (t + 1)
            if not first:
                v.wait_ge(b_proj, n - 2)
            nc.vector.tensor_copy(h2p[t % 2], h2all[:, i * 8 + t, :]).then_inc(b_copy, 1)

        def slot(i, t):
            if there(i, N1):
                v.wait_ge(b_proj, i * 8 + (t + 1))
                nc.vector.tensor_scalar(bk_s[t % 2], bank(2)[:, 0:128], c("bk"), None, ALU.add).then_inc(b_k, 1)
            ij, tj, n = back8(i, t, 1)
            if there(ij, N1):
                v.wait_ge(b_energy, n)
                nc.vector.tensor_reduce(bmx[tj % 2], bank(3 + tj % 2)[:, 0:256].rearrange("p (s n) -> p s n", s=2), X, ALU.max,
                                        negate=True).then_inc(b_max, 1)
            if t < 7 and there(i, N1):
                copy(i, t + 1, first=(isinstance(i, int) and i == 0 and t == 0))
            elif t == 7 and there(i if not isinstance(i, int) else i + 1, N1):
                copy(i + 1, 0)
            ik, tk, m = back8(i, t, 3)
            if there(ik, N1):
                v.wait_ge(b_att, m)
                nc.vector.scalar_tensor_tensor(h3g[tk // 4][:, tk % 4, 1:129], bank(6)[:, 0:128], gbv[:, 0:1], h2all[:, ik * 8 + tk, :],
                                               ALU.add, ALU.add).then_inc(b_h3, 1)
            if there(ij, N1):
                v.wait_ge(b_exp, n)
                nc.vector.reciprocal(brs[tj % 2], bsum[tj % 2]).then_inc(b_rs, 1)
                v.wait_ge(b_rs, n)
                for k in range(2):
                    P = bP[tj % 2][:, 128 * k:128 * (k + 1)]
                    m = nc.vector.tensor_scalar(P, P, brs[tj % 2][:, k:k + 1], c("gamma"), ALU.mult, ALU.mult)
                m.then_inc(b_norm, 1)
            ig, tg, _ = back8(i, t, 10)
            if tg % 4 == 0 and there(ig, N1):
                g = ig * 2 + tg // 4
                v.wait_ge(b_h, g + 2)
                centre(v, g + 1, ig * 16 + 2 * tg, 8, h)
            ig, tg, _ = back8(i, t, 11)
            if tg % 4 == 0 and there(ig, N1):
                g = ig * 2 + tg // 4
                variance(v, g + 1, ig * 16 + 2 * tg, 8, tg // 4)
        v.wait_ge(h2_ready, JA + 2)
        for k in range(2):
            nc.vector.memset(h3g[k], 0.0).then_inc(pads_zero, 1)
        copy(0, 0, first=True)
        v.wait_ge(pads_zero, 4)
        pipelined1(v, slot)

    def stage1b_act(act):
        def slot(i, t):
            ig, tg, _ = back8(i, t, 10)
            if tg % 4 == 0 and there(ig, N1):
                act.wait_ge(b_c3, ig * 2 + (tg // 4 + 1))
                nc.scalar.activation(h[:, bass.ds(ig * 16 + 2 * tg, 8), :].rearrange("p (r s) c -> p s r c", s=2),
                                     bank(7).rearrange("p (s r c) -> p s r c", s=2, r=4), ACT.Identity,
                                     bias=bn_t[:, 2:3], scale=bn_s[:, 82:83]).then_inc(b_h, 1)
            if there(i, N1):
                act.wait_ge(b_proj, i * 8 + (t + 1))
                for k in range(2):
                    m = nc.scalar.activation(bq_s[t % 2][:, 128 * k:128 * (k + 1)], bank(t % 2)[:, 128 * k:128 * (k + 1)],
                                             ACT.Identity, bias=c("bq", k, k + 1))
                m.then_inc(b_q, 1)
                nc.scalar.copy(bvT[t % 4], bank(t % 2)[:, 256:384]).then_inc(b_v, 1)
            ij, tj, n = back8(i, t, 1)
            if there(ij, N1):
                act.wait_ge(b_max, n)
                for k in range(2):
                    m = nc.scalar.activation(bP[tj % 2][:, 128 * k:128 * (k + 1)], bank(3 + tj % 2)[:, 128 * k:128 * (k + 1)], ACT.Exp,
                                             bias=bmx[tj % 2][:, k:k + 1], accum_out=bsum[tj % 2][:, k:k + 1])
                m.then_inc(b_exp, 1)
            ij, tj, n = back8(i, t, 2)
            if there(ij, N1):
                act.wait_ge(b_pT, n)
                nc.scalar.copy(bPT[tj % 2], bank(5)[:, 0:256]).then_inc(b_pTc, 1)
            ig, tg, _ = back8(i, t, 11)
            if tg % 4 == 0 and there(ig, N1):
                square(act, ig * 2 + (tg // 4 + 1), ig * 16 + 2 * tg, 8, tg // 4)
        pipelined1(act, slot)

    big = [big1, big2]

    def lane(at, cols):
        return [big[l][:, at:at + cols] for l in range(2)]
    xs, xT, a_q, a_k = lane(0, 128), lane(128, 128), lane(256, 128), lane(384, 128)
    a_v = lane(512, 2 * 168)
    a_kz = lane(1024, 2048)
    a_o, a_oT = lane(5136, 128), lane(5264, 128)

    def four(at, cols):
        return [big[k // 2][:, at + cols * (k % 2):at + cols * (k % 2 + 1)] for k in range(4)]
    a_P, a_PT, a_mx, a_rs = four(3072, 512), four(4096, 512), four(5120, 4), four(5128, 4)
    a_bqs, a_pb = sb("a_bqs", [128, 1]), sb("a_pb", [128, 128])
    (a_xs_r, a_t_r, a_xT_r, a_qkv_r, a_q_r, a_v_r, a_k_r, a_kz_r, a_sc_r, a_mx_r, a_e_r, a_pt_r, a_ptc_r, a_av_r, a_rs_r,
     a_o_r, a_ot_r, a_oT_r, a_pr_r, a_h_r) = (sem("2_" + n) for n in (
         "rows", "rowsT", "rowsT_copied", "qkv", "q_ready", "v_ready", "k_ready", "k_spread", "scores", "max", "exp", "pT", "pT_copied",
         "attended", "rsum", "heads_out", "outT", "outT_copied", "projected", "h_written"))
    a_setup, a_pb_ps, a_pb_r, a_ones = sem("2_constants"), sem("2_pb_product"), sem("2_pb"), sem("2_ones")

    N2 = NP // 2

    def back(i, t, d):
        return (i, t - d) if t >= d else (i - 1, t - d + 8)

    def exists(i, d, last=N2 - 1):
        return not isinstance(i, int) or 0 <= i + d <= last

    def pipelined(engine, slot):
        for t in range(8):
            slot(0, t)
        with engine.Fori(1, N2 - 1) as i:
            for t in range(8):
                slot(i, t)
        for t in range(8):
            slot(N2 - 1, t)
        for t in range(8):
            slot(N2, t)

    def stage2_pool(pool):
        def rows(i, l, first=False):
            n = i * 2 + (l + 1)
            if not first:
                pool.wait_ge(a_t_r, n - 2)
            nc.gpsimd.tensor_tensor(xs[l].rearrange("p (b c) -> p b c", c=C), xc[:, bass.ds(i * 4 + 2 * l, 2), :],
                                    rstd_of(i * 4 + 2 * l, 2), ALU.mult).then_inc(a_xs_r, 1)

        def spread(i, l):
            for u in range(4):
                pool.wait_ge(a_k_r, i * 2 + (l + 1))
                nc.gpsimd.tensor_tensor(a_kz[l][:, 512 * u:512 * (u + 1)].rearrange("p (h k) -> p h k", h=4),
                                        a_k[l].unsqueeze(1).to_broadcast([128, 4, 128]),
                                        c("a_mask", 4 * u, 4 * u + 4).unsqueeze(2).to_broadcast([128, 4, 128]), ALU.mult).then_inc(a_kz_r, 1)

        def finish(i):
            rsqrt(pool, i + (LN[1] + 1), i * 4, 4)

        rows(0, 0, True)
        rows(0, 1, True)
        spread(0, 0)
        for i in (1, 2):
            rows(i, 0)
            spread(i - 1, 1)
            rows(i, 1)
            spread(i, 0)
        with pool.Fori(3, N2) as i:
            finish(i - 3)
            rows(i, 0)
            spread(i - 1, 1)
            rows(i, 1)
            spread(i, 0)
        spread(N2 - 1, 1)
        pool.wait_ge(ln_rstd, LN[1] + 1)
        pool.wait_ge(a_t_r, NP)
        pool.wait_ge(f_still, 6)
        stage3_pool(pool, start=0)
        finish(N2 - 3)
        finish(N2 - 2)
        stage3_pool(pool, start=1)
        finish(N2 - 1)

    def stage2_pe(pe):
        def rows(i, l):
            pe.wait_ge(a_xs_r, i * 2 + (l + 1))
            if l or exists(i, -1):
                pe.wait_ge(a_v_r, i * 2 + l)
            pe.wait_ge(a_oT_r, i * 2 + (l + 1))
            nc.tensor.transpose(bank(2)[:, 0:128], xs[l], eye).then_inc(a_t_r, 1)

        def qkv(i, l):
            pe.wait_ge(a_xT_r, i * 2 + (l + 1))
            pe.wait_ge(a_h_r, i * 2 + (l + 1))
            nc.tensor.matmul(bank(2)[:, 128:256], c("a_q"), xT[l], start=True, stop=True)
            nc.tensor.matmul(bank(3)[:, 0:128], c("a_k"), xT[l], start=True, stop=True)
            nc.tensor.matmul(bank(2)[:, 256:384], xT[l], c("a_v"), start=True, stop=True).then_inc(a_qkv_r, 1)

        def slot(i, t):
            l, u = t // 4, t % 4
            if exists(i, 0):
                if u == 0:
                    pe.wait_ge(a_q_r, i * 2 + (l + 1))
                pe.wait_ge(a_kz_r, i * 8 + (t + 1))
                if t >= 2 or exists(i, -1):
                    pe.wait_ge(a_mx_r, i * 8 + (t - 1))
                nc.tensor.matmul(bank(t % 2), a_q[l], a_kz[l][:, 512 * u:512 * (u + 1)], start=True, stop=True).then_inc(a_sc_r, 1)
            if u == 0 and exists(i, l, N2 - 1):
                rows(i + l, 1 - l)
            if u == 1 and exists(i, l, N2 - 1):
                qkv(i + l, 1 - l)
            ib, tb = back(i, t, 2)
            if exists(ib, 0):
                pe.wait_ge(a_e_r, ib * 8 + (tb + 1))
                if tb >= 4 or exists(ib, -1):
                    pe.wait_ge(a_o_r, ib * 8 + (tb - 3))
                for k in range(4):
                    m = nc.tensor.transpose(bank(4 + tb % 4)[:, 128 * k:128 * (k + 1)], a_P[tb % 4][:, 128 * k:128 * (k + 1)], eye)
                m.then_inc(a_pt_r, 1)
            if u == 3:
                ij, lj = (i, 0) if l else (i - 1, 1)
                if exists(ij, 0):
                    if exists(i, l):
                        pe.wait_ge(a_v_r, i * 2 + (l + 2))
                    pe.wait_ge(a_o_r, ij * 8 + (4 * lj + 4))
                    nc.tensor.transpose(bank(2)[:, 384:512], a_o[lj], eye).then_inc(a_ot_r, 1)
            if u == 0 and exists(i, -1, N2 - 1):
                pe.wait_ge(a_oT_r, i * 2 + (l + 2))
                pe.wait_ge(a_h_r, i * 2 + (l + 1))
                nc.tensor.matmul(bank(3)[:, 128:256], a_oT[l], c("a_p"), start=True, stop=False)
                nc.tensor.matmul(bank(3)[:, 128:256], eye, a_pb[:, :], start=False, stop=True).then_inc(a_pr_r, 1)
            ib, tb = back(i, t, 3)
            if exists(ib, 0):
                pe.wait_ge(a_ptc_r, ib * 8 + (tb + 1))
                if tb % 4 == 0:
                    pe.wait_ge(a_v_r, ib * 2 + (tb // 4 + 1))
                at = 168 * (tb % 4 // 2) + 36 * (tb % 2)
                for k in range(4):
                    m = nc.tensor.matmul(bank(4 + tb % 4)[:, 96 * k:96 * (k + 1)], a_PT[tb % 4][:, 128 * k:128 * (k + 1)],
                                         a_v[tb // 4][:, at + 9 * k:at + 9 * k + 96], start=True, stop=True)
                m.then_inc(a_av_r, 1)
            if isinstance(i, int) and i == N2 and t < 2:
                stage3_pe(pe, start=t)
        rows(0, 0)
        qkv(0, 0)
        pe.wait_ge(f_dve, SETUP3)
        pipelined(pe, slot)

    def stage2_act(act):
        def rows(i, l):
            act.wait_ge(a_t_r, i * 2 + (l + 1))
            nc.scalar.copy(xT[l], bank(2)[:, 0:128]).then_inc(a_xT_r, 1)

        def queries(i, l):
            act.wait_ge(a_qkv_r, i * 2 + (l + 1))
            nc.scalar.activation(a_q[l], bank(2)[:, 128:256], ACT.Identity, bias=a_bqs[:, 0:1], scale=-HD ** -0.5).then_inc(a_q_r, 1)

        def values(i, l):
            if not isinstance(i, int) or i:
                act.wait_ge(a_av_r, i * 8 + (4 * l - 4))
            for s in range(2):
                m = nc.scalar.copy(a_v[l][:, 168 * s:168 * s + 72].rearrange("p (h d) -> p h d", h=8)[:, :, 0:8],
                                   bank(2)[:, 256 + 64 * s:320 + 64 * s].rearrange("p (h d) -> p h d", h=8))
            m.then_inc(a_v_r, 1)

        def slot(i, t):
            l, u = t // 4, t % 4
            if u == 0 and exists(i, l, N2 - 1):
                rows(i + l, 1 - l)
            ib, tb = back(i, t, 1)
            if exists(ib, 0):
                act.wait_ge(a_mx_r, ib * 8 + (tb + 1))
                for k in range(4):
                    P = a_P[tb % 4][:, 128 * k:128 * (k + 1)]
                    m = nc.scalar.activation(P, P, ACT.Exp, bias=a_mx[tb % 4][:, k:k + 1], scale=-1.0)
                m.then_inc(a_e_r, 1)
            if u == 1 and exists(i, l, N2 - 1):
                queries(i + l, 1 - l)
            if u == 3 and exists(i, l, N2 - 1):
                values(i + l, 1 - l)
            if u == 3:
                ij, lj = (i, 0) if l else (i - 1, 1)
                if exists(ij, 0):
                    act.wait_ge(a_ot_r, ij * 2 + (lj + 1))
                    nc.scalar.copy(a_oT[lj], bank(2)[:, 384:512]).then_inc(a_oT_r, 1)
            if t == 6 and exists(i, -1):
                square(act, i + LN[1], i * 4 - 4, 4, 0)
            if isinstance(i, int) and i == N2 and t in (0, 2):
                stage3_act(act, start=t // 2)
        rows(0, 0)
        queries(0, 0)
        values(0, 0)
        pipelined(act, slot)

    def stage2_dve(v):
        def keys(i, l):
            v.wait_ge(a_qkv_r, i * 2 + (l + 1))
            nc.vector.tensor_scalar(a_k[l], bank(3)[:, 0:128], c("a_bk"), None, ALU.add).then_inc(a_k_r, 1)

        def slot(i, t):
            l, u = t // 4, t % 4
            if exists(i, 0):
                v.wait_ge(a_sc_r, i * 8 + (t + 1))
                nc.vector.memset(spare[:, 24 + t:25 + t], 0.0)
                for k in range(4):
                    m = nc.vector.tensor_tensor_reduce(a_P[t % 4][:, 128 * k:128 * (k + 1)], bank(t % 2)[:, 128 * k:128 * (k + 1)],
                                                       c("a_bias", 512 * (u % 2) + 128 * k, 512 * (u % 2) + 128 * (k + 1)), 1.0, 3e38,
                                                       ALU.add, ALU.min, a_mx[t % 4][:, k:k + 1])
                m.then_inc(a_mx_r, 1)
            if u == 1 and exists(i, l, N2 - 1):
                keys(i + l, 1 - l)
            ib, tb = back(i, t, 2)
            if exists(ib, 0):
                v.wait_ge(a_pt_r, ib * 8 + (tb + 1))
                nc.vector.tensor_copy(a_PT[tb % 4], bank(4 + tb % 4)).then_inc(a_ptc_r, 1)
            if u == 0 and exists(i, -1, N2 - 1):
                v.wait_ge(a_pr_r, i * 2 + (l - 1))
                hp = h[:, bass.ds(i * 4 + (2 * l - 4), 2), :]
                nc.vector.tensor_tensor(hp, hp, bank(3)[:, 128:256].rearrange("p (b c) -> p b c", c=C), ALU.add).then_inc(a_h_r, 1)
            ib, tb = back(i, t, 3)
            if exists(ib, 0):
                v.wait_ge(a_av_r, ib * 8 + (tb + 1))
                res = bank(4 + tb % 4)[:, 0:384].rearrange("p (j y) -> p j y", y=96)
                nc.vector.reciprocal(a_rs[tb % 4], res[:, :, 8]).then_inc(a_rs_r, 1)
                v.wait_ge(a_rs_r, ib * 8 + (tb + 1))
                at = 32 * (tb % 4)
                nc.vector.tensor_tensor(a_o[tb // 4][:, at:at + 32].rearrange("p (j d) -> p j d", j=4), res[:, :, 0:8],
                                        a_rs[tb % 4].unsqueeze(2).to_broadcast([128, 4, 8]), ALU.mult).then_inc(a_o_r, 1)
            if isinstance(i, int) and i == N2 and t in (2, 4):
                stage3_dve(v, start=t // 2 - 1)
            if t == 5 and exists(i, -1):
                v.wait_ge(a_h_r, i * 2 + 3)
                centre(v, i + LN[1], i * 4 - 4, 4, h)
            if t == 7 and exists(i, -1):
                variance(v, i + LN[1], i * 4 - 4, 4, 0)
        keys(0, 0)
        pipelined(v, slot)

    f_xs1 = lane(7992, 192)
    f_w, f_wT = lane(512, 1024), lane(1536, 1024)
    f_tk, f_tT = lane(2560, 512), lane(3072, 512)
    f_y = lane(3584, 1024)
    f_vw, f_oT = lane(4608, 512), lane(5120, 128)
    f_le, f_uz, f_ebd = lane(5376, 512), lane(5888, 1024), lane(6912, 1024)
    f_mx, f_rs, f_nr, f_lmx, f_zr = lane(7936, 16), lane(7952, 16), lane(7968, 8), lane(7976, 8), lane(7984, 8)
    fA, fB, fX = sb("fA", [128, 1024]), sb("fB", [128, 1024]), sb("fX", [128, 1024])
    f_tmp = big1[0:64, :]
    fXT, fFT, fM, fV = (f_tmp[:, a:a + 512] for a in (2048, 3072, 3584, 4096))
    fsum, fGT, fti = f_tmp[:, 2560:2576], f_tmp[:, 2624:2688], sb("f_tinv", [128, 8])
    f_still, f_zero = sem("3_ones_and_zeros"), sem("3_weights_zeroed")
    f_dve, f_pe = sem("3_setup_vector"), sem("3_setup_products")
    (f_xs_r, f_xs1_r, f_t_r, f_xT_r, f_lg_r, f_mx_r, f_sub_r, f_exp_r, f_sum_r, f_rs_r, f_w_r, f_wt_r, f_s_r, f_wT_r, f_nr_r, f_nr2_r,
     f_tk_r, f_tt_r, f_tT_r, f_u_r, f_vw_r, f_uz0_r, f_uz1_r, f_vwc_r, f_l_r, f_lmx_r, f_ls_r, f_e_r, f_es_r, f_er_r, f_eb_r,
     f_y_r, f_ya_r, f_yv_r, f_o_r, f_oT_r, f_ot_r, f_h_r) = (sem("3_" + n) for n in (
         "rows", "rows_plus_1", "rowsT", "rowsT_copied", "logits", "max", "shifted", "exp", "sum", "rsum", "weights", "weightsT", "slices",
         "weightsT_copied", "norm", "rnorm", "tokens", "tokensT", "tokensT_copied", "keys_mixed", "values_mixed", "mixed_0", "mixed_1",
         "values_copied", "pairs", "pairs_max", "pairs_shifted", "pairs_exp", "pairs_sum", "pairs_rsum", "pairs_scaled",
         "attended", "attended_lo", "attended_hi", "outT", "outT_biased", "out", "h_written"))

    def heads(ap):
        return ap.rearrange("p (h c) -> p h c", h=8)

    def setup3_step(v, k):
        def step(ins):
            k[0] += 1
            ins.then_inc(f_dve, 1)
            v.wait_ge(f_dve, k[0])
        return step

    def setup3_rows_dve(v):
        step = setup3_step(v, [0])
        step(nc.vector.tensor_scalar(fti[:, :], c("f_temp"), 0.1, 5.0, ALU.max, ALU.min))
        step(nc.vector.reciprocal(fti[:, :], fti[:, :]))
        for raw, b, to, at in (("f_fxT", "f_bfxT", fFT, 0), ("f_xT", "f_bxT", fXT, 8)):
            part = fsum[:, at:at + 8]
            step(nc.vector.tensor_reduce(part, heads(c(raw)[0:64]), X, ALU.add))
            step(nc.vector.tensor_tensor(part, c(b)[0:64], part, ALU.subtract))
            step(nc.vector.scalar_tensor_tensor(heads(to), part.unsqueeze(2).to_broadcast([64, 8, 64]), 1.0 / C, heads(c(raw)[0:64]),
                                                ALU.mult, ALU.add))

    def setup3_middle_dve(v):
        step = setup3_step(v, [8])
        v.wait_ge(f_zero, 3)
        v.wait_ge(f_pe, 1)
        step(nc.vector.tensor_copy(fGT, T(0, 0)[0:64, 0:64]))
        step(nc.vector.tensor_copy(fV, T(0, 1)[0:64, :]))
        bs = heads(fX[0:64, 0:512])
        step(nc.vector.scalar_tensor_tensor(bs, c("f_bslice")[0:64].unsqueeze(1).to_broadcast([64, 8, 64]), 1.0 / C,
                                            heads(T(0, 2)[0:64, :]), ALU.mult, ALU.add))
        step(nc.vector.tensor_tensor(bs, bs, fti[0:64, :].unsqueeze(2).to_broadcast([64, 8, 64]), ALU.mult))
        bs = heads(fX[64:128, 512:1024])
        step(nc.vector.scalar_tensor_tensor(bs, c("f_bslice")[64:128].unsqueeze(1).to_broadcast([64, 8, 64]), 1.0 / C,
                                            heads(T(0, 3)[64:128, :]), ALU.mult, ALU.add))
        step(nc.vector.tensor_tensor(bs, bs, fti[64:128, :].unsqueeze(2).to_broadcast([64, 8, 64]), ALU.mult))

    def setup3_mixed_dve(v):
        step = setup3_step(v, [14])
        v.wait_ge(f_pe, 2)
        step(nc.vector.tensor_copy(fM, T(1, 0)[0:64, :]))

    def setup3_last_dve(v):
        step = setup3_step(v, [15])
        v.wait_ge(f_pe, 3)
        for s in range(2):
            r = slice(64 * s, 64 * s + 64)
            step(nc.vector.tensor_scalar(fA[r, 512 * s:512 * (s + 1)], T(0, 0)[r, :], 64.0 ** -0.5, None, ALU.mult))
            step(nc.vector.tensor_copy(fB[r, 512 * s:512 * (s + 1)], T(0, 1)[r, :]))
    SETUP3 = 19

    def setup3_first_pe(pe):
        pe.wait_ge(f_dve, 8)
        nc.tensor.matmul(T(0, 0)[0:64, 0:64], c("f_wkT")[0:64], c("f_wqT")[0:64], start=True, stop=True)
        nc.tensor.matmul(T(0, 1)[0:64, :], c("f_wvT")[0:64], c("f_out")[0:64], start=True, stop=True)
        for k in range(8):
            nc.tensor.matmul(T(0, 2)[0:64, 64 * k:64 * k + 64], fXT[:, 64 * k:64 * k + 64], c("f_slice")[0:64], start=True, stop=True)
        for k in range(8):
            m = nc.tensor.matmul(T(0, 3)[64:128, 64 * k:64 * k + 64], fXT[:, 64 * k:64 * k + 64], c("f_slice")[0:64], start=True, stop=True)
        m.then_inc(f_pe, 1)

    def setup3_middle_pe(pe):
        pe.wait_ge(f_dve, 14)
        nc.tensor.matmul(T(1, 0)[0:64, :], fGT, fFT, start=True, stop=True).then_inc(f_pe, 1)

    def setup3_last_pe(pe):
        pe.wait_ge(f_dve, 15)
        for r in (slice(0, 64), slice(64, 128)):
            for k in range(8):
                q = slice(64 * k, 64 * k + 64)
                nc.tensor.matmul(T(0, 0)[r, q], fFT[:, q], fM[:, q], start=True, stop=True)
                m = nc.tensor.matmul(T(0, 1)[r, q], fFT[:, q], fV[:, q], start=True, stop=True)
        m.then_inc(f_pe, 1)

    def job(i, l, d):
        i2, l2 = i + (l + d) // 2, (l + d) % 2
        return i2, l2, i2 * 2 + (l2 + 1)

    def pipelined3(engine, slot):
        for l in range(2):
            slot(0, l)
        for l in range(2):
            slot(1, l)
        with engine.Fori(2, N2 - 1) as i:
            for l in range(2):
                slot(i, l)
        for i in (N2 - 1, N2, N2 + 1):
            for l in range(2):
                slot(i, l)

    def regions():
        return T(0, 2, 2).rearrange("p (b x) -> p b x", b=2)[:, :, 0:384].rearrange("p b (j y) -> p b j y", y=96)

    def stage3_pool(pool, start=None):
        def rows(i, l, n, first=False):
            if not first:
                pool.wait_ge(f_t_r, n - 2)
            nc.gpsimd.tensor_tensor(xs[l].rearrange("p (b c) -> p b c", c=C), xc[:, bass.ds(i * 4 + 2 * l, 2), :],
                                    rstd_of(i * 4 + 2 * l, 2), ALU.mult).then_inc(f_xs_r, 1)

        def rows_plus_1(i, l, n):
            pool.wait_ge(f_xs_r, n)
            pool.wait_ge(f_s_r, n)
            nc.gpsimd.tensor_tensor(f_xs1[l].rearrange("p (s c) -> p s c", s=2)[:, :, 0:64], xs[l].rearrange("p (s c) -> p s c", s=2),
                                    one[:, 0:1].unsqueeze(1).to_broadcast([128, 2, 64]), ALU.add).then_inc(f_xs1_r, 1)

        def weights(i, l, n):
            pool.wait_ge(f_rs_r, n)
            for s in range(2):
                w = f_w[l][:, 512 * s:512 * (s + 1)].rearrange("p (h g) -> p h g", g=64)
                nc.gpsimd.tensor_tensor(w, w, f_rs[l][:, 8 * s:8 * s + 8].unsqueeze(2).to_broadcast([128, 8, 64]), ALU.mult).then_inc(f_w_r, 1)

        def slot(i, l):
            a, b = job(i, l, 1), job(i, l, 2)
            if exists(b[0], 0):
                pool.wait_ge(f_xs1_r, b[2] - 2)
                rows(*b)
            if exists(a[0], 0):
                rows_plus_1(*a)
            if not l and exists(i, -2):
                rsqrt(pool, i * 2 + (LN[2] - 3), i * 4 - 8, 4)
            if l and exists(i, -2):
                rsqrt(pool, i * 2 + (LN[2] - 2), (i - 2) * 4, 4)
                pool.wait_ge(r_res, i - 1)
                hp = part(h, (i - 2) * 4, 4)
                nc.gpsimd.tensor_tensor(hp, hp, c("g_bout").rearrange("p (b c) -> p b c", b=4), ALU.add).then_inc(r_bias, 1)
            if exists(a[0], 0):
                weights(*a)
        if start == 0:
            for l in range(2):
                rows(0, l, l + 1, first=True)
            rows_plus_1(0, 0, 1)
        elif start == 1:
            weights(0, 0, 1)
        else:
            pipelined3(pool, slot)

    def stage3_pe(pe, start=None):
        def rows(i, l, n):
            if not isinstance(n, int) or n > 1:
                pe.wait_ge(f_sub_r, n - 1)
            pe.wait_ge(f_xs_r, n)
            nc.tensor.transpose(T(0, 0)[:, 0:128], xs[l], eye).then_inc(f_t_r, 1)

        def logits(i, l, n, s):
            pe.wait_ge(f_xT_r, n)
            m = nc.tensor.matmul(T(0, s), xT[l], fX[:, 512 * s:512 * (s + 1)], start=True, stop=True)
            if s:
                m.then_inc(f_lg_r, 1)

        def slices(i, l, n):
            pe.wait_ge(f_xs1_r, n)
            if l or exists(i, -1):
                pe.wait_ge(f_vwc_r, n - 1)
            for k in range(8):
                if k % 4 == 0:
                    pe.wait_ge(f_w_r, n * 2 + (k // 4 - 1))
                m = nc.tensor.matmul(regions()[:, k // 4, k % 4, :], f_w[l][:, 128 * k:128 * k + 128],
                                     f_xs1[l][:, 96 * (k // 4):96 * (k // 4) + 96], start=True, stop=True)
            m.then_inc(f_s_r, 1)
            for k in range(8):
                m = nc.tensor.transpose(T(1, k // 4)[:, 128 * (k % 4):128 * (k % 4) + 128], f_w[l][:, 128 * k:128 * k + 128], eye)
            m.then_inc(f_wt_r, 1)

        def tokensT(i, l, n):
            pe.wait_ge(f_tk_r, n)
            pe.wait_ge(f_h_r, n)
            for k in range(4):
                m = nc.tensor.transpose(T(1, 2)[:, 128 * k:128 * k + 128], f_tk[l][:, 128 * k:128 * k + 128], eye)
            m.then_inc(f_tt_r, 1)

        def mixed(i, l, n):
            pe.wait_ge(f_tT_r, n)
            for s in range(2):
                for k in range(8):
                    m = nc.tensor.matmul(T(0, 2)[64 * s:64 * s + 64, 64 * k:64 * k + 64], fA[:, 512 * s + 64 * k:512 * s + 64 * k + 64],
                                         f_tT[l][:, 64 * k:64 * k + 64], start=True, stop=True)
            m.then_inc(f_u_r, 1)
            for s in range(2):
                for k in range(8):
                    o = 64 * (4 * s + k // 2)
                    m = nc.tensor.matmul(T(0, 3)[64 * (k % 2):64 * (k % 2) + 64, o:o + 64], f_tT[l][:, 64 * k:64 * k + 64],
                                         fB[:, 512 * s + 64 * k:512 * s + 64 * k + 64], start=True, stop=True)
            m.then_inc(f_vw_r, 1)

        def pairs(i, l, n):
            pe.wait_ge(f_uz0_r, n)
            pe.wait_ge(f_uz1_r, n)
            for s in range(2):
                for k in range(8):
                    o = 64 * (4 * s + k // 2)
                    m = nc.tensor.matmul(T(1, 3)[64 * (k % 2):64 * (k % 2) + 64, o:o + 64],
                                         f_uz[l][:, 512 * s + 64 * k:512 * s + 64 * k + 64], f_tT[l][:, 64 * k:64 * k + 64], start=True, stop=True)
            m.then_inc(f_l_r, 1)

        def attended(i, l, n):
            pe.wait_ge(f_eb_r, n)
            for k in range(8):
                m = nc.tensor.matmul(T(1, k // 4)[:, 128 * (k % 4):128 * (k % 4) + 128], f_ebd[l][:, 128 * k:128 * k + 128],
                                     f_wT[l][:, 128 * k:128 * k + 128], start=True, stop=True)
            m.then_inc(f_y_r, 1)

        def outT(i, l, n):
            pe.wait_ge(f_ya_r, n)
            pe.wait_ge(f_yv_r, n)
            for s in range(2):
                for j in range(4):
                    k = 4 * s + j
                    m = nc.tensor.matmul(T(1, 2)[64 * s:64 * s + 64, 0:128], f_vw[l][:, 64 * k:64 * k + 64],
                                         f_y[l][:, 128 * k:128 * k + 128], start=(j == 0), stop=(j == 3))
            m.then_inc(f_o_r, 1)

        def out(i, l, n):
            pe.wait_ge(f_oT_r, n)
            nc.tensor.transpose(T(1, 2)[:, 128:256], f_oT[l], eye).then_inc(f_ot_r, 1)

        def slot(i, l):
            z, a, b, y, x = job(i, l, 0), job(i, l, 1), job(i, l, 2), job(i, l, -1), job(i, l, -2)
            if exists(z[0], 0):
                slices(*z)
            if exists(x[0], 0):
                out(*x)
            if exists(a[0], 0):
                logits(*a, 0)
            if exists(z[0], 0):
                tokensT(*z)
            if exists(a[0], 0):
                logits(*a, 1)
            if exists(z[0], 0):
                mixed(*z)
                pe.wait_ge(f_wT_r, z[2])
            if exists(y[0], 0):
                attended(*y)
            if exists(z[0], 0):
                pairs(*z)
            if exists(y[0], 0):
                outT(*y)
            if exists(b[0], 0):
                rows(*b)
        if start == 0:
            rows(0, 0, 1)
        elif start == 1:
            logits(0, 0, 1, 0)
            logits(0, 0, 1, 1)
        else:
            rows(0, 1, 2)
            pipelined3(pe, slot)

    def stage3_act(act, start=None):
        def rowsT(i, l, n):
            act.wait_ge(f_t_r, n)
            nc.scalar.activation(xT[l], T(0, 0)[:, 0:128], ACT.Identity, bias=one[:, 0:1]).then_inc(f_xT_r, 1)

        def exp(i, l, n):
            act.wait_ge(f_sub_r, n)
            nc.scalar.activation(f_w[l], f_w[l], ACT.Exp).then_inc(f_exp_r, 1)

        def slot(i, l):
            (zi, zl, z), a, b, (yi, yl, y) = job(i, l, 0), job(i, l, 1), job(i, l, 2), job(i, l, -1)
            if exists(yi, 0):
                act.wait_ge(f_ls_r, y)
                nc.scalar.activation(f_le[yl], f_le[yl], ACT.Exp).then_inc(f_e_r, 1)
            if not l and exists(i, -2):
                square(act, i * 2 + (LN[2] - 3), i * 4 - 8, 4, 0)
            if l and exists(i, -2):
                square(act, i * 2 + (LN[2] - 2), (i - 2) * 4, 4, 1)
            if exists(zi, 0):
                act.wait_ge(f_wt_r, z)
                nc.scalar.copy(f_wT[zl], T(1, 0, 2)).then_inc(f_wT_r, 1)
                act.wait_ge(f_tt_r, z)
                nc.scalar.copy(f_tT[zl], T(1, 2)).then_inc(f_tT_r, 1)
                act.wait_ge(f_u_r, z)
                nc.scalar.copy(f_uz[zl][0:64, 0:512], T(0, 2)[0:64, :]).then_inc(f_uz0_r, 1)
            if exists(a[0], 0):
                exp(*a)
            if exists(zi, 0):
                act.wait_ge(f_vw_r, z)
                nc.scalar.copy(f_vw[zl], T(0, 3)).then_inc(f_vwc_r, 1)
            if exists(yi, 0):
                act.wait_ge(f_y_r, y)
                nc.scalar.copy(f_y[yl][:, 0:512], T(1, 0)).then_inc(f_ya_r, 1)
            if exists(yi, 0):
                act.wait_ge(f_o_r, y)
                nc.scalar.activation(f_oT[yl], T(1, 2)[:, 0:128], ACT.Identity, bias=c("f_bout")).then_inc(f_oT_r, 1)
            if exists(b[0], 0):
                rowsT(*b)
        if start == 0:
            rowsT(0, 0, 1)
        elif start == 1:
            exp(0, 0, 1)
        else:
            rowsT(0, 1, 2)
            pipelined3(act, slot)

    def stage3_dve(v, start=None):
        def shifted(i, l, n):
            v.wait_ge(f_lg_r, n)
            lg = T(0, 0, 2).rearrange("p (h g) -> p h g", g=64)
            nc.vector.tensor_reduce(f_mx[l], lg, X, ALU.max).then_inc(f_mx_r, 1)
            v.wait_ge(f_mx_r, n)
            nc.vector.tensor_tensor(f_w[l].rearrange("p (h g) -> p h g", g=64), lg, f_mx[l].unsqueeze(2).to_broadcast([128, 16, 64]),
                                    ALU.subtract).then_inc(f_sub_r, 1)

        def rsum(i, l, n):
            v.wait_ge(f_exp_r, n)
            nc.vector.tensor_reduce(f_rs[l], f_w[l].rearrange("p (h g) -> p h g", g=64), X, ALU.add).then_inc(f_sum_r, 1)

        def rrsum(i, l, n):
            v.wait_ge(f_sum_r, n)
            nc.vector.reciprocal(f_rs[l], f_rs[l]).then_inc(f_rs_r, 1)

        def tokens(i, l, n):
            v.wait_ge(f_s_r, n + 2)
            nr = f_nr[l].rearrange("p (s j) -> p s j", s=2)
            nc.vector.tensor_scalar(nr, regions()[:, :, :, 64], 1e-5, None, ALU.add).then_inc(f_nr_r, 1)
            v.wait_ge(f_nr_r, n)
            nc.vector.reciprocal(f_nr[l], f_nr[l]).then_inc(f_nr2_r, 1)
            v.wait_ge(f_nr2_r, n)
            nc.vector.tensor_tensor(f_tk[l].rearrange("p (j s c) -> p s j c", j=4, s=2), regions()[:, :, :, 0:64],
                                    nr.unsqueeze(3).to_broadcast([128, 2, 4, 64]), ALU.mult).then_inc(f_tk_r, 1)

        def pairs_shifted(i, l, n):
            v.wait_ge(f_l_r, n)
            pairs = T(1, 3).rearrange("p (k c) -> p k c", c=64)
            nc.vector.tensor_reduce(f_lmx[l], pairs, X, ALU.max).then_inc(f_lmx_r, 1)
            v.wait_ge(f_lmx_r, n)
            nc.vector.tensor_tensor(f_le[l].rearrange("p (k c) -> p k c", c=64), pairs,
                                    f_lmx[l].unsqueeze(2).to_broadcast([128, 8, 64]), ALU.subtract).then_inc(f_ls_r, 1)

        def pairs_scaled(i, l, n):
            e = f_le[l].rearrange("p (k c) -> p k c", c=64)
            v.wait_ge(f_e_r, n)
            nc.vector.tensor_reduce(f_zr[l], e, X, ALU.add).then_inc(f_es_r, 1)
            v.wait_ge(f_es_r, n)
            nc.vector.reciprocal(f_zr[l], f_zr[l]).then_inc(f_er_r, 1)
            v.wait_ge(f_er_r, n)
            for r in (slice(0, 64), slice(64, 128)):
                m = nc.vector.tensor_tensor(f_ebd[l][r, :].rearrange("p (k y) -> p k y", y=128)[:, :, r], e[r],
                                            f_zr[l][r, :].unsqueeze(2).to_broadcast([64, 8, 64]), ALU.mult)
            m.then_inc(f_eb_r, 1)

        def slot(i, l):
            z, a, y, (xi, xl, x) = job(i, l, 0), job(i, l, 1), job(i, l, -1), job(i, l, -2)
            if exists(y[0], 0):
                pairs_shifted(*y)
            if exists(z[0], 0):
                tokens(*z)
            if exists(xi, 0):
                v.wait_ge(f_ot_r, x)
                hp = h[:, bass.ds(xi * 4 + 2 * xl, 2), :]
                nc.vector.tensor_tensor(hp, hp, T(1, 2)[:, 128:256].rearrange("p (b c) -> p b c", c=C), ALU.add).then_inc(f_h_r, 1)
            if exists(y[0], 0):
                pairs_scaled(*y)
            if exists(a[0], 0):
                shifted(*a)
            if exists(z[0], 0):
                v.wait_ge(f_u_r, z[2])
                nc.vector.tensor_copy(f_uz[z[1]][64:128, 512:1024], T(0, 2)[64:128, :]).then_inc(f_uz1_r, 1)
            if not l and exists(i, -2):
                variance(v, i * 2 + (LN[2] - 3), i * 4 - 8, 4, 0)
            if l and exists(i, -2):
                variance(v, i * 2 + (LN[2] - 2), (i - 2) * 4, 4, 1)
            if exists(a[0], 0):
                rsum(*a)
            if exists(y[0], 0):
                v.wait_ge(f_y_r, y[2])
                nc.vector.tensor_copy(f_y[y[1]][:, 512:1024], T(1, 1)).then_inc(f_yv_r, 1)
            if exists(a[0], 0):
                rrsum(*a)
            if not l and exists(i, -2):
                v.wait_ge(ln_rstd, i * 2 + (LN[2] - 3))
                first = i * 4 - 8
                nc.vector.tensor_tensor(part(xc, first, 4), part(xc, first, 4), rstd_of(first, 4), ALU.mult).then_inc(r_x1, 1)
                v.wait_ge(r_x1, i - 1)
                nc.vector.tensor_tensor(part(h, first, 4), part(h, first, 4), part(xc, first, 4), ALU.add).then_inc(r_res, 1)
                centre(v, i * 2 + (LN[2] - 2), first, 4, xc)
            if l and exists(i, -1):
                v.wait_ge(f_h_r, i * 2 + 2)
                centre(v, i * 2 + (LN[2] - 1), i * 4 - 4, 4, h)
        if start == 0:
            shifted(0, 0, 1)
        elif start == 1:
            rsum(0, 0, 1)
            rrsum(0, 0, 1)
        else:
            pipelined3(v, slot)

    xg = big1[:, :].rearrange("p (t b) -> p t b", b=B)
    ys = big2[:, :].rearrange("p (t b) -> p t b", b=B)
    r_x1, r_res, r_bias = sem("4_normed"), sem("4_residual"), sem("6_bias_added")
    r_dup, r_t, r_xgf, r_xgr = sem("4_rows"), sem("4_rowsT"), sem("4_forward"), sem("4_reverse")
    r_rows = [squares[k][:, 0:256].rearrange("p (b c) -> p b c", b=4) for k in range(2)]
    NJ4 = B // 4

    def stage4_pool(pool):
        with pool.Fori(0, NJ4 // 2) as i:
            for l in range(2):
                n = i * 2 + (l + 1)
                pool.wait_ge(r_t, n)
                nc.gpsimd.tensor_tensor(r_rows[l], xc[:, bass.ds(i * 8 + 4 * l, 4), :], rstd_of(i * 8 + 4 * l, 4), ALU.mult).then_inc(r_dup, 1)

    def stage4_pe(pe):
        with pe.Fori(0, NJ4 // 2) as i:
            for l in range(2):
                n = i * 2 + (l + 1)
                pe.wait_ge(r_dup, n)
                pe.wait_ge(r_xgf, n)
                pe.wait_ge(r_xgr, n)
                for b in range(4):
                    for d in range(2):
                        to = T(l, 0)[64 * d:64 * d + 64, 128 * b:128 * b + 128]
                        if b == 0 or d:
                            m = nc.tensor.matmul(to, r_rows[l][:, b, :], eye, start=True, stop=True)
                        else:
                            nc.tensor.transpose(to, r_rows[l][:, b, :], eye)
                m.then_inc(r_t, 1)

    def stage4_act(act):
        with act.Fori(0, NJ4 // 2) as i:
            for l in range(2):
                act.wait_ge(r_t, i * 2 + (l + 3))
                nc.scalar.activation(xg[0:64, :, bass.ds(i * 8 + 4 * l, 4)].rearrange("p t b -> p b t"),
                                     T(l, 0)[0:64, :].rearrange("p (b t) -> p b t", b=4), ACT.Identity,
                                     bias=c("g_lnb")[0:64], scale=c("g_lng")[0:64]).then_inc(r_xgf, 1)

    def stage4_dve(v):
        with v.Fori(0, NJ4 // 2) as i:
            for l in range(2):
                v.wait_ge(r_t, i * 2 + (l + 3))
                nc.vector.tensor_scalar(xg[64:128, :, bass.ds(i * 8 + 4 * l, 4)].rearrange("p t b -> p b t"),
                                        T(l, 0)[64:128, :].rearrange("p (b t) -> p b t", b=4)[:, :, ::-1],
                                        c("g_lng")[64:128], c("g_lnb")[64:128], ALU.mult, ALU.add).then_inc(r_xgr, 1)

    UN = 16
    g_bias, g_nbz = sb("g_bias", [128, 3]), sb("g_nbz", [128, 1])
    g_set, g_r, g_z, g_omz, g_t, g_t2, g_n, g_a, g_b, g_hs = (
        [sb(f"g_{n}{u}", [128, B]) for u in range(2)] for n in ("set", "r", "z", "omz", "t", "t2", "n", "a", "b", "h"))
    (g_setup, g_rp, g_hp, g_zp, g_rr, g_zr, g_tr, g_t2r, g_nr, g_ar, g_br, g_hr, g_yr) = (sem("5_" + n) for n in (
        "setup", "r_sum", "hn_sum", "z_sum", "r", "z", "gated", "n_sum", "n", "a", "b", "h", "stored"))

    GS = 8

    def gru_x(gate, half, group, first):
        w = 64 * GS // 2
        nc.tensor.matmul(T(group, gate)[:, w * half:w * (half + 1)], c("g_ih", 128 * gate, 128 * gate + 128),
                         big1[:, bass.ds(first * B + w * half, w)], start=(half == 0), stop=True, skip_group_check=True)

    def gru_products(to, gate, state, start):
        for d in range(2):
            m = nc.tensor.matmul(to[64 * d:64 * d + 64, :], c("g_hh", 128 * gate + 64 * d, 128 * gate + 64 * d + 64), state[:, :],
                                 start=start, stop=True, skip_group_check=True)
        return m

    def gru_pe(pe):
        def steps(i, last):
            for st in range(UN):
                u, group, col = st % 2, st // GS, B * (st % GS)
                n = i * UN + st
                R, Z = (T(group, k)[:, col:col + B] for k in range(2))
                HN = T(u, 3)[:, 0:B]
                pe.wait_ge(g_br, n + 1)
                gru_products(R, 0, g_b[1 - u], False)
                gru_products(HN, 2, g_b[1 - u], True)
                pe.wait_ge(g_ar, n + 1)
                gru_products(R, 0, g_a[1 - u], False).then_inc(g_rp, 1)
                gru_products(HN, 2, g_a[1 - u], False).then_inc(g_hp, 1)
                pe.wait_ge(g_hr, n + 1)
                gru_products(Z, 1, g_hs[1 - u], False).then_inc(g_zp, 1)
                more = st % GS < 6 and not (last and group == 1)
                if more:
                    gru_x(st % GS // 2, st % 2, 1 - group, i * UN + GS * (group + 1))
                nc.tensor.matmul(T(1 - u, 3)[:, 128:384 if more else 512], c("g_hh", 0, 128), c("m_w1", 0, 256 if more else 384),
                                 start=True, stop=True, skip_group_check=True)
        for gate in range(3):
            for half in range(2):
                gru_x(gate, half, 0, 0)
        with pe.Fori(0, L // UN - 1) as i:
            steps(i, False)
        steps(L // UN - 1, True)

    def gru_act(act):
        with act.Fori(0, L // UN) as i:
            for st in range(UN):
                u, n = st % 2, i * UN + (st + 1)
                group, col = st // GS, B * (st % GS)
                act.wait_ge(g_rp, n)
                nc.scalar.activation(g_r[u][:, :], T(group, 0)[:, col:col + B], ACT.Sigmoid, bias=g_bias[:, 0:1]).then_inc(g_rr, 1)
                act.wait_ge(g_zp, n)
                nc.scalar.activation(g_z[u][:, :], T(group, 1)[:, col:col + B], ACT.Sigmoid, bias=g_bias[:, 1:2])
                nc.scalar.activation(g_omz[u][:, :], T(group, 1)[:, col:col + B], ACT.Sigmoid, bias=g_nbz[:, 0:1], scale=-1.0).then_inc(g_zr, 1)
                act.wait_ge(g_t2r, n)
                nc.scalar.activation(g_n[u][:, :], g_t2[u][:, :], ACT.Tanh, bias=c("g_bih", 2, 3)).then_inc(g_nr, 1)

    def gru_dve(v):
        with v.Fori(0, L // UN) as i:
            for st in range(UN):
                u, n = st % 2, i * UN + (st + 1)
                group, col = st // GS, B * (st % GS)
                v.wait_ge(g_hp, n)
                v.wait_ge(g_rr, n)
                nc.vector.scalar_tensor_tensor(g_t[u][:, :], T(u, 3)[:, 0:B], c("g_bhh", 2, 3), g_r[u][:, :], ALU.add, ALU.mult).then_inc(g_tr, 1)
                v.wait_ge(g_tr, n)
                nc.vector.tensor_tensor(g_t2[u][:, :], T(group, 2)[:, col:col + B], g_t[u][:, :], ALU.add).then_inc(g_t2r, 1)
                v.wait_ge(g_zr, n)
                v.wait_ge(g_hr, n)
                v.wait_ge(g_yr, n)
                nc.vector.tensor_tensor(g_b[u][:, :], g_z[u][:, :], g_hs[1 - u][:, :], ALU.mult).then_inc(g_br, 1)
                v.wait_ge(g_nr, n)
                nc.vector.tensor_tensor(g_a[u][:, :], g_omz[u][:, :], g_n[u][:, :], ALU.mult).then_inc(g_ar, 1)
                v.wait_ge(g_ar, n + 1)
                nc.vector.tensor_tensor(g_hs[u][:, :], g_a[u][:, :], g_b[u][:, :], ALU.add).then_inc(g_hr, 1)

    def gru_pool(pool):
        with pool.Fori(0, L // UN) as i:
            for st in range(UN):
                u = st % 2
                t = i * UN + st
                pool.wait_ge(g_ar, t + 2)
                nc.gpsimd.tensor_tensor(big2[0:64, bass.ds(t * B, B)], g_a[u][0:64, :], g_b[u][0:64, :], ALU.add)
                nc.gpsimd.tensor_tensor(big2[64:128, bass.ds((i * (-UN) + (L - 1 - st)) * B, B)], g_a[u][64:128, :], g_b[u][64:128, :],
                                        ALU.add).then_inc(g_yr, 1)

    gg = [big1[0:64, 512 * l:512 * (l + 1)] for l in range(2)]
    cb = [big1[:, 1024 + 512 * l:1024 + 512 * (l + 1)] for l in range(2)]
    o_p, o_g, o_c, o_r, o_o, o_h = (sem("6_" + n) for n in ("products", "gate", "gated", "reverse", "projected", "h_written"))

    gate_diff = cst[:, AT["g_gate"][0]:AT["g_gate"][0] + 128]

    N6 = NJ4 // 4

    def pipelined6(engine, slot):
        for q in range(4):
            slot(0, q)
        with engine.Fori(1, N6 - 1) as i:
            for q in range(4):
                slot(i, q)
        for q in range(4):
            slot(N6 - 1, q)
        for q in range(2):
            slot(N6, q)

    def stage6_pe(pe):
        def products(i, q):
            nc.tensor.matmul(T(q // 2, q % 2), gate_diff, ys[:, :, bass.ds(i * 16 + 4 * q, 4)].rearrange("p t b -> p b t"),
                             start=True, stop=True).then_inc(o_p, 1)

        def slot(i, q):
            if q < 2 and there(i, N6):
                products(i, q + 2)
            elif q >= 2 and there(i if not isinstance(i, int) else i + 1, N6):
                products(i + 1, q - 2)
            if there(i, N6):
                n, l = i * 4 + (q + 1), q % 2
                pe.wait_ge(o_h, n)
                pe.wait_ge(o_r, n)
                pe.wait_ge(o_c, n + 2)
                for b in range(4):
                    m = nc.tensor.matmul(T(l, 2)[:, 64 * b:64 * b + 64], cb[l][:, 128 * b:128 * b + 128], c("g_out"), start=True, stop=True)
                m.then_inc(o_o, 1)
        products(0, 0)
        products(0, 1)
        pipelined6(pe, slot)

    def stage6_act(act):
        def slot(i, q):
            if there(i, N6):
                n, l = i * 4 + (q + 1), q % 2
                act.wait_ge(o_p, n)
                act.wait_ge(o_c, n)
                nc.scalar.activation(gg[l], T(q // 2, q % 2)[0:64, :], ACT.Sigmoid, bias=c("g_bgate")[0:64]).then_inc(o_g, 1)
                act.wait_ge(o_o, n)
                nc.scalar.activation(cb[l][64:128, :].rearrange("p (b t) -> p b t", b=4),
                                     ys[64:128, :, bass.ds(i * 16 + 4 * q, 4)].rearrange("p t b -> p b t"), ACT.Identity).then_inc(o_r, 1)
            if q == 1 and there(i if not isinstance(i, int) else i - 1, N6):
                square(act, i * 2 + LN[3], i * 16 - 8, 8, 1)
            if q == 3 and there(i, N6):
                square(act, i * 2 + (LN[3] + 1), i * 16, 8, 0)
        pipelined6(act, slot)

    def stage6_dve(v):
        def slot(i, q):
            before = there(i if not isinstance(i, int) else i - 1, N6)
            if there(i, N6):
                n, l = i * 4 + (q + 1), q % 2
                v.wait_ge(o_o, n)
                v.wait_ge(o_g, n)
                nc.vector.tensor_tensor(cb[l][0:64, :], T(q // 2, q % 2)[64:128, :], gg[l], ALU.mult).then_inc(o_c, 1)
            if (q and there(i, N6)) or (q == 0 and before):
                v.wait_ge(o_o, i * 4 + (q + 2))
                hp = h[:, bass.ds(i * 16 + (4 * q - 4), 4), :]
                nc.vector.tensor_tensor(hp, hp, T((q + 1) % 2, 2)[:, 0:256].rearrange("p (b c) -> p b c", c=C), ALU.add).then_inc(o_h, 1)
            if q == 0 and before:
                v.wait_ge(o_h, i * 4 + 2)
                centre(v, i * 2 + LN[3], i * 16 - 8, 8, h)
            if q == 2 and there(i, N6):
                v.wait_ge(o_h, i * 4 + 4)
                centre(v, i * 2 + (LN[3] + 1), i * 16, 8, h)
            if q == 1 and before:
                variance(v, i * 2 + LN[3], i * 16 - 8, 8, 1)
            if q == 3 and there(i, N6):
                variance(v, i * 2 + (LN[3] + 1), i * 16, 8, 0)
        pipelined6(v, slot)

    NJ7 = B // 8
    m_xs = [big1[:, 6144 + 512 * k:6144 + 512 * (k + 1)] for k in range(2)]
    m_xT = [big1[:, 7168 + 512 * k:7168 + 512 * (k + 1)] for k in range(2)]
    m_y = [big1[:, 2048 + 512 * k:2048 + 512 * (k + 1)] for k in range(2)]
    m_red = [big1[:, 3072 + 512 * k:3072 + 512 * (k + 1)] for k in range(2)]
    hid = [big2[:, 4096 * k:4096 * (k + 1)] for k in range(2)]

    def small(at, cols):
        return [big1[:, 4096 + 1024 * k + at:4096 + 1024 * k + at + cols] for k in range(2)]
    m_lg, m_m8, m_i8 = small(0, 64), small(64, 64), small(128, 64)
    m_if, m_d, m_w1, m_w2 = small(192, 16), small(208, 8), small(216, 8), small(224, 8)
    m_e1, m_e2, m_c1, m_c2, m_comb = small(256, 64), small(320, 64), small(384, 64), small(448, 64), small(512, 64)
    (m_xs_r, m_t_r, m_xT_r, m_lg_r, m_d_r, m_ex_r, m_comb_r, m_step, m_hp, m_ra, m_yp, m_add, m_mul, m_rd, m_h_r) = (
        sem("7_" + n) for n in ("rows", "rowsT", "rowsT_copied", "gate_logits", "top_diff", "top_exp", "combine", "gate_steps", "hidden",
                                "relu", "expert_out", "biased", "weighted", "reduced", "h_written"))
    STEPS7 = 27

    def hidden_bank(e):
        return (T(1, 0), T(1, 1), T(0, 2), T(0, 3))[e % 4]

    def jobs7(engine, job):
        with engine.Fori(0, NJ7 // 2 - 1) as i:
            for l in range(2):
                job(i, l, True)
        for l in range(2):
            job(NJ7 // 2 - 1, l, l == 0)

    def stage7_pool(pool, start=False):
        def rows(i, l):
            pool.wait_ge(m_t_r, i * 2 + (l + 1))
            nc.gpsimd.tensor_tensor(m_xs[l].rearrange("p (b c) -> p b c", c=C), xc[:, bass.ds(i * 16 + 8 * l, 8), :],
                                    rstd_of(i * 16 + 8 * l, 8), ALU.mult).then_inc(m_xs_r, 1)

        def job(i, l, more):
            J = i * 2 + l
            if more:
                rows(i + l, 1 - l)
            pool.wait_ge(m_comb_r, J + 1)
            for s in range(2):
                for p in range(4):
                    pool.wait_ge(m_add, J * 8 + (4 * s + p + 3))
                    y = m_y[p % 2].rearrange("p (e c) -> p e c", e=8)
                    nc.gpsimd.tensor_tensor(y, y, m_comb[l][:, 8 * (2 * p + s):8 * (2 * p + s) + 8].unsqueeze(2).to_broadcast([128, 8, C]),
                                            ALU.mult).then_inc(m_mul, 1)
        if start:
            rows(0, 0)
        else:
            jobs7(pool, job)

    def stage7_pe(pe):
        def rows(i, l):
            pe.wait_ge(m_xs_r, i * 2 + (l + 1))
            for p in range(4):
                m = nc.tensor.transpose(T(0, 0)[:, 128 * p:128 * p + 128], m_xs[l][:, 128 * p:128 * p + 128], eye)
            m.then_inc(m_t_r, 1)

        def gate(i, l):
            pe.wait_ge(m_xT_r, i * 2 + (l + 1))
            for p in range(4):
                m = nc.tensor.matmul(T(0, 1)[:, 16 * p:16 * p + 16], m_xT[l][:, 128 * p:128 * p + 128], c("m_g"), start=True, stop=True)
            m.then_inc(m_lg_r, 1)

        def job(i, l, more):
            J = i * 2 + l
            for s in range(2):
                for e in range(8):
                    pe.wait_ge(m_ra, J * 16 + (8 * s + e + 1))
                    if s == 0 and e == 0:
                        pe.wait_ge(m_add, J * 8 + 1)
                    nc.tensor.matmul(hidden_bank(e), c("m_w1", 128 * (8 * s + e), 128 * (8 * s + e + 1)), m_xT[l],
                                     start=True, stop=True).then_inc(m_hp, 1)
            if more:
                rows(i + l, 1 - l)
            for s in range(2):
                pe.wait_ge(m_ra, J * 16 + (18 + 2 * s))
                for p in range(4):
                    pe.wait_ge(m_add, J * 8 + (4 * s + p + 1))
                    for e in range(8):
                        o = 512 * (2 * (p % 2) + e // 4) + 96 * (e % 4)
                        m = nc.tensor.matmul(pt[1][:, o:o + 96], hid[s][:, 512 * e + 128 * p:512 * e + 128 * p + 128],
                                             c("m_w2", 64 * e, 64 * e + 96), start=True, stop=True)
                    m.then_inc(m_yp, 1)
                if more and s == 0:
                    pe.wait_ge(m_comb_r, J + 1)
                    gate(i + l, 1 - l)
        rows(0, 0)
        gate(0, 0)
        pe.wait_ge(o_h, NJ4 + 2)
        jobs7(pe, job)

    def stage7_act(act):
        def rowsT(i, l):
            act.wait_ge(m_t_r, i * 2 + (l + 3))
            nc.scalar.copy(m_xT[l], T(0, 0)).then_inc(m_xT_r, 1)

        def job(i, l, more):
            J = i * 2 + l
            for s in range(2):
                act.wait_ge(m_yp, J * 8 + (4 * s + 4))
                for e in range(8):
                    act.wait_ge(m_hp, J * 16 + (8 * s + e + 1))
                    nc.scalar.activation(hid[s][:, 512 * e:512 * (e + 1)], hidden_bank(e), ACT.Relu, bias=c("m_b1", e, e + 1)).then_inc(m_ra, 1)
                if s == 0:
                    act.wait_ge(m_d_r, J + 1)
                    nc.scalar.activation(m_d[l], m_d[l], ACT.Exp).then_inc(m_ex_r, 1)
            if more:
                rowsT(i + l, 1 - l)
        rowsT(0, 0)
        jobs7(act, job)

    def stage7_dve(v):
        def reduce(i, l, s, p):
            v.wait_ge(m_mul, (i * 2 + l) * 8 + (4 * s + p + 1))
            b = 2 * p + s
            nc.vector.tensor_reduce(m_red[l][:, 64 * b:64 * b + 64], m_y[p % 2].rearrange("p (e c) -> p c e", e=8), X, ALU.add).then_inc(m_rd, 1)
        with v.Fori(0, NJ7 // 2) as i:
            for l in range(2):
                J = i * 2 + l
                k = [0]

                def step(ins, ordered=True):
                    k[0] += 1
                    ins.then_inc(m_step, 1)
                    if ordered:
                        v.wait_ge(m_step, J * STEPS7 + k[0])
                v.wait_ge(m_lg_r, J + 1)
                step(nc.vector.tensor_tensor(m_lg[l], T(0, 1)[:, 0:64], m_bg[:, :], ALU.add))
                step(nc.vector.memset(spare[:, 30:31], 0.0), ordered=False)
                for b in range(8):
                    step(nc.vector.max(m_m8[l][:, 8 * b:8 * b + 8], m_lg[l][:, 8 * b:8 * b + 8]), ordered=(b == 7))
                step(nc.vector.memset(spare[:, 31:32], 0.0), ordered=False)
                for b in range(8):
                    step(nc.vector.max_index(m_i8[l][:, 8 * b:8 * b + 8].bitcast(U32), m_m8[l][:, 8 * b:8 * b + 8],
                                             m_lg[l][:, 8 * b:8 * b + 8]), ordered=(b == 7))
                top = m_m8[l].rearrange("p (b k) -> p b k", k=8)
                nc.vector.tensor_tensor(m_d[l], top[:, :, 1], top[:, :, 0], ALU.subtract).then_inc(m_d_r, 1)
                step(nc.vector.tensor_copy(m_if[l].rearrange("p (b k) -> p b k", k=2),
                                           m_i8[l].bitcast(U32).rearrange("p (b k) -> p b k", k=8)[:, :, 0:2]))
                which = m_if[l].rearrange("p (b k) -> p b k", k=2)
                iota = c("iota").unsqueeze(1).to_broadcast([128, 8, 8])

                def e8(t):
                    return t.rearrange("p (b e) -> p b e", e=8)
                step(nc.vector.tensor_tensor(e8(m_e1[l]), iota, which[:, :, 0:1].to_broadcast([128, 8, 8]), ALU.is_equal), ordered=False)
                step(nc.vector.tensor_tensor(e8(m_e2[l]), iota, which[:, :, 1:2].to_broadcast([128, 8, 8]), ALU.is_equal))
                v.wait_ge(m_ex_r, J + 1)
                step(nc.vector.tensor_scalar(m_w1[l], m_d[l], 1.0, None, ALU.add))
                step(nc.vector.reciprocal(m_w1[l], m_w1[l]))
                step(nc.vector.tensor_tensor(m_w2[l], m_d[l], m_w1[l], ALU.mult), ordered=False)
                step(nc.vector.tensor_tensor(e8(m_c1[l]), e8(m_e1[l]), m_w1[l].unsqueeze(2).to_broadcast([128, 8, 8]), ALU.mult))
                step(nc.vector.tensor_tensor(e8(m_c2[l]), e8(m_e2[l]), m_w2[l].unsqueeze(2).to_broadcast([128, 8, 8]), ALU.mult))
                nc.vector.tensor_tensor(m_comb[l], m_c1[l], m_c2[l], ALU.add).then_inc(m_comb_r, 1)
                assert k[0] == 19 + 8, k[0]
                for s in range(2):
                    for p in range(4):
                        v.wait_ge(m_yp, J * 8 + (4 * s + p + 9))
                        v.wait_ge(m_rd, J * 8 + (4 * s + p + 1))
                        y = pt[1][:, 1024 * (p % 2):1024 * (p % 2) + 1024].rearrange("p (b x) -> p b x", b=2)[:, :, 0:384]
                        nc.vector.tensor_tensor(m_y[p % 2].rearrange("p (b j c) -> p b j c", b=2, j=4),
                                                y.rearrange("p b (j y) -> p b j y", y=96)[:, :, :, 0:64],
                                                c("m_b2").rearrange("p (b j c) -> p b j c", b=2, j=4), ALU.add).then_inc(m_add, 1)
                        if p:
                            reduce(i, l, s, p - 1)
                    reduce(i, l, s, 3)
                v.wait_ge(m_rd, J * 8 + 10)
                hp = h[:, bass.ds(i * 16 + 8 * l, 8), :]
                nc.vector.tensor_tensor(hp, hp, m_red[l].rearrange("p (b c) -> p b c", c=C), ALU.add).then_inc(m_h_r, 1)

    m_bg, m_bg_r = sb("m_bgs", [128, 64]), sem("7_gate_bias")

    with nc.Block() as block:
        @block.sync
        def _(sp):
            front = AT["eye"][0]
            sp.dma_start(cst[:, 0:front], consts[:, 0:front]).then_inc(conv_loaded, 16)
            for i in range(JA // 2):
                if i >= 2:
                    sp.wait_ge(c1_max, 8 * (i - 1) + 2)
                for t in range(3):
                    sp.dma_start(xin[i % 2][32 * t:32 * (t + 1), :], xp[i, :, t:t + LEN]).then_inc(x_loaded[i % 2], 16)
                if i == 1:
                    sp.dma_start(cst[:, front:WIDTH], consts[:, front:WIDTH]).then_inc(loaded, 16)
            with sp.Fori(0, NJ7) as j:
                sp.wait_ge(m_h_r, j + 1)
                sp.dma_start(out[bass.ds(j * 8, 8), :, :].rearrange("b l c -> l b c"), h[:, bass.ds(j * 8, 8), :]).then_inc(stored, 16)
            sp.wait_ge(stored, 16 * NJ7)

        @block.gpsimd
        def _(pool):
            nc.gpsimd.memset(half_neg[:, :], -0.5)
            nc.gpsimd.memset(eps[:, :], EPS).then_inc(bn_var, 1)
            nc.gpsimd.memset(one[:, :], 1.0).then_inc(one_set, 1)
            pool.wait_ge(conv_loaded, 16)
            nc.gpsimd.tensor_scalar(bn_s[:, :], c("bn_v"), EPS, None, ALU.add).then_inc(bn_var, 1)
            pool.wait_ge(bn_var, 2)
            for a, b in ((0, 16), (80, 83), (16, 80)):
                nc.gpsimd.tensor_tensor(bn_s[:, a:b], bn_s[:, a:b], half_neg[:, 0:1].to_broadcast([128, b - a]), ALU.pow).then_inc(bn_rs, 1)
            for t in (fA, fB, fX):
                nc.gpsimd.memset(t[:, :], 0.0).then_inc(f_zero, 1)
            stage1b_pool(pool)
            pool.wait_ge(ln_rstd, LN[1])
            stage2_pool(pool)
            pool.wait_ge(ln_rstd, LN[2])
            pool.wait_ge(f_still, 6)
            stage3_pool(pool)
            pool.wait_ge(ln_rstd, LN[3])
            stage4_pool(pool)
            pool.wait_ge(f_h_r, NP + 2)
            gru_pool(pool)
            rsqrt(pool, LN[3] + 1, 0, 8)
            pool.wait_ge(ln_rstd, LN[3] + 1)
            stage7_pool(pool, start=True)
            with pool.Fori(1, NJ4 // 2) as i:
                rsqrt(pool, i + (LN[3] + 1), i * 8, 8)
            pool.wait_ge(ln_rstd, LN[4])
            stage7_pool(pool)

        @block.vector
        def _(v):
            nc.vector.memset(taps[0:32, :, 0:1], 0.0).then_inc(pads_zero, 1)
            nc.vector.memset(taps[64:96, :, 511:512], 0.0).then_inc(pads_zero, 1)
            for k, (credited, n) in enumerate(((c1_max, 2), (c2_max, 4), (h1_ready, 8), (h2_ready, 2), (b_h3, 1), (b_h, 1), (ln_var, 2), (a_h_r, 3), (a_oT_r, 3), (f_h_r, 2), (f_s_r, 2),
                                               (r_t, 2), (r_xgf, 2), (r_xgr, 2), (g_yr, 2), (o_h, 2), (o_c, 2), (o_o, 2), (m_t_r, 2), (m_ra, 4),
                                               (m_add, 2), (m_yp, 8), (m_rd, 2))):
                nc.vector.memset(spare[:, k:k + 1], 0.0).then_inc(credited, n)
            v.wait_ge(conv_loaded, 16)
            nc.vector.tensor_tensor(bn_t[:, :], c("bn_b"), c("bn_m"), ALU.subtract).then_inc(bn_scale, 1)
            v.wait_ge(bn_rs, 1)
            nc.vector.tensor_tensor(bn_s[:, 0:16], bn_s[:, 0:16], c("bn_g", 0, 16), ALU.mult).then_inc(bn_scale, 1)
            v.wait_ge(bn_scale, 2)
            nc.vector.tensor_tensor(w1s[:, :].rearrange("p (a c) -> p a c", c=16), c("w1").rearrange("p (a c) -> p a c", c=16),
                                    bn_s[:, 0:16].unsqueeze(1).to_broadcast([128, 16, 16]), ALU.mult).then_inc(w_scaled, 1)
            v.wait_ge(bn_rs, 2)
            nc.vector.tensor_tensor(bn_s[:, 80:83], bn_s[:, 80:83], c("bn_g", 80, 83), ALU.mult).then_inc(bn_scale, 1)
            v.wait_ge(bn_scale, 3)
            nc.vector.tensor_tensor(bn_t[:, :], bn_t[:, :], bn_s[:, 80:83], ALU.mult).then_inc(bn_shift, 1)
            v.wait_ge(bn_shift, 1)
            nc.vector.tensor_tensor(bn_t[:, :], bn_t[:, :], c("bn_be"), ALU.add).then_inc(bn_shift, 1)
            stage1a_dve(v)
            nc.vector.tensor_scalar(gbv[:, :], c("bv"), c("gamma"), None, ALU.mult).then_inc(gbv_ready, 1)
            setup3_mixed_dve(v)
            v.wait_ge(a_pb_ps, 1)
            nc.vector.tensor_tensor(a_pb[:, :], T(1, 3)[:, 0:128], c("a_bp"), ALU.add).then_inc(a_pb_r, 1)
            stage1b_dve(v)
            setup3_last_dve(v)
            for l in range(2):
                nc.vector.memset(a_v[l], 1.0).then_inc(a_ones, 1)
            v.wait_ge(a_setup, 2)
            stage2_dve(v)
            v.wait_ge(a_h_r, NP + 3)
            v.wait_ge(f_still, 6)
            stage3_dve(v)
            for u in range(2):
                nc.vector.memset(g_hs[u][:, :], 0.0).then_inc(g_setup, 1)
            nc.vector.memset(g_a[1][:, :], 0.0).then_inc(g_ar, 1)
            nc.vector.memset(g_b[1][:, :], 0.0).then_inc(g_br, 1)
            nc.vector.tensor_tensor(g_bias[:, :], c("g_bih"), c("g_bhh"), ALU.add).then_inc(g_setup, 1)
            nc.vector.tensor_tensor(m_bg[:, :], c("m_bg"), c("m_bias"), ALU.add).then_inc(m_bg_r, 1)
            v.wait_ge(g_setup, 3)
            nc.vector.tensor_scalar(g_nbz[:, :], g_bias[:, 1:2], -1.0, None, ALU.mult).then_inc(g_hr, 1)
            stage4_dve(v)
            gru_dve(v)
            v.wait_ge(r_bias, NP // 2)
            stage6_dve(v)
            v.wait_ge(m_bg_r, 1)
            stage7_dve(v)

        @block.tensor
        def _(pe):
            stage1a_pe(pe)
            pe.wait_ge(loaded, 16)
            pe.wait_ge(h2_ready, JA + 2)
            nc.tensor.matmul(T(1, 3)[:, 0:128], c("a_bv"), c("a_p"), start=True, stop=True).then_inc(a_pb_ps, 1)
            setup3_middle_pe(pe)
            stage1b_pe(pe)
            setup3_last_pe(pe)
            pe.wait_ge(a_pb_r, 1)
            pe.wait_ge(b_h, NG + 1)
            stage2_pe(pe)
            pe.wait_ge(a_h_r, NP + 3)
            stage3_pe(pe)
            pe.wait_ge(f_h_r, NP + 2)
            stage4_pe(pe)
            pe.wait_ge(r_xgf, NJ4 + 2)
            pe.wait_ge(r_xgr, NJ4 + 2)
            gru_pe(pe)
            pe.wait_ge(g_yr, L + 2)
            pe.wait_ge(g_hr, L + 1)
            stage6_pe(pe)
            stage7_pe(pe)

        @block.scalar
        def _(act):
            stage1a_act(act)
            act.wait_ge(loaded, 16)
            stage1b_act(act)
            act.wait_ge(a_ones, 2)
            act.wait_ge(a_setup, 2)
            stage2_act(act)
            act.wait_ge(f_still, 6)
            act.wait_ge(one_set, 1)
            stage3_act(act)
            act.wait_ge(f_h_r, NP + 2)
            stage4_act(act)
            act.wait_ge(g_setup, 3)
            act.wait_ge(g_hr, 1)
            gru_act(act)
            stage6_act(act)
            stage7_act(act)


def lay_out(w):
    big = np.zeros((128, WIDTH), np.float32)

    def put(name, a):
        a = np.asarray(a, np.float32)
        o, n = AT[name]
        assert a.shape[1] == n, (name, a.shape, n)
        big[:a.shape[0], o:o + n] = a

    def col(a):
        return np.asarray(a).reshape(-1, 1)

    def rows(a):
        return np.broadcast_to(np.asarray(a).reshape(1, -1), (128, np.asarray(a).size))

    def diag2(a):
        z = np.zeros((128, 2 * a.shape[1]), np.float32)
        z[:64, :a.shape[1]] = a
        z[64:, a.shape[1]:] = a
        return z

    put("eye", np.eye(128))
    w1 = np.zeros((3, 2, 16, 2, 8, 16), np.float32)
    for b in range(16):
        w1[:, :, b, b // 8, b % 8, :] = w["L0_tok_w1"].transpose(2, 1, 0)
    put("w1", w1.reshape(96, 256))
    w2 = np.zeros((3, 2, 16, 2, 64), np.float32)
    for k in range(2):
        w2[:, k, :, k] = w["L0_tok_w2"].transpose(2, 1, 0)
    put("w2", w2.reshape(96, 128))
    w3 = np.zeros((2, 64, 2, 4, 128), np.float32)
    for s in range(2):
        w3[s, :, s] = w["L0_tok_w3"].transpose(1, 2, 0)
    put("w3", w3.reshape(128, 8 * 128))
    for n, part in (("v", "v"), ("g", "g")):
        a1, a2, a3 = (np.asarray(w[f"L0_tok_{part}{k}"]) for k in (1, 2, 3))
        put("bn_" + n, np.concatenate([rows(a1), rows(a2), col(np.tile(a1, 8)), col(np.tile(a2, 2)), col(a3)], 1))
    for n, part in (("b", "b"), ("m", "m"), ("be", "be")):
        a1, a2, a3 = (np.asarray(w[f"L0_tok_{part}{k}"]) for k in (1, 2, 3))
        put("bn_" + n, np.concatenate([col(np.tile(a1, 8)), col(np.tile(a2, 2)), col(a3)], 1))
    zq, zk = np.zeros((2, 64, 2, 2, 64), np.float32), np.zeros((2, 64, 2, 64), np.float32)
    zbq, zbk = np.zeros((2, 64, 2), np.float32), np.zeros((2, 64, 1), np.float32)
    for s in range(2):
        zq[s, :, s, s, :8] = w["L0_tok_wq"].T
        zk[s, :, s, :8] = w["L0_tok_wk"].T
        zbq[s, :8, s] = w["L0_tok_bq"]
        zbk[s, :8, 0] = w["L0_tok_bk"]
    put("wq", zq.reshape(128, 256))
    put("wk", zk.reshape(128, 128))
    put("bq", zbq.reshape(128, 2))
    put("bk", zbk.reshape(128, 1))
    put("wv", diag2(w["L0_tok_wv"].T))
    put("bv", col(np.tile(w["L0_tok_bv"], 2)))
    put("gamma", col(np.broadcast_to(w["L0_tok_gamma"], (128,))))
    lay_out_more(w, put, col, rows, diag2)
    return big


def lay_out_more(w, put, col, rows, diag2):
    qkv = w["L0_attn_qkv_weight"]
    qkv_b = w["L0_attn_qkv_bias"]
    for k, n in enumerate(("a_q", "a_k", "a_v")):
        put(n, diag2(qkv[64 * k:64 * (k + 1)].T))
    put("a_bq", col(np.tile(qkv_b[0:64], 2)))
    put("a_bk", col(np.tile(qkv_b[64:128], 2)))
    put("a_bv", np.broadcast_to(col(np.tile(qkv_b[128:192], 2)), (128, 128)))
    put("a_p", diag2(w["L0_attn_proj_weight"].T))
    put("a_bp", rows(np.tile(w["L0_attn_proj_bias"], 2)))
    mask = np.zeros((2, 8, 8, 2, 8), np.float32)
    for s in range(2):
        for k in range(8):
            mask[s, k, :, s, k] = 1.0
    put("a_mask", mask.reshape(128, 16))
    table = w["L0_attn_bias_table"].T
    put("a_bias", np.stack([table[:, q:q + 128][:, ::-1] for q in range(128)]).reshape(128, 1024))
    def headT(a):
        return a.reshape(64, 8, 64).transpose(2, 1, 0).reshape(64, 512)
    put("f_fxT", headT(w["L0_ffn_W_fx"]))
    put("f_xT", headT(w["L0_ffn_W_x"]))
    put("f_bfxT", w["L0_ffn_b_fx"].reshape(8, 64).T)
    put("f_bxT", w["L0_ffn_b_x"].reshape(8, 64).T)
    put("f_slice", w["L0_ffn_W_slice"])
    put("f_bslice", rows(w["L0_ffn_b_slice"]))
    for n in "qkv":
        put(f"f_w{n}T", w[f"L0_ffn_W_{n}"].T)
    put("f_out", w["L0_ffn_W_out"].reshape(8, 64, 64).transpose(1, 0, 2).reshape(64, 512))
    put("f_bout", col(np.tile(w["L0_ffn_b_out"], 2)))
    put("f_temp", rows(w["L0_ffn_temperature"]))
    a = "L1_attn_"
    put("g_lng", col(np.tile(w[a + "ln_g"], 2)))
    put("g_lnb", col(np.tile(w[a + "ln_b"], 2)))
    for n in ("ih", "hh"):
        z = np.zeros((2, 64, 3, 2, 64), np.float32)
        zb = np.zeros((2, 64, 3), np.float32)
        for d, way in enumerate(("fwd", "rev")):
            z[d, :, :, d] = w[f"{a}{way}_w_{n}"].reshape(3, 64, 64).transpose(2, 0, 1)
            zb[d] = w[f"{a}{way}_b_{n}"].reshape(3, 64).T
        put("g_" + n, z.reshape(128, 384))
        put("g_b" + n, zb.reshape(128, 3))
    put("g_gate", w[a + "gate_w"].T)
    put("g_bgate", col(w[a + "gate_b"]))
    put("g_diff", np.concatenate([np.eye(64), -np.eye(64)]))
    put("g_out", np.tile(w[a + "out_w"].T, (2, 1)))
    put("g_bout", rows(np.tile(w[a + "out_b"], 4)))
    put("m_g", diag2(w["L1_ffn_Wg"]))
    put("m_bg", rows(np.tile(w["L1_ffn_bg"], 8)))
    put("m_bias", rows(np.tile(w["L1_ffn_bias"], 8)))
    z = np.zeros((2, 64, 2, 8, 128), np.float32)
    for s in range(2):
        z[s, :, s] = w["L1_ffn_W1"].transpose(1, 0, 2)
    put("m_w1", z.reshape(128, 2048))
    put("m_b1", w["L1_ffn_b1"].T)
    put("m_w2", np.concatenate([w["L1_ffn_W2"].transpose(1, 0, 2).reshape(128, 512), np.zeros((128, 32), np.float32)], 1))
    put("m_b2", rows(w["L1_ffn_b2"]))
    put("iota", rows(np.arange(8)))


def kernel(**inputs):
    import concourse.bacc as bacc
    from concourse.bass_utils import run_bass_kernel_spmd

    w = {k: np.asarray(v) for k, v in inputs.items()}
    xp = np.zeros((4, 2, 16, LEN + 2), np.float32)
    xp[:, :, :, 1:LEN + 1] = w["x"].reshape(4, 16, 2, LEN).transpose(0, 2, 1, 3)
    arrays = {"x_dram": xp.reshape(4, 32, LEN + 2), "consts_dram": lay_out(w)}
    nc = bacc.Bacc("TRN2", target_bir_lowering=False, num_devices=1)
    args = [nc.dram_tensor(n, a.shape, F32, kind="ExternalInput").ap() for n, a in arrays.items()]
    out = nc.dram_tensor("out_dram", (B, L, C), F32, kind="ExternalOutput").ap()
    build(nc, *args, out)
    return run_bass_kernel_spmd(nc, [arrays], core_ids=[0]).results[0]["out_dram"]
```
